# Optimizing a Trainium2 kernel written in Bass

```python
import numpy as np
import jax
import jax.numpy as jnp

def _softmax(x, axis=-1):
    return jax.nn.softmax(x, axis=axis)

def _gelu(x):
    return jax.nn.gelu(x, approximate=True)

def _silu(x):
    return jax.nn.silu(x)

def _sigmoid(x):
    return jax.nn.sigmoid(x)

def _layernorm(x, axis=-1, eps=1e-05):
    m = jnp.mean(x, axis=axis, keepdims=True)
    v = jnp.var(x, axis=axis, keepdims=True)
    return (x - m) / jnp.sqrt(v + eps)

def _scatter_add(tgt, idx, src, axis=0):
    return tgt.at[idx].add(src)

def _segment_sum(src, seg, n):
    return jax.ops.segment_sum(src, seg, n)
kernel_name = 'mk_cond_seq_d2_seqx_r2_f11f21'

def setup_inputs(seed: int=0):
    np.random.seed(seed)
    _w = jnp.asarray

    def _rec_inputs():
        import jax
        import jax.numpy as jnp
        _rk = jax.random.key(seed)
        x = -0.0002928 + 1 * jax.random.normal(jax.random.fold_in(_rk, 1), (8, 512, 512), jnp.float32)
        _lenS = 512 - jax.random.randint(jax.random.fold_in(_rk, 7), (8,), 0, max(1, 512 // 4) + 1, jnp.int32)
        _lenS2 = 512 - jax.random.randint(jax.random.fold_in(_rk, 8), (8,), 0, max(1, 512 // 4) + 1, jnp.int32)
        cond_1024 = 0.000887014 + 1.03683 * jax.random.normal(jax.random.fold_in(_rk, 11), (8, 512), jnp.float32)
        fside_BxSx3_0 = jax.random.uniform(jax.random.fold_in(_rk, 12), (8, 512, 3), jnp.float32, 0.0, 0.999943)
        return (x, cond_1024, fside_BxSx3_0)
    x, cond_1024, fside_BxSx3_0 = _rec_inputs()

    def _L0_cond_setup():
        import jax, jax.numpy as jnp
        import numpy as np
        DIM = 512
        HEADS = 16
        HIDDEN = 2048
        EPS = 1e-05

        def _ln(h):
            mu = jnp.mean(h, axis=-1, keepdims=True)
            var = jnp.var(h, axis=-1, keepdims=True)
            return (h - mu) / jnp.sqrt(var + EPS)
        key = jax.random.key(seed)
        ks = jax.random.split(key, 11)
        B, N, D, H = (2, 1024, DIM, HIDDEN)
        s = lambda fan: 1.0 / np.sqrt(fan)
        return {'x': jax.random.normal(ks[0], (B, N, D), jnp.float32), 'c': jax.random.normal(ks[1], (B, D), jnp.float32), 'w_qkv': jax.random.normal(ks[2], (D, 3 * D), jnp.float32) * s(D), 'w_proj': jax.random.normal(ks[3], (D, D), jnp.float32) * s(D), 'b_proj': jax.random.normal(ks[4], (D,), jnp.float32) * 0.01, 'w_fc1': jax.random.normal(ks[5], (D, H), jnp.float32) * s(D), 'b_fc1': jax.random.normal(ks[6], (H,), jnp.float32) * 0.01, 'w_fc2': jax.random.normal(ks[7], (H, D), jnp.float32) * s(H), 'b_fc2': jax.random.normal(ks[8], (D,), jnp.float32) * 0.01, 'w_ada': jax.random.normal(ks[9], (D, 6 * D), jnp.float32) * s(D), 'b_ada': jax.random.normal(ks[10], (6 * D,), jnp.float32) * 0.01}
    _L0_cond_all = _L0_cond_setup()
    _L0_cond_in = {k: v for k, v in _L0_cond_all.items() if k in ('w_qkv', 'w_proj', 'b_proj', 'w_fc1', 'b_fc1', 'w_fc2', 'b_fc2', 'w_ada', 'b_ada')}
    del _L0_cond_all

    def _L1_cond_setup():
        import jax, jax.numpy as jnp
        import numpy as np
        HID = 512
        HEADS = 16
        HEAD_DIM = HID // HEADS
        ROPE_DIM = HEAD_DIM // 6 * 6
        HALF = ROPE_DIM // 3 // 2
        SWIGLU_HID = int(2 * (HID * 4) / 3)
        EPS = 1e-06
        THETA = 10000.0

        def rmsnorm(x, w, eps=EPS):
            xf = x.astype(jnp.float32)
            v = jnp.mean(xf * xf, axis=-1, keepdims=True)
            return w * (xf * jax.lax.rsqrt(v + eps)).astype(x.dtype)

        def modulate(x, shift, scale):
            return x * (1.0 + scale) + shift

        def rope_freqs():
            return 1.0 / THETA ** (jnp.arange(HALF, dtype=jnp.float32) / HALF)

        def apply_rope3d(q, k, positions):
            freqs = rope_freqs()
            ang = positions[..., :, None] * freqs
            ang = ang.reshape(ang.shape[0], ang.shape[1], -1)
            cos = jnp.cos(ang)[:, :, None, :]
            sin = jnp.sin(ang)[:, :, None, :]

            def rot(t):
                B, N, H, D = t.shape
                tr = t.reshape(B, N, H, D // 2, 2)
                t0, t1 = (tr[..., 0], tr[..., 1])
                out = jnp.stack([t0 * cos - t1 * sin, t0 * sin + t1 * cos], axis=-1)
                return out.reshape(B, N, H, D)
            return (rot(q), rot(k))
        key = jax.random.key(seed)
        ks = jax.random.split(key, 12)
        B, N = (2, 1024)
        s = 0.02
        return {'x': jax.random.normal(ks[0], (B, N, HID), jnp.float32), 'c': jax.random.normal(ks[1], (B, HID), jnp.float32), 'positions': jax.random.uniform(ks[2], (B, N, 3), jnp.float32), 'norm1_w': jnp.ones((HID,), jnp.float32), 'qkv_w': jax.random.normal(ks[3], (3 * HID, HID), jnp.float32) * s, 'q_norm_w': jnp.ones((HEAD_DIM,), jnp.float32), 'k_norm_w': jnp.ones((HEAD_DIM,), jnp.float32), 'proj_w': jax.random.normal(ks[4], (HID, HID), jnp.float32) * s, 'proj_b': jnp.zeros((HID,), jnp.float32), 'norm2_w': jnp.ones((HID,), jnp.float32), 'w1': jax.random.normal(ks[5], (SWIGLU_HID, HID), jnp.float32) * s, 'w3': jax.random.normal(ks[6], (SWIGLU_HID, HID), jnp.float32) * s, 'w2': jax.random.normal(ks[7], (HID, SWIGLU_HID), jnp.float32) * s, 'ada_w': jax.random.normal(ks[8], (6 * HID, HID), jnp.float32) * s, 'ada_b': jnp.zeros((6 * HID,), jnp.float32)}
    _L1_cond_all = _L1_cond_setup()
    _L1_cond_in = {k: v for k, v in _L1_cond_all.items() if k in ('norm1_w', 'qkv_w', 'q_norm_w', 'k_norm_w', 'proj_w', 'proj_b', 'norm2_w', 'w1', 'w3', 'w2', 'ada_w', 'ada_b')}
    del _L1_cond_all
    return {'x': x, 'cond_1024': cond_1024, 'fside_BxSx3_0': fside_BxSx3_0, 'L0_cond_w_qkv': _L0_cond_in['w_qkv'], 'L0_cond_w_proj': _L0_cond_in['w_proj'], 'L0_cond_b_proj': _L0_cond_in['b_proj'], 'L0_cond_w_fc1': _L0_cond_in['w_fc1'], 'L0_cond_b_fc1': _L0_cond_in['b_fc1'], 'L0_cond_w_fc2': _L0_cond_in['w_fc2'], 'L0_cond_b_fc2': _L0_cond_in['b_fc2'], 'L0_cond_w_ada': _L0_cond_in['w_ada'], 'L0_cond_b_ada': _L0_cond_in['b_ada'], 'L1_cond_norm1_w': _L1_cond_in['norm1_w'], 'L1_cond_qkv_w': _L1_cond_in['qkv_w'], 'L1_cond_q_norm_w': _L1_cond_in['q_norm_w'], 'L1_cond_k_norm_w': _L1_cond_in['k_norm_w'], 'L1_cond_proj_w': _L1_cond_in['proj_w'], 'L1_cond_proj_b': _L1_cond_in['proj_b'], 'L1_cond_norm2_w': _L1_cond_in['norm2_w'], 'L1_cond_w1': _L1_cond_in['w1'], 'L1_cond_w3': _L1_cond_in['w3'], 'L1_cond_w2': _L1_cond_in['w2'], 'L1_cond_ada_w': _L1_cond_in['ada_w'], 'L1_cond_ada_b': _L1_cond_in['ada_b']}

def reference(x, cond_1024, fside_BxSx3_0, L0_cond_w_qkv, L0_cond_w_proj, L0_cond_b_proj, L0_cond_w_fc1, L0_cond_b_fc1, L0_cond_w_fc2, L0_cond_b_fc2, L0_cond_w_ada, L0_cond_b_ada, L1_cond_norm1_w, L1_cond_qkv_w, L1_cond_q_norm_w, L1_cond_k_norm_w, L1_cond_proj_w, L1_cond_proj_b, L1_cond_norm2_w, L1_cond_w1, L1_cond_w3, L1_cond_w2, L1_cond_ada_w, L1_cond_ada_b):
    import jax
    import jax.numpy as jnp

    def _L0_cond_ref(x, c, w_qkv, w_proj, b_proj, w_fc1, b_fc1, w_fc2, b_fc2, w_ada, b_ada):
        import jax, jax.numpy as jnp
        import numpy as np
        DIM = 512
        HEADS = 16
        HIDDEN = 2048
        EPS = 1e-05

        def _ln(h):
            mu = jnp.mean(h, axis=-1, keepdims=True)
            var = jnp.var(h, axis=-1, keepdims=True)
            return (h - mu) / jnp.sqrt(var + EPS)
        B, N, D = x.shape
        hd = D // HEADS
        scale = hd ** (-0.5)
        mod = jax.nn.silu(c) @ w_ada + b_ada
        shift_msa, scale_msa, gate_msa, shift_mlp, scale_mlp, gate_mlp = jnp.split(mod, 6, axis=1)
        h = _ln(x) * (1.0 + scale_msa[:, None, :]) + shift_msa[:, None, :]
        qkv = (h @ w_qkv).reshape(B, N, 3, HEADS, hd)
        q = qkv[:, :, 0].transpose(0, 2, 1, 3)
        k = qkv[:, :, 1].transpose(0, 2, 1, 3)
        v = qkv[:, :, 2].transpose(0, 2, 1, 3)
        attn = jax.nn.softmax(jnp.einsum('bhqd,bhkd->bhqk', q, k) * scale, axis=-1)
        o = jnp.einsum('bhqk,bhkd->bhqd', attn, v).transpose(0, 2, 1, 3).reshape(B, N, D)
        o = o @ w_proj + b_proj
        x = x + gate_msa[:, None, :] * o
        h2 = _ln(x) * (1.0 + scale_mlp[:, None, :]) + shift_mlp[:, None, :]
        m = jax.nn.gelu(h2 @ w_fc1 + b_fc1, approximate=False) @ w_fc2 + b_fc2
        return x + gate_mlp[:, None, :] * m

    def _L1_cond_ref(x, c, positions, norm1_w, qkv_w, q_norm_w, k_norm_w, proj_w, proj_b, norm2_w, w1, w3, w2, ada_w, ada_b):
        import jax, jax.numpy as jnp
        import numpy as np
        HID = 512
        HEADS = 16
        HEAD_DIM = HID // HEADS
        ROPE_DIM = HEAD_DIM // 6 * 6
        HALF = ROPE_DIM // 3 // 2
        SWIGLU_HID = int(2 * (HID * 4) / 3)
        EPS = 1e-06
        THETA = 10000.0

        def rmsnorm(x, w, eps=EPS):
            xf = x.astype(jnp.float32)
            v = jnp.mean(xf * xf, axis=-1, keepdims=True)
            return w * (xf * jax.lax.rsqrt(v + eps)).astype(x.dtype)

        def modulate(x, shift, scale):
            return x * (1.0 + scale) + shift

        def rope_freqs():
            return 1.0 / THETA ** (jnp.arange(HALF, dtype=jnp.float32) / HALF)

        def apply_rope3d(q, k, positions):
            freqs = rope_freqs()
            ang = positions[..., :, None] * freqs
            ang = ang.reshape(ang.shape[0], ang.shape[1], -1)
            cos = jnp.cos(ang)[:, :, None, :]
            sin = jnp.sin(ang)[:, :, None, :]

            def rot(t):
                B, N, H, D = t.shape
                tr = t.reshape(B, N, H, D // 2, 2)
                t0, t1 = (tr[..., 0], tr[..., 1])
                out = jnp.stack([t0 * cos - t1 * sin, t0 * sin + t1 * cos], axis=-1)
                return out.reshape(B, N, H, D)
            return (rot(q), rot(k))
        B, N, C = x.shape
        H, D = (HEADS, HEAD_DIM)
        mod = (c @ ada_w.T + ada_b)[:, None, :]
        sh_msa, sc_msa, g_msa, sh_mlp, sc_mlp, g_mlp = jnp.split(mod, 6, axis=-1)
        h = modulate(rmsnorm(x, norm1_w), sh_msa, sc_msa)
        qkv = (h @ qkv_w.T).reshape(B, N, 3, H, D)
        q, k, v = (qkv[:, :, 0], qkv[:, :, 1], qkv[:, :, 2])
        q = rmsnorm(q, q_norm_w)
        k = rmsnorm(k, k_norm_w)
        q_r, k_r = apply_rope3d(q[..., :ROPE_DIM], k[..., :ROPE_DIM], positions)
        q = jnp.concatenate([q_r, q[..., ROPE_DIM:]], axis=-1)
        k = jnp.concatenate([k_r, k[..., ROPE_DIM:]], axis=-1)
        scale = D ** (-0.5)
        attn = jnp.einsum('bnhd,bmhd->bhnm', q, k) * scale
        attn = jax.nn.softmax(attn, axis=-1)
        o = jnp.einsum('bhnm,bmhd->bnhd', attn, v).reshape(B, N, C)
        o = o @ proj_w.T + proj_b
        x = x + g_msa * o
        h2 = modulate(rmsnorm(x, norm2_w), sh_mlp, sc_mlp)
        ff = jax.nn.silu(h2 @ w1.T) * (h2 @ w3.T) @ w2.T
        x = x + g_mlp * ff
        return x
    x = _L0_cond_ref(x, cond_1024, L0_cond_w_qkv, L0_cond_w_proj, L0_cond_b_proj, L0_cond_w_fc1, L0_cond_b_fc1, L0_cond_w_fc2, L0_cond_b_fc2, L0_cond_w_ada, L0_cond_b_ada)
    x = _L1_cond_ref(x, cond_1024, fside_BxSx3_0, L1_cond_norm1_w, L1_cond_qkv_w, L1_cond_q_norm_w, L1_cond_k_norm_w, L1_cond_proj_w, L1_cond_proj_b, L1_cond_norm2_w, L1_cond_w1, L1_cond_w3, L1_cond_w2, L1_cond_ada_w, L1_cond_ada_b)
    return x

_drawn_inputs = setup_inputs


def setup_inputs(seed=0):
    import zlib

    import numpy as np

    out = dict(_drawn_inputs(seed))
    spreads = {'L1_cond_norm1_w': (1.0, 0.6),
     'L1_cond_q_norm_w': (1.0, 0.6),
     'L1_cond_k_norm_w': (1.0, 0.6),
     'L1_cond_proj_b': (0.0, 0.1),
     'L1_cond_norm2_w': (1.0, 0.6),
     'L1_cond_ada_b': (0.0, 0.388)}
    factors = {'fside_BxSx3_0': 8.0,
     'L0_cond_b_proj': 8.0,
     'L0_cond_b_fc1': 8.0,
     'L0_cond_b_fc2': 8.0,
     'L0_cond_b_ada': 4.454}
    for name, (base, spread) in spreads.items():
        noise = np.random.default_rng([zlib.crc32(name.encode()), seed]).standard_normal(out[name].shape)
        drawn = base * np.exp(spread * noise) if base else spread * noise
        out[name] = jnp.asarray(drawn.astype(out[name].dtype))
    for name, factor in factors.items():
        out[name] = (out[name] * factor).astype(out[name].dtype)
    return out
```

```python
from contextlib import ExitStack

import numpy as np

import concourse.bass as bass
from concourse import mybir

F32 = mybir.dt.float32
F32R = mybir.dt.float32r
ALU = mybir.AluOpType
ACT = mybir.ActivationFunctionType
AX = mybir.AxisListType
ds = bass.ds

P = 128
B, N, D = 8, 512, 512
HEADS = 16
HD = D // HEADS
TT = N // P
DC = D // P
GH = P // HD
NG = HEADS // GH
HID = (2048, 1365)
EPS = (1e-5, 1e-6)
PAIRS = HD // 2
KROWS = 3 * HD
AROWS = KROWS + 2
SCALE = float(HD) ** -0.5
TWO_PI = 6.283185307179586
PI_A, PI_B = 6.28125, 0.0019350051879882812
PI_C = TWO_PI - PI_A - PI_B
ROUND = 12582912.0


class Banks:

    def __init__(self, before, per, now, b):
        count = lambda uses, bank: sum(1 for _, k in uses if k == bank)
        self.place = {}
        if b is None:
            for i, (key, bank) in enumerate(before):
                self.place[key] = (bank, i, count(before[:i], bank))
        else:
            for i, (key, bank) in enumerate(now):
                self.place[key] = (bank, b * len(per) + (len(before) + i),
                                   b * count(per, bank) + (count(before, bank) + count(now[:i], bank)))

    def bank(self, key):
        return self.place[key][0]

    def filled(self, key):
        return self.place[key][1] + 1

    def freed_before(self, key):
        return self.place[key][2] + 1

    def released(self, key):
        return self.place[key][2] + 2


class Stage:

    def __init__(self, nc, ctx, name, banks, sems):
        self.nc = nc
        self.name = name
        self.bank = [ctx.enter_context(nc.psum_tensor(f"{name}_bank{i}", [P, 512], F32)) for i in range(banks)]
        self.sem = {s: ctx.enter_context(nc.semaphore(f"{name}_{s}")) for s in sems}

    def __getitem__(self, s):
        return self.sem[s]


def over_sequences(eng, body, before=None):
    if before is not None:
        before()
    with eng.Fori(0, B - 1) as b:
        body(b, False)
    body(B - 1, True)


def seq_view(x, b):
    return x[ds(b, 1), :, :].rearrange("o (t p) d -> p (o t) d", p=P)


def wait_and_note(eng, sem, value, noted):
    eng.wait_ge(sem, value)
    eng.sem_inc(noted, 1)


def modulation_stage(nc, dram, mod_rows, modT, ident):
    with ExitStack() as ctx:
        sb = lambda n, s, d=F32: ctx.enter_context(nc.sbuf_tensor(n, s, d))
        cT = sb("mod_cT", [P, DC, B])
        act_c = sb("mod_act_c", [P, DC, B])
        wada = [sb(f"mod_wada{l}", [P, DC, 6 * D]) for l in range(2)]
        bias = sb("mod_bias", [B, 2, 6 * D])
        rows = sb("mod_rows_sb", [B, 2, 6 * D])
        normw = sb("mod_normw", [P, 2, DC])
        st = Stage(nc, ctx, "mod", 5, ["c_in", "w0_in", "w1_in", "b_in", "silu", "filled", "rows_ready",
                                       "turned", "modT_raw", "id0", "id1", "stored"])
        block = ctx.enter_context(nc.Block())

        @block.sync
        def _(sp):
            sp.dma_start(cT[:], dram["cT"]).then_inc(st["c_in"], 16)
            for l in range(2):
                for j in range(6):
                    sp.dma_start(wada[l][:, :, j * D:(j + 1) * D],
                                 dram[f"w_ada{l}"].rearrange("(c p) n -> p c n", p=P)[:, :, j * D:(j + 1) * D]
                                 ).then_inc(st[f"w{l}_in"], 16)
                if l == 0:
                    sp.dma_start(normw[:, 0, :], dram["norm1"]).then_inc(st["b_in"], 16)
                    sp.dma_start(normw[:, 1, :], dram["norm2"]).then_inc(st["b_in"], 16)
                    for k in range(2):
                        sp.dma_start(bias[:, k, :], dram[f"b_ada{k}"].rearrange("(o n) -> o n", o=1)
                                     .to_broadcast([B, 6 * D])).then_inc(st["b_in"], 16)
            for l in range(2):
                sp.wait_ge(st["rows_ready"], 6 * (l + 1))
                sp.dma_start(mod_rows[l, :, :], rows[:, l, :]).then_inc(st["stored"], 16)
            sp.wait_ge(st["stored"], 32)

        @block.gpsimd
        def _(pool):
            pool.memset(ident[:], 0.0).then_inc(st["id0"], 1)
            pool.wait_ge(st["id0"], 1)
            pool.affine_select(out=ident[:], in_=ident[:], compare_op=ALU.not_equal, fill=1.0, base=0,
                               pattern=[[-1, P]], channel_multiplier=1).then_inc(st["id1"], 1)

        @block.scalar
        def _(act):
            act.wait_ge(st["c_in"], 16)
            act.activation(act_c[:], cT[:], ACT.Silu).then_inc(st["silu"], 1)

        @block.tensor
        def _(pe):
            for l in range(2):
                cond = act_c if l == 0 else cT
                if l == 0:
                    pe.wait_ge(st["silu"], 1)
                pe.wait_ge(st[f"w{l}_in"], 96)
                for c in range(DC):
                    for j in range(6):
                        mm = pe.matmul(st.bank[2 * l + j // 4][32 * (j % 4):32 * (j % 4) + B, :], cond[:, c, :],
                                       wada[l][:, c, j * D:(j + 1) * D], start=(c == 0), stop=(c == DC - 1))
                mm.then_inc(st["filled"], 1)
            pe.wait_ge(st["id1"], 1)
            for l in range(2):
                pe.wait_ge(st["rows_ready"], 6 * (l + 1))
                for k in range(4 * DC):
                    off = (0, 1, 3, 4)[k // DC] * D + (k % DC) * P
                    mm = pe.transpose(st.bank[4][:, (l * 16 + k) * B:(l * 16 + k + 1) * B],
                                      rows[:, l, off:off + P], ident[0:B, 0:B])
                mm.then_inc(st["turned"], 1)

        @block.vector
        def _(dve):
            dve.wait_ge(st["b_in"], 64)
            for l in range(2):
                dve.wait_ge(st["filled"], l + 1)
                for j in range(6):
                    dve.tensor_tensor(rows[:, l, j * D:(j + 1) * D],
                                      st.bank[2 * l + j // 4][32 * (j % 4):32 * (j % 4) + B, :],
                                      bias[:, l, j * D:(j + 1) * D], ALU.add).then_inc(st["rows_ready"], 1)
            dve.wait_ge(st["turned"], 2)
            dve.tensor_copy(modT[:].rearrange("p l k b -> p (l k b)"), st.bank[4][:, 0:2 * 16 * B])
            dve.drain()
            for l in range(2):
                for half in range(2):
                    scale = modT[:, l, 4 + 8 * half:8 + 8 * half, :]
                    dve.tensor_scalar(scale, scale, 1.0, None, ALU.add)
                    if l == 1:
                        dve.drain()
                        dve.tensor_tensor(scale, scale, normw[:, half, :].unsqueeze(2).to_broadcast([P, DC, B]),
                                          ALU.mult)


def load_weights(nc, name, items, extra=None):
    with ExitStack() as ctx:
        SLOTS, WIDTH = 3, 2048
        stage = ctx.enter_context(nc.sbuf_tensor(f"{name}_stage", [P, SLOTS, WIDTH], F32))
        sem = {s: ctx.enter_context(nc.semaphore(f"{name}_{s}")) for s in
               ["in0", "in1", "in2", "high_done", "low_done", "extra"]}
        block = ctx.enter_context(nc.Block())

        @block.sync
        def _(sp):
            for i, (src, _, _) in enumerate(items):
                if i >= SLOTS:
                    sp.wait_ge(sem["low_done"], i - SLOTS + 1)
                r, n = src.shape
                sp.dma_start(stage[0:r, i % SLOTS, 0:n], src).then_inc(sem[f"in{i % SLOTS}"], 16)

        @block.scalar
        def _(act):
            for i, (src, high, _) in enumerate(items):
                r, n = src.shape
                act.wait_ge(sem[f"in{i % SLOTS}"], 16 * (i // SLOTS + 1))
                act.activation(high, stage[0:r, i % SLOTS, 0:n], ACT.Copy).then_inc(sem["high_done"], 1)

        @block.vector
        def _(dve):
            for i, (src, high, low) in enumerate(items):
                r, n = src.shape
                dve.wait_ge(sem["high_done"], i + 1)
                dve.tensor_tensor(low, stage[0:r, i % SLOTS, 0:n], high.bitcast(F32), ALU.subtract
                                  ).then_inc(sem["low_done"], 1)

        if extra is not None:
            extra(block, sem["extra"])


def norm_stats(dve, l, x, stats, mv, t):
    dve.bn_stats(stats[:, t, :], x[:, t, :])
    dve.drain()
    dve.bn_aggr(mv[:, t, :], stats[:, t, :])


def norm_power_input(dve, l, mv, power_in, eps):
    dve.drain()
    if l == 0:
        return dve.tensor_scalar(power_in[:, :], mv[:, :, 1], eps, None, ALU.add)
    dve.tensor_tensor(power_in[:, :], mv[:, :, 0], mv[:, :, 0], ALU.mult)
    dve.drain()
    return dve.scalar_tensor_tensor(out=power_in[:, :], in0=power_in[:, :], scalar=eps, in1=mv[:, :, 1],
                                    op0=ALU.add, op1=ALU.add)


def norm_apply(dve, l, x, mv, rstd, t):
    if l == 0:
        return dve.tensor_scalar(x[:, t, :], x[:, t, :], mv[:, t, 0:1], rstd[:, t:t + 1], ALU.subtract, ALU.mult)
    return dve.tensor_scalar(x[:, t, :], x[:, t, :], rstd[:, t:t + 1], None, ALU.mult)


def attention_steps(l, last):
    s = []
    if l == 1:
        for i in range(8):
            s += [("Q", i), ("rope", i)]
        s += [("rope", 8), ("rope", 9)]
    s += [("q", 0), ("k", 0)]
    for t in range(TT):
        s += [("v", t), ("max", 0, t)]
    s += [("q", 1), ("m", 0), ("k", 1)]
    for g in range(NG):
        for kt in range(TT):
            s.append(("s", g, kt))
            if not last and g == 0:
                s.append(("stats", kt))
            if not last and g == 1:
                s.append(("apply", kt))
        if not last and g == 0:
            s.append(("power",))
        if g + 2 < NG:
            s += [("q", g + 2), ("pv", g), ("m", g + 1), ("k", g + 2)]
        elif g + 1 < NG:
            s += [] if last else [("t", 0), ("t", 1)]
            s += [("pv", g), ("m", g + 1)]
            s += [] if last else [("t", 2), ("t", 3)]
        else:
            s.append(("pv", g))
    return s + [("p", t) for t in range(TT)]


def uses_of(steps, kinds):
    return [(s, i % 2) for i, s in enumerate(x for x in steps if x[0] in kinds)]


def attention_stage(nc, l, dram, x_in, x_out, mod_rows, modT, ident):
    nm = f"att{l}"
    with ExitStack() as ctx:
        sb = lambda n, s, d=F32: ctx.enter_context(nc.sbuf_tensor(f"{nm}_{n}", s, d))
        w_high, w_low = sb("w_high", [P, DC, 3 * D], F32R), sb("w_low", [P, DC, 3 * D], F32R)
        p_high, p_low = sb("p_high", [P, DC, D], F32R), sb("p_low", [P, DC, D], F32R)
        ones = sb("ones", [P, HD])
        minus_half = sb("minus_half", [P, HEADS])
        keys = sb("keys", [AROWS, 2, GH, N], F32R)
        if l == 1:
            cos_t, sin_t = sb("cos_t", [P, B * TT, PAIRS]), sb("sin_t", [P, B * TT, PAIRS])
            w_turn = sb("w_turn", [P, 2, PAIRS, 2])
            w_swap = sb("w_swap", [P, 2, PAIRS, 2])

        wv = dram[f"w_qkv{l}"].rearrange("(c p) n -> p c n", p=P)
        pv_ = dram[f"w_proj{l}"].rearrange("(c p) n -> p c n", p=P)
        items = [(wv[:, c, :], w_high[:, c, :], w_low[:, c, :]) for c in range(DC)]
        items += [(pv_[:, c, :], p_high[:, c, :], p_low[:, c, :]) for c in range(DC)]

        with ExitStack() as tmp:
            if l == 1:
                tsb = lambda n, s: tmp.enter_context(nc.sbuf_tensor(f"{nm}_{n}", s, F32))
                pos = tsb("pos", [P, B * TT, 3])
                freqs = tsb("freqs", [P, 5])
                angle = tsb("angle", [P, B * TT, 3, 5])
                turns = tsb("turns", [P, B * TT, 3, 5])
                part = tsb("part", [P, B * TT, 3, 5])
                wrow = tsb("wrow", [P, 2, PAIRS, 2])
                tab_in = tmp.enter_context(nc.semaphore(f"{nm}_tab_in"))
                tab_red = tmp.enter_context(nc.semaphore(f"{nm}_tab_red"))
                tab_sin = tmp.enter_context(nc.semaphore(f"{nm}_tab_sin"))

            def extra(block, sem):
                @block.gpsimd
                def _(pool):
                    pool.memset(ones[:], 1.0)
                    pool.memset(minus_half[:], -0.5)
                    pool.drain()
                    pool.memset(keys[KROWS:AROWS, :, :, :].bitcast(F32), 1.0)
                    if l == 1:
                        pool.dma_start(pos[:], dram["pos"]).then_inc(tab_in, 16)
                        pool.dma_start(freqs[:], dram["freqs"]).then_inc(tab_in, 16)
                        for k in range(2):
                            pool.dma_start(wrow[:, k, :, :].rearrange("p a b -> p (a b)"),
                                           dram["qk_norm"][k:k + 1, :].to_broadcast([P, HD])).then_inc(tab_in, 16)

                if l == 1:
                    @block.vector
                    def _(dve):
                        flat = lambda a: a[:].rearrange("p a b c -> p (a b c)")
                        dve.wait_ge(tab_in, 64)
                        dve.tensor_copy(w_turn[:], wrow[:])
                        dve.tensor_copy(w_swap[:, :, :, 1], wrow[:, :, :, 0])
                        dve.tensor_scalar(w_swap[:, :, :, 0], wrow[:, :, :, 1], -1.0, None, ALU.mult)
                        dve.memset(cos_t[:, :, 15:16], 1.0)
                        dve.memset(sin_t[:, :, 15:16], 0.0)
                        dve.tensor_tensor(angle[:], pos[:].unsqueeze(3).to_broadcast([P, B * TT, 3, 5]),
                                          freqs[:].unsqueeze(1).unsqueeze(1).to_broadcast([P, B * TT, 3, 5]),
                                          ALU.mult)
                        for k, shift in enumerate((0.0, 0.25)):
                            dve.drain()
                            if k == 1:
                                dve.wait_ge(tab_sin, 1)
                            dve.tensor_scalar(flat(turns), flat(angle), 1.0 / TWO_PI, shift, ALU.mult, ALU.add)
                            dve.drain()
                            dve.tensor_scalar(flat(turns), flat(turns), ROUND, None, ALU.add)
                            dve.drain()
                            dve.tensor_scalar(flat(turns), flat(turns), -ROUND, None, ALU.add)
                            dve.drain()
                            dve.scalar_tensor_tensor(out=flat(part), in0=flat(turns), scalar=-PI_A, in1=flat(angle),
                                                     op0=ALU.mult, op1=ALU.add)
                            for piece in (PI_B, PI_C):
                                dve.drain()
                                dve.scalar_tensor_tensor(out=flat(part), in0=flat(turns), scalar=-piece,
                                                         in1=flat(part), op0=ALU.mult, op1=ALU.add)
                            dve.drain()
                            dve.tensor_scalar(flat(part), flat(part), TWO_PI * shift, 3.1415925, ALU.add, ALU.min)
                            dve.drain()
                            dve.tensor_scalar(flat(part), flat(part), -3.1415925, None, ALU.max
                                              ).then_inc(tab_red, 1)

                    @block.scalar
                    def _(act):
                        for k, out in enumerate((sin_t, cos_t)):
                            act.wait_ge(tab_red, k + 1)
                            act.activation(out[:, :, 0:15].rearrange("p t (a f) -> p t a f", f=5), part[:], ACT.Sin
                                           ).then_inc(tab_sin, 1)

            load_weights(nc, f"{nm}w", items, extra)

        x = sb("x", [P, TT, D])
        h_full = sb("h_full", [P, N])
        h_high, h_low = sb("h_high", [P, DC, N], F32R), sb("h_low", [P, DC, N], F32R)
        qk_high, qk_low = sb("qk_high", [P, 2, N], F32R), sb("qk_low", [P, 2, N], F32R)
        queries = sb("queries", [AROWS, 2, GH, N], F32R)
        values = sb("values", [P, TT, D])
        probs = sb("probs", [P, 2, GH, N])
        o_high, o_low = sb("o_high", [P, DC, N], F32R), sb("o_low", [P, DC, N], F32R)
        tmp2 = sb("tmp2", [P, 2, D])
        gate, gate_bias = sb("gate", [P, D]), sb("gate_bias", [P, D])
        row_max = sb("row_max", [P, 2, GH * TT])
        max_high, max_low = sb("max_high", [GH * TT, 2, P], F32R), sb("max_low", [GH * TT, 2, P], F32R)
        stats, mv = sb("stats", [P, TT, 6]), sb("mv", [P, TT, 2])
        power_in, rstd = sb("power_in", [P, TT]), sb("rstd", [P, TT])
        if l == 1:
            qk_nat = sb("qk_nat", [P, 2, TT, N])
            turn, swap = sb("turn", [P, TT, 2, PAIRS, 2]), sb("swap", [P, TT, 2, PAIRS, 2])
            ssum, sinv = sb("ssum", [P, 2, HEADS]), sb("sinv", [P, 2, HEADS])

        st = Stage(nc, ctx, nm, 8, [
            "filled", "free0", "free1", "max_filled", "max_free", "score_filled", "exp_done", "pv_done", "o_read",
            "o_ready", "high_done", "max_high_done", "stacked0", "stacked1",
            "rows0", "rows1", "x_loaded", "power_ready", "rstd_ready", "x_normed", "h_full_done", "h_ready",
            "res_loaded", "gate_loaded", "x_done", "stored", "noted",
            "nat_done", "sum_ready", "inv_ready", "scaled", "swapped", "roped", "tables_ready"])
        gen, mxb, scb = st.bank[0:2], st.bank[2:4], st.bank[4:6]
        o_acc, s_acc = st.bank[6], st.bank[7]
        kinds = "qkvmtpQ"
        before = uses_of([("t", c) for c in range(DC)], kinds)
        per = uses_of(attention_steps(l, False), kinds)
        banks_for = lambda b, last: Banks(before, per, uses_of(attention_steps(l, last), kinds), b)
        block = ctx.enter_context(nc.Block())

        @block.tensor
        def _(pe):
            pe.sem_inc(st["free0"], 1)
            pe.sem_inc(st["free1"], 1)
            pe.sem_inc(st["max_free"], 2)
            pe.sem_inc(st["exp_done"], 2)
            pe.sem_inc(st["pv_done"], 2)
            pe.sem_inc(st["o_read"], 1)

            def claim(u, key):
                pe.wait_ge(st[f"free{u.bank(key)}"], u.freed_before(key))
                return gen[u.bank(key)]

            def turn_x(u, key):
                g = claim(u, key)
                c = key[1]
                for t in range(TT):
                    mm = pe.transpose(g[:, t * P:(t + 1) * P], x[:, t, c * P:(c + 1) * P], ident[:])
                mm.then_inc(st["filled"], 1)

            def split_product(out, terms):
                n = len(terms)
                for i, (sh, sl, mh, ml) in enumerate(terms):
                    pe.matmul(out, sh, mh, start=(i == 0), stop=False)
                    pe.matmul(out, sh, ml, start=False, stop=False)
                    mm = pe.matmul(out, sl, mh, start=False, stop=(i == n - 1))
                return mm

            def first():
                u = Banks(before, per, None, None)
                pe.wait_ge(st["x_normed"], TT)
                for c in range(DC):
                    turn_x(u, ("t", c))

            def body(b, last):
                u = banks_for(b, last)

                def max_products(g, i):
                    for qt in range(TT):
                        n = b * 64 + (16 * g + 4 * i + qt)
                        pe.wait_ge(st["max_free"], n + 1)
                        pe.matmul(mxb[qt % 2][:], queries[0:KROWS, g % 2, i, qt * P:(qt + 1) * P],
                                  keys[0:KROWS, g % 2, i, :], start=True, stop=True).then_inc(st["max_filled"], 1)
                        if qt == 1:
                            yield
                    yield

                def score_products(g, kt, heads):
                    for h in heads:
                        n = b * 64 + (16 * g + 4 * kt + h)
                        pe.wait_ge(st["exp_done"], n + 1)
                        pe.matmul(scb[h % 2][:], keys[0:AROWS, g % 2, h, kt * P:(kt + 1) * P],
                                  queries[0:AROWS, g % 2, h, :], start=True, stop=True
                                  ).then_inc(st["score_filled"], 1)

                def values_product(g, kt):
                    pe.wait_ge(st["exp_done"], b * 64 + (16 * g + 4 * kt + 4 + 2))
                    if kt == 0:
                        pe.wait_ge(st["o_read"], b * NG + (g + 1))
                        if g == 0:
                            for t in (TT - 2, TT - 1):
                                pe.wait_ge(st[f"free{u.bank(('v', t))}"], u.released(("v", t)))
                    for h in range(GH):
                        pe.matmul(o_acc[HD * h:HD * (h + 1), :], values[:, kt, (GH * g + h) * HD:(GH * g + h + 1) * HD],
                                  probs[:, kt % 2, h, :], start=(kt == 0), stop=(kt == TT - 1))

                def sums_product(g, kt):
                    for h in range(GH):
                        mm = pe.matmul(s_acc[HD * h:HD * (h + 1), :], ones[:], probs[:, kt % 2, h, :],
                                       start=(kt == 0), stop=(kt == TT - 1))
                    mm.then_inc(st["pv_done"], 1)

                for i, step in enumerate(attention_steps(l, last)):
                    kind = step[0]
                    if i == 0:
                        pe.wait_ge(st["h_ready"], b * DC + (DC + 1))
                    if kind == "Q":
                        half, t = divmod(step[1], TT)
                        g = claim(u, step)
                        split_product(g[:], [(h_high[:, c, t * P:(t + 1) * P], h_low[:, c, t * P:(t + 1) * P],
                                              w_high[:, c, half * D:(half + 1) * D],
                                              w_low[:, c, half * D:(half + 1) * D])
                                             for c in range(DC)]).then_inc(st["filled"], 1)
                    elif kind in "qk" and l == 0:
                        a = "qk".index(kind) * D + step[1] * P
                        g = claim(u, step)
                        split_product(g[:], [(w_high[:, c, a:a + P], w_low[:, c, a:a + P],
                                              h_high[:, c, :], h_low[:, c, :])
                                             for c in range(DC)]).then_inc(st["filled"], 1)
                    elif kind in "qk":
                        g = claim(u, step)
                        half, a = step[1] // 2, "qk".index(kind) * 256 + (step[1] % 2) * P
                        if step[1] == 0 and kind == "q":
                            pe.wait_ge(st["roped"], b * 8 + (8 + 1))
                        for t in range(TT):
                            mm = pe.transpose(g[:, t * P:(t + 1) * P], qk_nat[:, half, t, a:a + P], ident[:])
                        mm.then_inc(st["filled"], 1)
                    elif kind == "v":
                        t = step[1]
                        g = claim(u, step)
                        split_product(g[:], [(h_high[:, c, t * P:(t + 1) * P], h_low[:, c, t * P:(t + 1) * P],
                                              w_high[:, c, 2 * D:3 * D], w_low[:, c, 2 * D:3 * D])
                                             for c in range(DC)]).then_inc(st["filled"], 1)
                    elif kind == "max":
                        if step[2] == 0:
                            pe.wait_ge(st["stacked0"], b * 768 + 384)
                        for _ in max_products(0, step[2]):
                            pass
                    elif kind == "m":
                        gi = step[1]
                        g = claim(u, step)
                        pe.wait_ge(st["max_free"], b * 64 + (16 * (gi + 1) + 2))
                        pe.transpose(g[0:GH * TT, 0:P], row_max[:, gi % 2, :], ident[:]).then_inc(st["filled"], 1)
                    elif kind == "s":
                        gi, kt = step[1], step[2]
                        nxt = iter(()) if gi + 1 == NG else max_products(gi + 1, kt)
                        if kt == 0:
                            pe.wait_ge(st[f"rows{gi % 2}"], b * 64 + (32 * (gi // 2) + 32))
                            if gi + 1 < NG:
                                s = (gi + 1) % 2
                                pe.wait_ge(st[f"stacked{s}"], b * 768 + (384 * ((gi + 1) // 2) + 384))
                        score_products(gi, kt, (0, 1))
                        next(nxt, None)
                        if kt:
                            values_product(gi, kt - 1)
                        score_products(gi, kt, (2, 3))
                        next(nxt, None)
                        if kt:
                            sums_product(gi, kt - 1)
                    elif kind == "pv":
                        values_product(step[1], TT - 1)
                        sums_product(step[1], TT - 1)
                    elif kind == "t":
                        if step[1] == 0:
                            pe.wait_ge(st["x_normed"], b * TT + 2 * TT)
                        turn_x(u, step)
                    elif kind == "p":
                        t = step[1]
                        g = claim(u, step)
                        if t == 0:
                            pe.wait_ge(st["o_ready"], b * NG + NG)
                        split_product(g[:], [(o_high[:, c, t * P:(t + 1) * P], o_low[:, c, t * P:(t + 1) * P],
                                              p_high[:, c, :], p_low[:, c, :])
                                             for c in range(DC)]).then_inc(st["filled"], 1)

            over_sequences(pe, body, first)

        @block.scalar
        def _(act):
            act.sem_inc(st["h_ready"], 1)

            def free(ins, u, key):
                ins.then_inc(st[f"free{u.bank(key)}"], 1)

            def modulate(u, key, nb):
                c = key[1]
                act.wait_ge(st["filled"], u.filled(key))
                act.wait_ge(st["h_ready"], nb * DC + (c + 1))
                act.activation(h_full[:], gen[u.bank(key)][:], ACT.Identity, bias=modT[:, l, c, ds(nb, 1)],
                               scale=modT[:, l, 4 + c, ds(nb, 1)]).then_inc(st["h_full_done"], 1)

            def first():
                u = Banks(before, per, None, None)
                for c in range(DC):
                    modulate(u, ("t", c), 0)

            def body(b, last):
                u = banks_for(b, last)
                for step in attention_steps(l, last):
                    kind = step[0]
                    if kind in "qkQvmt":
                        g = gen[u.bank(step)]
                    if kind == "Q":
                        half, t = divmod(step[1], TT)
                        act.wait_ge(st["filled"], u.filled(step))
                        act.activation(qk_nat[:, half, t, :], g[:], ACT.Copy).then_inc(st["nat_done"], 1)
                        if step[1] == 0:
                            act.wait_ge(st["pv_done"], b * 16 + 2)
                        if step[1] >= 2:
                            act.wait_ge(st["sum_ready"], b * 8 + (step[1] - 1))
                        free(act.activation(probs[:, 0, step[1] % 2, :], g[:], ACT.Square), u, step)
                    elif kind in "qk":
                        act.wait_ge(st["filled"], u.filled(step))
                        act.activation(qk_high[:, "qk".index(kind), :], g[:], ACT.Copy).then_inc(st["high_done"], 1)
                    elif kind == "v":
                        act.wait_ge(st["filled"], u.filled(step))
                        free(act.activation(values[:, step[1], :], g[:], ACT.Copy), u, step)
                    elif kind == "m":
                        act.wait_ge(st["filled"], u.filled(step))
                        act.activation(max_high[:, step[1] % 2, :], g[0:GH * TT, 0:P], ACT.Copy, scale=-1.0
                                       ).then_inc(st["max_high_done"], 1)
                    elif kind == "s":
                        gi, kt = step[1], step[2]
                        if l == 1 and gi == 0 and kt == 0:
                            act.wait_ge(st["roped"], b * 8 + (8 + 1))
                        act.wait_ge(st["pv_done"], b * 16 + (4 * gi + kt + 1))
                        for h in range(GH):
                            act.wait_ge(st["score_filled"], b * 64 + (16 * gi + 4 * kt + h + 1))
                            act.activation(probs[:, kt % 2, h, :], scb[h % 2][:], ACT.Exp, scale=SCALE
                                           ).then_inc(st["exp_done"], 1)
                    elif kind == "t":
                        modulate(u, step, b + 1)

            over_sequences(act, body, first)

        @block.vector
        def _(dve):
            dve.sem_inc(st["x_done"], 2)
            dve.sem_inc(st["roped"], 1)

            def split_h(u, key, nb):
                c = key[1]
                dve.wait_ge(st["h_full_done"], nb * DC + (c + 1))
                dve.tensor_copy(h_high[:, c, :], h_full[:]).then_inc(st[f"free{u.bank(key)}"], 1)
                dve.drain()
                dve.tensor_tensor(h_low[:, c, :], h_full[:], h_high[:, c, :].bitcast(F32), ALU.subtract
                                  ).then_inc(st["h_ready"], 1)

            def first():
                u = Banks(before, per, None, None)
                dve.wait_ge(st["x_loaded"], 16)
                for t in range(TT):
                    norm_stats(dve, l, x, stats, mv, t)
                norm_power_input(dve, l, mv, power_in, EPS[l]).then_inc(st["power_ready"], 1)
                dve.wait_ge(st["rstd_ready"], 1)
                for t in range(TT):
                    norm_apply(dve, l, x, mv, rstd, t).then_inc(st["x_normed"], 1)
                for c in range(DC):
                    split_h(u, ("t", c), 0)

            def body(b, last):
                u = banks_for(b, last)
                for step in attention_steps(l, last):
                    kind = step[0]
                    if kind in "qkQvmtp":
                        g = gen[u.bank(step)]
                        freed = st[f"free{u.bank(step)}"]
                    if kind == "rope":
                        i = step[1]
                        if i < 8:
                            key = ("Q", i)
                            dve.wait_ge(st[f"free{u.bank(key)}"], u.released(key))
                            dve.tensor_reduce(ssum[:, i % 2, :], probs[:, 0, i % 2, :].rearrange("p (h d) -> p h d", d=HD),
                                              AX.X, ALU.add)
                            dve.drain()
                            dve.tensor_scalar(ssum[:, i % 2, :], ssum[:, i % 2, :], 1.0 / HD, EPS[1], ALU.mult, ALU.add
                                              ).then_inc(st["sum_ready"], 1)
                        if 1 <= i < 9:
                            half, t = divmod(i - 1, TT)
                            slot = (i - 1) % 2
                            nat = qk_nat[:, half, t, :]
                            dve.wait_ge(st["nat_done"], b * 8 + i)
                            dve.wait_ge(st["inv_ready"], b * 8 + i)
                            dve.tensor_tensor(nat.rearrange("p (h d) -> p h d", d=HD), nat.rearrange("p (h d) -> p h d", d=HD),
                                              sinv[:, slot, :].unsqueeze(2).to_broadcast([P, HEADS, HD]), ALU.mult
                                              ).then_inc(st["scaled"], 1)
                            dve.drain()
                            dve.tensor_tensor(probs[:, 1, slot, :].rearrange("p (s h d) -> p s h d", s=2, d=HD),
                                              nat.rearrange("p (s h d) -> p s h d", s=2, d=HD),
                                              turn[:, t, :, :, :].rearrange("p s a e -> p s (a e)").unsqueeze(2)
                                              .to_broadcast([P, 2, HEADS // 2, HD]), ALU.mult)
                        if i >= 2:
                            half, t = divmod(i - 2, TT)
                            slot = (i - 2) % 2
                            dve.drain()
                            dve.wait_ge(st["swapped"], b * 8 + (i - 1))
                            dve.tensor_tensor(qk_nat[:, half, t, :], probs[:, 1, slot, :], probs[:, 1, 2 + slot, :],
                                              ALU.add).then_inc(st["roped"], 1)
                    elif kind in "qk":
                        n = b * 8 + (2 * step[1] + "qk".index(kind) + 1)
                        i = "qk".index(kind)
                        dve.wait_ge(st["high_done"], n)
                        dve.tensor_tensor(qk_low[:, i, :], g[:], qk_high[:, i, :].bitcast(F32), ALU.subtract
                                          ).then_inc(freed, 1)
                    elif kind == "m":
                        gi = step[1]
                        dve.wait_ge(st["max_high_done"], b * NG + (gi + 1))
                        dve.scalar_tensor_tensor(out=max_low[:, gi % 2, :], in0=g[0:GH * TT, 0:P], scalar=-1.0,
                                                 in1=max_high[:, gi % 2, :].bitcast(F32), op0=ALU.mult,
                                                 op1=ALU.subtract).then_inc(freed, 1)
                    elif kind in ("max", "s"):
                        gi, i = (0, step[2]) if kind == "max" else (step[1] + 1, step[2])
                        if gi < NG:
                            for qt in range(TT):
                                dve.wait_ge(st["max_filled"], b * 64 + (16 * gi + 4 * i + qt + 1))
                                dve.tensor_reduce(row_max[:, gi % 2, 4 * i + qt:4 * i + qt + 1], mxb[qt % 2][:],
                                                  AX.X, ALU.max).then_inc(st["max_free"], 1)
                    elif kind == "pv":
                        gi = step[1]
                        dve.wait_ge(st["pv_done"], b * 16 + (4 * gi + 4 + 2))
                        if gi == 0:
                            dve.wait_ge(st["x_done"], b * TT + 2)
                        dve.reciprocal(tmp2[:, 0, :], s_acc[:])
                        dve.drain()
                        dve.tensor_tensor(tmp2[:, 1, :], o_acc[:], tmp2[:, 0, :], ALU.mult).then_inc(st["o_read"], 1)
                        dve.drain()
                        dve.tensor_copy(o_high[:, gi, :], tmp2[:, 1, :])
                        dve.drain()
                        dve.tensor_tensor(o_low[:, gi, :], tmp2[:, 1, :], o_high[:, gi, :].bitcast(F32),
                                          ALU.subtract).then_inc(st["o_ready"], 1)
                    elif kind == "t":
                        split_h(u, step, b + 1)
                    elif kind == "stats":
                        if step[1] == 0:
                            dve.wait_ge(st["x_loaded"], b * 16 + 32)
                        norm_stats(dve, l, x, stats, mv, step[1])
                    elif kind == "power":
                        norm_power_input(dve, l, mv, power_in, EPS[l]).then_inc(st["power_ready"], 1)
                    elif kind == "apply":
                        if step[1] == 0:
                            dve.wait_ge(st["rstd_ready"], b + 2)
                        norm_apply(dve, l, x, mv, rstd, step[1]).then_inc(st["x_normed"], 1)
                    elif kind == "p":
                        t = step[1]
                        if t == 0:
                            dve.drain()
                            dve.wait_ge(st["gate_loaded"], b * 32 + 32)
                        dve.wait_ge(st["filled"], u.filled(step))
                        dve.wait_ge(st["x_done"], b * TT + (t + 1))
                        dve.tensor_tensor(tmp2[:, t % 2, :], g[:], gate[:], ALU.mult).then_inc(freed, 1)

            over_sequences(dve, body, first)

        @block.gpsimd
        def _(pool):
            def power(n):
                wait_and_note(pool, st["power_ready"], n + 1, st["noted"])
                pool.tensor_tensor(rstd[:], power_in[:], minus_half[:, 0:TT], ALU.pow).then_inc(st["rstd_ready"], 1)

            def body(b, last):
                u = banks_for(b, last)
                if l == 1:
                    wait_and_note(pool, st["roped"], b * 8 + 1, st["noted"])
                    for table, w, trig in ((turn, w_turn, cos_t), (swap, w_swap, sin_t)):
                        for s in range(2):
                            for e in range(2):
                                pool.tensor_tensor(table[:, :, s, :, e], trig[:, ds(b * TT, TT), :],
                                                   w[:, s, :, e].unsqueeze(1).to_broadcast([P, TT, PAIRS]), ALU.mult
                                                   ).then_inc(st["tables_ready"], 1)
                for step in attention_steps(l, last):
                    kind = step[0]
                    if kind == "rope":
                        i = step[1]
                        if i < 8:
                            wait_and_note(pool, st["sum_ready"], b * 8 + (i + 1), st["noted"])
                            pool.tensor_tensor(sinv[:, i % 2, :], ssum[:, i % 2, :], minus_half[:], ALU.pow
                                               ).then_inc(st["inv_ready"], 1)
                        if 1 <= i < 9:
                            half, t = divmod(i - 1, TT)
                            slot = 2 + (i - 1) % 2
                            nat = qk_nat[:, half, t, :].rearrange("p (s h a e) -> p s h a e", s=2, e=2, a=PAIRS)
                            out = probs[:, 1, slot, :].rearrange("p (s h a e) -> p s h a e", s=2, e=2, a=PAIRS)
                            wait_and_note(pool, st["scaled"], b * 8 + i, st["noted"])
                            if i == 1:
                                wait_and_note(pool, st["tables_ready"], b * 8 + 8, st["noted"])
                            for s in range(2):
                                for e in range(2):
                                    mult = pool.tensor_tensor(
                                        out[:, s, :, :, e], nat[:, s, :, :, 1 - e],
                                        swap[:, t, s, :, e].unsqueeze(1).to_broadcast([P, HEADS // 2, PAIRS]),
                                        ALU.mult)
                            mult.then_inc(st["swapped"], 1)
                    elif kind == "power":
                        power(b + 1)
                    elif kind == "s" and step[1] == 0 and step[2] == 0:
                        wait_and_note(pool, st["gate_loaded"], b * 32 + 32, st["noted"])
                        pool.tensor_tensor(gate_bias[:], gate_bias[:], gate[:], ALU.mult)
                        pool.drain()
                    elif kind == "pv" and step[1] == NG - 1:
                        wait_and_note(pool, st["res_loaded"], b * 16 + 16, st["noted"])
                        for t in range(TT):
                            pool.tensor_tensor(x[:, t, :], x[:, t, :], gate_bias[:], ALU.add)
                        pool.drain()
                    elif kind == "p":
                        t = step[1]
                        wait_and_note(pool, st[f"free{u.bank(step)}"], u.released(step), st["noted"])
                        pool.tensor_tensor(x[:, t, :], x[:, t, :], tmp2[:, t % 2, :], ALU.add
                                           ).then_inc(st["x_done"], 1)

            def first():
                power(0)

            over_sequences(pool, body, first)

        @block.sync
        def _(sp):
            def first():
                sp.sem_inc(st["stored"], 16)
                sp.dma_start(x[:], seq_view(x_in, 0)).then_inc(st["x_loaded"], 16)
                sp.wait_ge(st["filled"], DC)

            def body(b, last):
                u = banks_for(b, last)
                wait_and_note(sp, st["stored"], b * 64 + 16, st["noted"])
                sp.dma_start(gate[:], mod_rows[l, ds(b, 1), 2 * D:3 * D].to_broadcast([P, D])
                             ).then_inc(st["gate_loaded"], 16)
                sp.dma_start(gate_bias[:], dram[f"b_proj{l}"].rearrange("(o n) -> o n", o=1).to_broadcast([P, D])
                             ).then_inc(st["gate_loaded"], 16)
                if not last:
                    sp.dma_start(x[:], seq_view(x_in, b + 1)).then_inc(st["x_loaded"], 16)
                else:
                    sp.dma_start(x[:], seq_view(x_in, b)).then_inc(st["res_loaded"], 16)
                for step in attention_steps(l, last):
                    kind = step[0]
                    if kind in "qk":
                        gi, i = step[1], "qk".index(kind)
                        target = (queries, keys)[i]
                        layout = ((qk_high, qk_low, qk_high), (qk_high, qk_high, qk_low))[i]
                        wait_and_note(sp, st[f"free{u.bank(step)}"], u.released(step), st["noted"])
                        for h in range(GH):
                            for r, src in enumerate(layout):
                                sp.dma_start(target[HD * r:HD * (r + 1), gi % 2, h, :].bitcast(F32),
                                             src[HD * h:HD * (h + 1), i, :].bitcast(F32)
                                             ).then_inc(st[f"stacked{gi % 2}"], 16)
                    elif kind == "m":
                        gi = step[1]
                        wait_and_note(sp, st[f"free{u.bank(step)}"], u.released(step), st["noted"])
                        for r, src in enumerate((max_high, max_low)):
                            sp.dma_start(queries[KROWS + r:KROWS + r + 1, gi % 2, :, :].rearrange("p h n -> p (h n)")
                                         .bitcast(F32), src[:, gi % 2, :].bitcast(F32)).then_inc(st[f"rows{gi % 2}"], 16)
                    elif kind == "t" and step[1] == DC - 1:
                        wait_and_note(sp, st["filled"], u.filled(step), st["noted"])
                        sp.dma_start(x[:], seq_view(x_in, b)).then_inc(st["res_loaded"], 16)
                    elif kind == "p":
                        t = step[1]
                        wait_and_note(sp, st["x_done"], b * TT + (t + 1 + 2), st["noted"])
                        sp.dma_start(x_out[ds(b, 1), t * P:(t + 1) * P, :].rearrange("o p d -> p (o d)"), x[:, t, :]
                                     ).then_inc(st["stored"], 16)

            over_sequences(sp, body, first)
            sp.wait_ge(st["stored"], 16 + 64 * B)


def mlp_steps(l, last):
    chunks = -(-HID[l] // P)
    turn_at = chunks - 5
    s = []
    for j in range(chunks):
        s.append(("a", j))
        if l == 1:
            s.append(("g", j))
        if not last and 1 <= j <= 4:
            s.append(("stats", j - 1))
        if j >= 2 and j < chunks - 1:
            s.append(("c", j - 2))
        if not last and j == 4:
            s.append(("power",))
        if not last and j == 5:
            s += [("apply", t) for t in range(TT)]
        if not last and j == turn_at:
            s += [("t", c) for c in range(DC)]
    if not last:
        s.append(("split",))
    s += [("c", j) for j in (chunks - 3, chunks - 2, chunks - 1)]
    return s + [("p", t) for t in range(TT)]


def mlp_uses(steps):
    bank = {"a": 0, "g": 2, "t": 2}
    return [(s, bank[s[0]] + s[1] % 2) for s in steps if s[0] in bank]


def mlp_stage(nc, l, dram, x_in, x_out, mod_rows, modT, ident):
    nm = f"mlp{l}"
    hid = HID[l]
    chunks = -(-hid // P)
    width = lambda j: min(P, hid - j * P)
    with ExitStack() as ctx:
        sb = lambda n, s, d=F32: ctx.enter_context(nc.sbuf_tensor(f"{nm}_{n}", s, d))
        ups = ["a"] if l == 0 else ["a", "g"]
        up_high = {k: sb(f"up_{k}_high", [P, DC, hid], F32R) for k in ups}
        up_low = {k: sb(f"up_{k}_low", [P, DC, hid], F32R) for k in ups}
        dn_high, dn_low = sb("dn_high", [P, chunks, D], F32R), sb("dn_low", [P, chunks, D], F32R)
        minus_half = sb("minus_half", [P, TT])
        hid_bias = sb("hid_bias", [P, chunks])
        items = []
        for k in ups:
            v = dram[f"up_{k}{l}"].rearrange("(c p) n -> p c n", p=P)
            items += [(v[:, c, :], up_high[k][:, c, :], up_low[k][:, c, :]) for c in range(DC)]
        items += [(dram[f"down{l}"][j * P:j * P + width(j), :], dn_high[0:width(j), j, :], dn_low[0:width(j), j, :])
                  for j in range(chunks)]

        def extra(block, sem):
            @block.gpsimd
            def _(pool):
                pool.memset(minus_half[:], -0.5)
                if l == 0:
                    pool.dma_start(hid_bias[:], dram["b_fc1"]).then_inc(sem, 16)
                    pool.wait_ge(sem, 16)

        load_weights(nc, f"{nm}w", items, extra)

        x = sb("x", [P, TT, D])
        h_full = sb("h_full", [P, DC, N])
        h_high, h_low = sb("h_high", [P, DC, N], F32R), sb("h_low", [P, DC, N], F32R)
        hid_full = sb("hid_full", [P, 2, N])
        hid_high, hid_low = sb("hid_high", [P, 3, N], F32R), sb("hid_low", [P, 3, N], F32R)
        tmp2 = sb("tmp2", [P, 2, D])
        gate = sb("gate", [P, D])
        gate_bias = sb("gate_bias", [P, D]) if l == 0 else None
        stats, mv = sb("stats", [P, TT, 6]), sb("mv", [P, TT, 2])
        power_in, rstd = sb("power_in", [P, TT]), sb("rstd", [P, TT])
        st = Stage(nc, ctx, nm, 8, [
            "filled", "free0", "free1", "free2", "free3", "down_done", "acc_done", "x_loaded",
            "power_ready", "rstd_ready", "x_normed", "h_high_done", "h_ready", "hid_ready", "res_loaded", "gate_loaded", "gated", "x_done", "stored", "noted"])
        ring, acc = st.bank[0:4], st.bank[4:8]
        before = mlp_uses([("t", c) for c in range(DC)])
        per = mlp_uses(mlp_steps(l, False))
        banks_for = lambda b, last: Banks(before, per, mlp_uses(mlp_steps(l, last)), b)
        loads = 32 if l == 0 else 16
        block = ctx.enter_context(nc.Block())

        def hid_slot(j):
            return j % 3

        def hid_full_slot(j):
            return j % 2

        def slot_free(b, j, slots):
            if j >= slots:
                return b * chunks + (j + 1)
            last_use = max(i for i in range(chunks) if i % slots == j)
            return b * chunks + (slots - (chunks - 1 - last_use))

        @block.tensor
        def _(pe):
            for i in range(4):
                pe.sem_inc(st[f"free{i}"], 1)
            pe.sem_inc(st["gated"], TT)
            pe.sem_inc(st["down_done"], 3)

            def turn_x(u, key):
                c = key[1]
                g = ring[u.bank(key)]
                pe.wait_ge(st[f"free{u.bank(key)}"], u.freed_before(key))
                for t in range(TT):
                    mm = pe.transpose(g[:, t * P:(t + 1) * P], x[:, t, c * P:(c + 1) * P], ident[:])
                mm.then_inc(st["filled"], 1)

            def first():
                u = Banks(before, per, None, None)
                pe.wait_ge(st["x_normed"], TT)
                for c in range(DC):
                    turn_x(u, ("t", c))

            def body(b, last):
                u = banks_for(b, last)
                for step in mlp_steps(l, last):
                    kind = step[0]
                    if kind in ("a", "g"):
                        j = step[1]
                        w = width(j)
                        g = ring[u.bank(step)]
                        pe.wait_ge(st[f"free{u.bank(step)}"], u.freed_before(step))
                        if j == 0 and kind == "a":
                            pe.wait_ge(st["h_ready"], b * DC + DC)
                        for c in range(DC):
                            wh = up_high[kind][:, c, j * P:j * P + w]
                            wl = up_low[kind][:, c, j * P:j * P + w]
                            pe.matmul(g[0:w, :], wh, h_high[:, c, :], start=(c == 0), stop=False)
                            pe.matmul(g[0:w, :], wh, h_low[:, c, :], start=False, stop=False)
                            mm = pe.matmul(g[0:w, :], wl, h_high[:, c, :], start=False, stop=(c == DC - 1))
                        mm.then_inc(st["filled"], 1)
                    elif kind == "c":
                        j = step[1]
                        w = width(j)
                        pe.wait_ge(st["hid_ready"], b * chunks + (j + 1 + 2))
                        if j == 0:
                            pe.wait_ge(st["gated"], b * TT + TT)
                        for t in range(TT):
                            hh = hid_high[0:w, hid_slot(j), t * P:(t + 1) * P]
                            hl = hid_low[0:w, hid_slot(j), t * P:(t + 1) * P]
                            pe.matmul(acc[t][:], hh, dn_high[0:w, j, :], start=(j == 0), stop=False)
                            pe.matmul(acc[t][:], hh, dn_low[0:w, j, :], start=False, stop=False)
                            mm = pe.matmul(acc[t][:], hl, dn_high[0:w, j, :], start=False, stop=(j == chunks - 1))
                            if j == chunks - 1 and t < TT - 1:
                                mm.then_inc(st["acc_done"], 1)
                        mm.then_inc(st["down_done"], 1)
                    elif kind == "t":
                        if step[1] == 0:
                            pe.wait_ge(st["x_normed"], b * TT + 2 * TT)
                        turn_x(u, step)

            over_sequences(pe, body, first)

        @block.scalar
        def _(act):
            act.sem_inc(st["hid_ready"], 2)

            def modulate(u, key, nb):
                c = key[1]
                act.wait_ge(st["filled"], u.filled(key))
                act.activation(h_full[:, c, :], ring[u.bank(key)][:], ACT.Identity, bias=modT[:, l, 8 + c, ds(nb, 1)],
                               scale=modT[:, l, 12 + c, ds(nb, 1)]
                               ).then_inc(st[f"free{u.bank(key)}"], 1)

            def high_h(u):
                for c in range(DC):
                    act.wait_ge(st[f"free{u.bank(('t', c))}"], u.released(("t", c)))
                    act.activation(h_high[:, c, :], h_full[:, c, :], ACT.Copy).then_inc(st["h_high_done"], 1)

            def first():
                u = Banks(before, per, None, None)
                for c in range(DC):
                    modulate(u, ("t", c), 0)
                high_h(u)

            def body(b, last):
                u = banks_for(b, last)
                for step in mlp_steps(l, last):
                    kind = step[0]
                    if kind == "a":
                        j = step[1]
                        w = width(j)
                        act.wait_ge(st["filled"], u.filled(step))
                        act.wait_ge(st["hid_ready"], slot_free(b, j, 2))
                        if l == 0:
                            ins = act.activation(hid_full[0:w, hid_full_slot(j), :],
                                                 ring[u.bank(step)][0:w, :], ACT.Gelu, bias=hid_bias[0:w, j:j + 1])
                        else:
                            ins = act.activation(hid_full[0:w, hid_full_slot(j), :], ring[u.bank(step)][0:w, :], ACT.Silu)
                        ins.then_inc(st[f"free{u.bank(step)}"], 1)
                    elif kind == "t":
                        modulate(u, step, b + 1)
                    elif kind == "split":
                        act.wait_ge(st["filled"], u.filled((ups[-1], chunks - 1)))
                        high_h(u)

            over_sequences(act, body, first)

        @block.vector
        def _(dve):
            dve.sem_inc(st["x_done"], 2)

            def low_h(nb):
                for c in range(DC):
                    dve.wait_ge(st["h_high_done"], nb * DC + (c + 1))
                    dve.tensor_tensor(h_low[:, c, :], h_full[:, c, :], h_high[:, c, :].bitcast(F32), ALU.subtract
                                      ).then_inc(st["h_ready"], 1)

            def split_hidden(b, j):
                w = width(j)
                full = hid_full[0:w, hid_full_slot(j), :]
                high, low = hid_high[0:w, hid_slot(j), :], hid_low[0:w, hid_slot(j), :]
                dve.wait_ge(st["down_done"], slot_free(b, j, 3))
                dve.tensor_copy(high, full)
                dve.drain()
                dve.tensor_tensor(low, full, high.bitcast(F32), ALU.subtract).then_inc(st["hid_ready"], 1)

            def first():
                dve.wait_ge(st["x_loaded"], 16)
                for t in range(TT):
                    norm_stats(dve, l, x, stats, mv, t)
                norm_power_input(dve, l, mv, power_in, EPS[l]).then_inc(st["power_ready"], 1)
                dve.wait_ge(st["rstd_ready"], 1)
                for t in range(TT):
                    norm_apply(dve, l, x, mv, rstd, t).then_inc(st["x_normed"], 1)
                low_h(0)

            def body(b, last):
                u = banks_for(b, last)
                for step in mlp_steps(l, last):
                    kind = step[0]
                    if kind == "a" and l == 0:
                        dve.wait_ge(st[f"free{u.bank(step)}"], u.released(step))
                        split_hidden(b, step[1])
                    elif kind == "g":
                        j = step[1]
                        w = width(j)
                        full = hid_full[0:w, hid_full_slot(j), :]
                        dve.wait_ge(st[f"free{u.bank(('a', j))}"], u.released(("a", j)))
                        dve.wait_ge(st["filled"], u.filled(step))
                        dve.tensor_tensor(full, ring[u.bank(step)][0:w, :], full, ALU.mult
                                          ).then_inc(st[f"free{u.bank(step)}"], 1)
                        dve.drain()
                        split_hidden(b, j)
                    elif kind == "stats":
                        if step[1] == 0:
                            dve.wait_ge(st["x_loaded"], b * 16 + 32)
                        norm_stats(dve, l, x, stats, mv, step[1])
                    elif kind == "power":
                        norm_power_input(dve, l, mv, power_in, EPS[l]).then_inc(st["power_ready"], 1)
                    elif kind == "apply":
                        if step[1] == 0:
                            dve.wait_ge(st["rstd_ready"], b + 2)
                        norm_apply(dve, l, x, mv, rstd, step[1]).then_inc(st["x_normed"], 1)
                    elif kind == "split":
                        low_h(b + 1)
                    elif kind == "p":
                        t = step[1]
                        if t == 0:
                            dve.wait_ge(st["gate_loaded"], b * loads + loads)
                        if t < TT - 1:
                            dve.wait_ge(st["acc_done"], b * (TT - 1) + (t + 1))
                        else:
                            dve.wait_ge(st["down_done"], b * chunks + (chunks + 3))
                        dve.wait_ge(st["x_done"], b * TT + (t + 1))
                        dve.tensor_tensor(tmp2[:, t % 2, :], acc[t][:], gate[:], ALU.mult
                                          ).then_inc(st["gated"], 1)

            over_sequences(dve, body, first)

        @block.gpsimd
        def _(pool):
            def power(n):
                wait_and_note(pool, st["power_ready"], n + 1, st["noted"])
                pool.tensor_tensor(rstd[:], power_in[:], minus_half[:], ALU.pow).then_inc(st["rstd_ready"], 1)

            def body(b, last):
                for step in mlp_steps(l, last):
                    kind = step[0]
                    if kind == "power":
                        power(b + 1)
                    elif kind == "c" and step[1] == chunks - 2 and l == 0:
                        wait_and_note(pool, st["gate_loaded"], b * loads + loads, st["noted"])
                        pool.tensor_tensor(gate_bias[:], gate_bias[:], gate[:], ALU.mult)
                        pool.drain()
                        wait_and_note(pool, st["res_loaded"], b * 16 + 16, st["noted"])
                        for t in range(TT):
                            pool.tensor_tensor(x[:, t, :], x[:, t, :], gate_bias[:], ALU.add)
                        pool.drain()
                    elif kind == "p":
                        t = step[1]
                        if t == 0:
                            wait_and_note(pool, st["res_loaded"], b * 16 + 16, st["noted"])
                        wait_and_note(pool, st["gated"], b * TT + (t + 1 + TT), st["noted"])
                        pool.tensor_tensor(x[:, t, :], x[:, t, :], tmp2[:, t % 2, :], ALU.add
                                           ).then_inc(st["x_done"], 1)

            over_sequences(pool, body, lambda: power(0))

        @block.sync
        def _(sp):
            def first():
                sp.sem_inc(st["stored"], 16)
                sp.dma_start(x[:], seq_view(x_in, 0)).then_inc(st["x_loaded"], 16)
                sp.wait_ge(st["filled"], DC)

            def body(b, last):
                wait_and_note(sp, st["stored"], b * 64 + 16, st["noted"])
                if not last:
                    sp.dma_start(x[:], seq_view(x_in, b + 1)).then_inc(st["x_loaded"], 16)
                else:
                    sp.dma_start(x[:], seq_view(x_in, b)).then_inc(st["res_loaded"], 16)
                sp.dma_start(gate[:], mod_rows[l, ds(b, 1), 5 * D:6 * D].to_broadcast([P, D])
                             ).then_inc(st["gate_loaded"], 16)
                if l == 0:
                    sp.dma_start(gate_bias[:], dram["b_fc2"].rearrange("(o n) -> o n", o=1).to_broadcast([P, D])
                                 ).then_inc(st["gate_loaded"], 16)
                for step in mlp_steps(l, last):
                    if step == ("t", DC - 1):
                        wait_and_note(sp, st["filled"], banks_for(b, last).filled(step), st["noted"])
                        sp.dma_start(x[:], seq_view(x_in, b)).then_inc(st["res_loaded"], 16)
                    elif step[0] == "p":
                        t = step[1]
                        wait_and_note(sp, st["x_done"], b * TT + (t + 1 + 2), st["noted"])
                        sp.dma_start(x_out[ds(b, 1), t * P:(t + 1) * P, :].rearrange("o p d -> p (o d)"), x[:, t, :]
                                     ).then_inc(st["stored"], 16)

            over_sequences(sp, body, first)
            sp.wait_ge(st["stored"], 16 + 64 * B)


def build_program(nc, dram, out):
    mod_rows = nc.dram_tensor("mod_rows", [2, B, 6 * D], F32).ap()
    mid = [nc.dram_tensor(f"x_mid{i}", [B, N, D], F32).ap() for i in range(3)]
    with ExitStack() as ctx:
        ident = ctx.enter_context(nc.sbuf_tensor("ident", [P, P], F32))
        modT = ctx.enter_context(nc.sbuf_tensor("modT", [P, 2, 4 * DC, B], F32))
        modulation_stage(nc, dram, mod_rows, modT, ident)
        attention_stage(nc, 0, dram, dram["x"], mid[0], mod_rows, modT, ident)
        mlp_stage(nc, 0, dram, mid[0], mid[1], mod_rows, modT, ident)
        attention_stage(nc, 1, dram, mid[1], mid[2], mod_rows, modT, ident)
        mlp_stage(nc, 1, dram, mid[2], out, mod_rows, modT, ident)


def kernel(**inputs):
    import concourse.bacc as bacc
    from concourse.bass_utils import run_bass_kernel_spmd

    c = {k: np.asarray(v) for k, v in inputs.items()}
    by_chunk = lambda v: v.reshape(-1, P).T
    wq = c["L1_cond_qkv_w"].T
    half = D // 2
    w_qkv1 = np.concatenate([wq[:, 0:half], wq[:, D:D + half], wq[:, half:D], wq[:, D + half:2 * D],
                             wq[:, 2 * D:]], axis=1)
    arrays = {
        "x": c["x"],
        "cT": c["cond_1024"].T.reshape(DC, P, B).transpose(1, 0, 2),
        "w_ada0": c["L0_cond_w_ada"], "b_ada0": c["L0_cond_b_ada"],
        "w_ada1": c["L1_cond_ada_w"].T, "b_ada1": c["L1_cond_ada_b"],
        "norm1": by_chunk(c["L1_cond_norm1_w"]), "norm2": by_chunk(c["L1_cond_norm2_w"]),
        "w_qkv0": c["L0_cond_w_qkv"], "w_qkv1": w_qkv1,
        "w_proj0": c["L0_cond_w_proj"], "w_proj1": c["L1_cond_proj_w"].T,
        "b_proj0": c["L0_cond_b_proj"], "b_proj1": c["L1_cond_proj_b"],
        "up_a0": c["L0_cond_w_fc1"], "b_fc1": by_chunk(c["L0_cond_b_fc1"]),
        "down0": c["L0_cond_w_fc2"], "b_fc2": c["L0_cond_b_fc2"],
        "up_a1": c["L1_cond_w1"].T, "up_g1": c["L1_cond_w3"].T, "down1": c["L1_cond_w2"].T,
        "qk_norm": np.stack([c["L1_cond_q_norm_w"], c["L1_cond_k_norm_w"]]),
        "pos": c["fside_BxSx3_0"].reshape(B * TT, P, 3).transpose(1, 0, 2),
        "freqs": np.tile((1.0 / np.float32(10000.0) ** (np.arange(5, dtype=np.float32) / np.float32(5)))
                         .astype(np.float32), (P, 1)),
    }
    arrays = {k: np.ascontiguousarray(v) for k, v in arrays.items()}
    nc = bacc.Bacc("TRN2", target_bir_lowering=False, num_devices=1)
    dram = {k: nc.dram_tensor(f"in_{k}", v.shape, mybir.dt.from_np(v.dtype), kind="ExternalInput").ap()
            for k, v in arrays.items()}
    out = nc.dram_tensor("out_0", (B, N, D), F32, kind="ExternalOutput").ap()
    build_program(nc, dram, out)
    r = run_bass_kernel_spmd(nc, [{f"in_{k}": v for k, v in arrays.items()}], core_ids=[0])
    return r.results[0]["out_0"]
```

```python
from contextlib import ExitStack

import numpy as np

import concourse.bass as bass
from concourse import mybir

F32 = mybir.dt.float32
F32R = mybir.dt.float32r
ALU = mybir.AluOpType
ACT = mybir.ActivationFunctionType
AX = mybir.AxisListType
ds = bass.ds

P = 128
B, N, D = 8, 512, 512
HEADS = 16
HD = D // HEADS
TT = N // P
DC = D // P
GH = P // HD
NG = HEADS // GH
HID = (2048, 1365)
EPS = (1e-5, 1e-6)
PAIRS = HD // 2
KROWS = 3 * HD
AROWS = KROWS + 2
SCALE = float(HD) ** -0.5
TWO_PI = 6.283185307179586
PI_A, PI_B = 6.28125, 0.0019350051879882812
PI_C = TWO_PI - PI_A - PI_B
ROUND = 12582912.0


class Banks:

    def __init__(self, before, per, now, b):
        count = lambda uses, bank: sum(1 for _, k in uses if k == bank)
        self.opening = b is None
        self.place = {}
        self.earlier = {}
        for bank in {k for _, k in before + per}:
            self.earlier[bank] = 0 if b is None else b * count(per, bank) + count(before, bank)
        for i, (key, bank) in enumerate(before if b is None else now):
            if b is None:
                self.place[key] = (bank, i, count(before[:i], bank))
            else:
                self.place[key] = (bank, b * len(per) + (len(before) + i),
                                   b * count(per, bank) + (count(before, bank) + count(now[:i], bank)))

    def bank(self, key):
        return self.place[key][0]

    def filled(self, key):
        return self.place[key][1] + 1

    def freed_before(self, key):
        return self.place[key][2] + 1

    def all_before(self, bank):
        return self.earlier[bank] + 1

    def released(self, key):
        return self.place[key][2] + 2


class Stage:

    def __init__(self, nc, ctx, name, banks, sems):
        self.nc = nc
        self.name = name
        self.bank = [ctx.enter_context(nc.psum_tensor(f"{name}_bank{i}", [P, 512], F32)) for i in range(banks)]
        self.sem = {s: ctx.enter_context(nc.semaphore(f"{name}_{s}")) for s in sems}

    def __getitem__(self, s):
        return self.sem[s]


def over_sequences(eng, body, before=None):
    if before is not None:
        before()
    with eng.Fori(0, B - 1) as b:
        body(b, False)
    body(B - 1, True)


def seq_view(x, b):
    return x[ds(b, 1), :, :].rearrange("o (t p) d -> p (o t) d", p=P)


def wait_and_note(eng, sem, value, noted):
    eng.wait_ge(sem, value)
    eng.sem_inc(noted, 1)


def modulation_stage(nc, dram, mod_rows, modT, ident):
    with ExitStack() as ctx:
        sb = lambda n, s, d=F32: ctx.enter_context(nc.sbuf_tensor(n, s, d))
        cT = sb("mod_cT", [P, DC, B])
        act_c = sb("mod_act_c", [P, DC, B])
        wada = [sb(f"mod_wada{l}", [P, DC, 6 * D]) for l in range(2)]
        bias = sb("mod_bias", [B, 2, 6 * D])
        rows = sb("mod_rows_sb", [B, 2, 6 * D])
        normw = sb("mod_normw", [P, 2, DC])
        st = Stage(nc, ctx, "mod", 5, ["c_in", "w0_in", "w1_in", "b_in", "silu", "filled", "rows_ready",
                                       "turned", "modT_raw", "id0", "id1", "stored"])
        block = ctx.enter_context(nc.Block())

        @block.sync
        def _(sp):
            sp.dma_start(cT[:], dram["cT"]).then_inc(st["c_in"], 16)
            for l in range(2):
                for j in range(6):
                    sp.dma_start(wada[l][:, :, j * D:(j + 1) * D],
                                 dram[f"w_ada{l}"].rearrange("(c p) n -> p c n", p=P)[:, :, j * D:(j + 1) * D]
                                 ).then_inc(st[f"w{l}_in"], 16)
                if l == 0:
                    sp.dma_start(normw[:, 0, :], dram["norm1"]).then_inc(st["b_in"], 16)
                    sp.dma_start(normw[:, 1, :], dram["norm2"]).then_inc(st["b_in"], 16)
                    for k in range(2):
                        sp.dma_start(bias[:, k, :], dram[f"b_ada{k}"].rearrange("(o n) -> o n", o=1)
                                     .to_broadcast([B, 6 * D])).then_inc(st["b_in"], 16)
            for l in range(2):
                sp.wait_ge(st["rows_ready"], 6 * (l + 1))
                sp.dma_start(mod_rows[l, :, :], rows[:, l, :]).then_inc(st["stored"], 16)
            sp.wait_ge(st["stored"], 32)

        @block.gpsimd
        def _(pool):
            pool.memset(ident[:], 0.0).then_inc(st["id0"], 1)
            pool.wait_ge(st["id0"], 1)
            pool.affine_select(out=ident[:], in_=ident[:], compare_op=ALU.not_equal, fill=1.0, base=0,
                               pattern=[[-1, P]], channel_multiplier=1).then_inc(st["id1"], 1)

        @block.scalar
        def _(act):
            act.wait_ge(st["c_in"], 16)
            act.activation(act_c[:], cT[:], ACT.Silu).then_inc(st["silu"], 1)

        @block.tensor
        def _(pe):
            for l in range(2):
                cond = act_c if l == 0 else cT
                if l == 0:
                    pe.wait_ge(st["silu"], 1)
                pe.wait_ge(st[f"w{l}_in"], 96)
                for c in range(DC):
                    for j in range(6):
                        mm = pe.matmul(st.bank[2 * l + j // 4][32 * (j % 4):32 * (j % 4) + B, :], cond[:, c, :],
                                       wada[l][:, c, j * D:(j + 1) * D], start=(c == 0), stop=(c == DC - 1))
                mm.then_inc(st["filled"], 1)
            pe.wait_ge(st["id1"], 1)
            for l in range(2):
                pe.wait_ge(st["rows_ready"], 6 * (l + 1))
                for k in range(4 * DC):
                    off = (0, 1, 3, 4)[k // DC] * D + (k % DC) * P
                    mm = pe.transpose(st.bank[4][:, (l * 16 + k) * B:(l * 16 + k + 1) * B],
                                      rows[:, l, off:off + P], ident[0:B, 0:B])
                mm.then_inc(st["turned"], 1)

        @block.vector
        def _(dve):
            dve.wait_ge(st["b_in"], 64)
            for l in range(2):
                dve.wait_ge(st["filled"], l + 1)
                for j in range(6):
                    dve.tensor_tensor(rows[:, l, j * D:(j + 1) * D],
                                      st.bank[2 * l + j // 4][32 * (j % 4):32 * (j % 4) + B, :],
                                      bias[:, l, j * D:(j + 1) * D], ALU.add).then_inc(st["rows_ready"], 1)
            dve.wait_ge(st["turned"], 2)
            dve.tensor_copy(modT[:].rearrange("p l k b -> p (l k b)"), st.bank[4][:, 0:2 * 16 * B])
            dve.drain()
            for l in range(2):
                for half in range(2):
                    scale = modT[:, l, 4 + 8 * half:8 + 8 * half, :]
                    dve.tensor_scalar(scale, scale, 1.0, None, ALU.add)
                    if l == 1:
                        dve.drain()
                        dve.tensor_tensor(scale, scale, normw[:, half, :].unsqueeze(2).to_broadcast([P, DC, B]),
                                          ALU.mult)


class WeightLoader:

    def __init__(self, nc, ctx, name, slots, pieces):
        self.slots, self.pieces = slots, pieces
        self.sem = {s: ctx.enter_context(nc.semaphore(f"{name}_w_{s}")) for s in
                    ["high_done", "low_done"] + [f"in{i}" for i in range(len(slots))]}

    def staged(self, i):
        src = self.pieces[i][0]
        r, c, n = src.shape
        return self.slots[i % len(self.slots)][0:r, 0:c * n].rearrange("p (c n) -> p c n", c=c)

    def load(self, sp):
        for i, (src, _, _) in enumerate(self.pieces):
            k = len(self.slots)
            if i >= k:
                sp.wait_ge(self.sem["low_done"], i - k + 1)
            sp.dma_start(self.staged(i), src).then_inc(self.sem[f"in{i % k}"], 16)

    def high(self, act, i):
        k = len(self.slots)
        act.wait_ge(self.sem[f"in{i % k}"], 16 * (i // k + 1))
        act.activation(self.pieces[i][1], self.staged(i), ACT.Copy).then_inc(self.sem["high_done"], 1)

    def low(self, dve, i):
        dve.wait_ge(self.sem["high_done"], i + 1)
        dve.tensor_tensor(self.pieces[i][2], self.staged(i), self.pieces[i][1].bitcast(F32), ALU.subtract
                          ).then_inc(self.sem["low_done"], 1)

    def ready(self, eng, i):
        eng.wait_ge(self.sem["low_done"], i + 1)


def norm_stats(dve, l, x, stats, mv, t):
    dve.bn_stats(stats[:, t, :], x[:, t, :])
    dve.drain()
    dve.bn_aggr(mv[:, t, :], stats[:, t, :])


def norm_power_input(dve, l, mv, power_in, eps):
    dve.drain()
    if l == 0:
        return dve.tensor_scalar(power_in[:, :], mv[:, :, 1], eps, None, ALU.add)
    dve.tensor_tensor(power_in[:, :], mv[:, :, 0], mv[:, :, 0], ALU.mult)
    dve.drain()
    return dve.scalar_tensor_tensor(out=power_in[:, :], in0=power_in[:, :], scalar=eps, in1=mv[:, :, 1],
                                    op0=ALU.add, op1=ALU.add)


def norm_apply(dve, l, x, mv, rstd, t):
    if l == 0:
        return dve.tensor_scalar(x[:, t, :], x[:, t, :], mv[:, t, 0:1], rstd[:, t:t + 1], ALU.subtract, ALU.mult)
    return dve.tensor_scalar(x[:, t, :], x[:, t, :], rstd[:, t:t + 1], None, ALU.mult)


def attention_opening(l):
    s = [("t", c) for c in range(DC)]
    if l == 1:
        s.append(("tables",))
        for i in range(8):
            s += [("Q", i), ("rope", i)]
        s += [("rope", 8), ("rope", 9)]
    s += [("q", NG), ("k", NG)]
    for t in range(TT):
        s += [("v", t), ("max", NG, t)]
    return s + [("q", NG + 1), ("m", NG), ("k", NG + 1)]


def attention_steps(l, last):
    s = []
    for g in range(NG):
        more = g + 1 < NG or not last
        for kt in range(TT):
            s.append(("s", g, kt, more and kt > 0))
            if g > 0 and kt < 2:
                s.append(("norm", g - 1, kt))
            if g == 0 and kt == 1:
                s.append(("gate_bias",))
            if g == NG - 1 and kt == 2:
                s.append(("residual",))
            if not last:
                if l == 0 and g == 1:
                    s.append(("stats", kt))
                if l == 1 and g == 0 and kt >= 2:
                    s += [("stats", 2 * kt - 4), ("stats", 2 * kt - 3)]
                if l == 1 and g == 1 and kt == 0:
                    s.append(("tables",))
                if l == 1 and g in (1, 2) and kt < TT - 1:
                    i = TT * (g - 1) + kt
                    s += [("Q", i), ("rope", i)]
                if l == 1 and g == 3 and kt < 2:
                    s.append(("rope", 8 + kt))
        if more:
            s.append(("max", g + 1, TT - 1))
        if g == 1 - l and not last:
            s.append(("power",))
        if g + 2 < NG or not last:
            s.append(("q", g + 2))
        if more:
            s.append(("m", g + 1))
        if g + 2 < NG or not last:
            s.append(("k", g + 2))
        if l == 1 and g in (1, 2) and not last:
            i = TT * g - 1
            s += [("Q", i), ("rope", i)]
        s.append(("pv", g))
        if g == 1 - l and not last:
            s += [("apply", t) for t in range(TT)] + [("t", c) for c in range(DC)]
    s += [("norm", NG - 1, 0), ("norm", NG - 1, 1)]
    if not last:
        s += [("v", t) for t in range(TT)]
    return s + [("p", t) for t in range(TT)]


def uses_of(steps):
    return [(s, i % 2) for i, s in enumerate(x for x in steps if x[0] in ("q", "k", "v", "m", "t", "p", "Q"))]


def attention_stage(nc, l, dram, x_in, x_out, mod_rows, modT, ident):
    nm = f"att{l}"
    with ExitStack() as ctx:
        sb = lambda n, s, d=F32: ctx.enter_context(nc.sbuf_tensor(f"{nm}_{n}", s, d))
        w_high, w_low = sb("w_high", [P, DC, 3 * D], F32R), sb("w_low", [P, DC, 3 * D], F32R)
        p_high, p_low = sb("p_high", [P, DC, D], F32R), sb("p_low", [P, DC, D], F32R)
        ones = sb("ones", [P, HD])
        minus_half = sb("minus_half", [P, HEADS])
        keys, queries = sb("keys", [AROWS, 2, GH, N], F32R), sb("queries", [AROWS, 2, GH, N], F32R)
        x = sb("x", [P, TT, D])
        h_full = sb("h_full", [P, N])
        h_high, h_low = sb("h_high", [P, DC, N], F32R), sb("h_low", [P, DC, N], F32R)
        QS = 2 - l
        qk_high, qk_low = sb("qk_high", [P, QS, N], F32R), sb("qk_low", [P, QS, N], F32R)
        values = sb("values", [P, TT, D])
        probs = sb("probs", [P, 2, GH, N])
        o_high, o_low = sb("o_high", [P, DC, N], F32R), sb("o_low", [P, DC, N], F32R)
        tmp2 = sb("tmp2", [P, 2, D])
        gate, gate_bias = sb("gate", [P, D]), sb("gate_bias", [P, D])
        row_max = sb("row_max", [P, 2, GH * TT])
        max_high, max_low = sb("max_high", [GH * TT, 2, P], F32R), sb("max_low", [GH * TT, 2, P], F32R)
        stats, mv = sb("stats", [P, TT, 6]), sb("mv", [P, TT, 2])
        power_in, rstd = sb("power_in", [P, TT]), sb("rstd", [P, TT])
        if l == 1:
            cos_t, sin_t = sb("cos_t", [P, B * TT, PAIRS]), sb("sin_t", [P, B * TT, PAIRS])
            w_turn = sb("w_turn", [P, 2, PAIRS, 2])
            w_swap = sb("w_swap", [P, 2, PAIRS, 2])
            qk_nat = sb("qk_nat", [P, 2, TT, N])
            turn, swap = sb("turn", [P, TT, 2, PAIRS, 2]), sb("swap", [P, TT, 2, PAIRS, 2])
            squares, turned, swapped = sb("squares", [P, N]), sb("turned", [P, N]), sb("swapped", [P, N])
            ssum, sinv = sb("ssum", [P, 2, HEADS]), sb("sinv", [P, 2, HEADS])
            room = values[:].rearrange("p t n -> p (t n)")
            n_ang = B * TT * 15
            angle, turns, part = (room[:, i * n_ang:(i + 1) * n_ang] for i in range(3))
            pos = room[:, 3 * n_ang:3 * n_ang + B * TT * 3].rearrange("p (t a) -> p t a", a=3)
            freqs = room[:, 3 * n_ang + 96:3 * n_ang + 101]
            wrow = room[:, 3 * n_ang + 104:3 * n_ang + 104 + 2 * HD].rearrange("p (s a e) -> p s a e", s=2, e=2)

        st = Stage(nc, ctx, nm, 8, [
            "filled", "free0", "free1", "max_filled", "max_free", "score_filled", "exp_done", "pv_done", "o_read",
            "o_ready", "high_done", "max_high_done", "stacked0", "stacked1", "rows0", "rows1", "x_loaded",
            "power_ready", "rstd_ready", "x_normed", "h_full_done", "h_ready", "res_loaded", "gate_loaded",
            "x_done", "stored", "noted", "consts"]
            + ["nat_done", "sum_ready", "inv_ready", "scaled", "swap_done", "roped", "tables_ready",
               "tab_in", "tab_reduced", "tab_sin", "tab_ready"] * l)
        gen, mxb, scb = st.bank[0:2], st.bank[2:4], st.bank[4:6]
        o_acc, s_acc = st.bank[6], st.bank[7]
        before = uses_of(attention_opening(l))
        per = uses_of(attention_steps(l, False))

        def banks_for(b, last):
            return Banks(before, per, uses_of(attention_steps(l, last)), b)

        wv = dram[f"w_qkv{l}"].rearrange("(c p) n -> p c n", p=P)
        blocks = [(wv[:, :, i * D:(i + 1) * D], w_high[:, :, i * D:(i + 1) * D], w_low[:, :, i * D:(i + 1) * D])
                  for i in range(3)]
        blocks.append((dram[f"w_proj{l}"].rearrange("(c p) n -> p c n", p=P), p_high[:], p_low[:]))
        weights = WeightLoader(nc, ctx, nm, [probs[:, i, :, :].rearrange("p h n -> p (h n)") for i in range(2)], blocks)
        block = ctx.enter_context(nc.Block())

        @block.tensor
        def _(pe):
            def claim(u, key):
                pe.wait_ge(st[f"free{u.bank(key)}"], u.freed_before(key))
                return gen[u.bank(key)]

            def split_product(out, terms):
                for i, (sh, sl, mh, ml) in enumerate(terms):
                    pe.matmul(out, sh, mh, start=(i == 0), stop=False)
                    pe.matmul(out, sh, ml, start=False, stop=False)
                    mm = pe.matmul(out, sl, mh, start=False, stop=(i == len(terms) - 1))
                return mm

            def run(b, steps, u):
                opening = u.opening

                def max_products(g, i, tiles):
                    for qt in tiles:
                        pe.wait_ge(st["max_free"], b * 64 + (16 * g + 4 * i + qt + 1))
                        pe.matmul(mxb[qt % 2][:], queries[0:KROWS, g % 2, i, qt * P:(qt + 1) * P],
                                  keys[0:KROWS, g % 2, i, :], start=True, stop=True).then_inc(st["max_filled"], 1)

                def score_products(g, kt, heads):
                    for h in heads:
                        pe.wait_ge(st["exp_done"], b * 64 + (16 * g + 4 * kt + h + 1))
                        pe.matmul(scb[h % 2][:], keys[0:AROWS, g % 2, h, kt * P:(kt + 1) * P],
                                  queries[0:AROWS, g % 2, h, :], start=True, stop=True
                                  ).then_inc(st["score_filled"], 1)

                def values_product(g, kt):
                    pe.wait_ge(st["exp_done"], b * 64 + (16 * g + 4 * kt + 4 + 2))
                    if kt == 0:
                        pe.wait_ge(st["o_read"], b * NG + (g + 1))
                        if g == 0:
                            for i in range(2):
                                pe.wait_ge(st[f"free{i}"], u.all_before(i))
                    for h in range(GH):
                        pe.matmul(o_acc[HD * h:HD * (h + 1), :], values[:, kt, (GH * g + h) * HD:(GH * g + h + 1) * HD],
                                  probs[:, kt % 2, h, :], start=(kt == 0), stop=(kt == TT - 1))

                def sums_product(g, kt):
                    for h in range(GH):
                        mm = pe.matmul(s_acc[HD * h:HD * (h + 1), :], ones[:], probs[:, kt % 2, h, :],
                                       start=(kt == 0), stop=(kt == TT - 1))
                    mm.then_inc(st["pv_done"], 1)

                def stacked(g):
                    pe.wait_ge(st[f"stacked{g % 2}"], b * 192 + (96 * (g // 2) + 96))

                for step in steps:
                    kind = step[0]
                    if kind == "t":
                        c = step[1]
                        if c == 0:
                            pe.wait_ge(st["x_normed"], b * TT + 2 * TT)
                        g = claim(u, step)
                        for t in range(TT):
                            mm = pe.transpose(g[:, t * P:(t + 1) * P], x[:, t, c * P:(c + 1) * P], ident[:])
                        mm.then_inc(st["filled"], 1)
                    elif kind == "Q":
                        half, t = divmod(step[1], TT)
                        g = claim(u, step)
                        if step[1] == 0:
                            pe.wait_ge(st["h_ready"], b * DC + (2 * DC + 1))
                        if opening and t == 0:
                            weights.ready(pe, half)
                        split_product(g[:], [(h_high[:, c, t * P:(t + 1) * P], h_low[:, c, t * P:(t + 1) * P],
                                              w_high[:, c, half * D:(half + 1) * D],
                                              w_low[:, c, half * D:(half + 1) * D])
                                             for c in range(DC)]).then_inc(st["filled"], 1)
                    elif kind in ("q", "k") and l == 0:
                        i = ("q", "k").index(kind)
                        a = i * D + (step[1] % NG) * P
                        if step == ("q", NG):
                            pe.wait_ge(st["h_ready"], b * DC + (2 * DC + 1))
                        if opening:
                            weights.ready(pe, i)
                        g = claim(u, step)
                        split_product(g[:], [(w_high[:, c, a:a + P], w_low[:, c, a:a + P],
                                              h_high[:, c, :], h_low[:, c, :])
                                             for c in range(DC)]).then_inc(st["filled"], 1)
                    elif kind in ("q", "k"):
                        gi = step[1] % NG
                        half, a = gi // 2, ("q", "k").index(kind) * 256 + (gi % 2) * P
                        if kind == "q" and gi % 2 == 0:
                            pe.wait_ge(st["roped"], b * 8 + (5 + 8 if gi == 0 else 9))
                        g = claim(u, step)
                        for t in range(TT):
                            mm = pe.transpose(g[:, t * P:(t + 1) * P], qk_nat[:, half, t, a:a + P], ident[:])
                        mm.then_inc(st["filled"], 1)
                    elif kind == "v":
                        t = step[1]
                        if opening and t == 0:
                            weights.ready(pe, 2)
                        g = claim(u, step)
                        split_product(g[:], [(h_high[:, c, t * P:(t + 1) * P], h_low[:, c, t * P:(t + 1) * P],
                                              w_high[:, c, 2 * D:3 * D], w_low[:, c, 2 * D:3 * D])
                                             for c in range(DC)]).then_inc(st["filled"], 1)
                    elif kind == "max":
                        if opening and step[2] == 0:
                            stacked(step[1])
                        max_products(step[1], step[2], range(TT))
                    elif kind == "m":
                        gi = step[1]
                        g = claim(u, step)
                        pe.wait_ge(st["max_free"], b * 64 + (16 * gi + 18))
                        pe.transpose(g[0:GH * TT, 0:P], row_max[:, gi % 2, :], ident[:]).then_inc(st["filled"], 1)
                    elif kind == "s":
                        gi, kt, with_max = step[1:]
                        if kt == 0:
                            pe.wait_ge(st[f"rows{gi % 2}"], b * 64 + (32 * (gi // 2) + 32))
                        if kt == 1 and with_max:
                            stacked(gi + 1)
                        score_products(gi, kt, (0, 1))
                        if with_max:
                            max_products(gi + 1, kt - 1, (0, 1))
                        if kt:
                            values_product(gi, kt - 1)
                        score_products(gi, kt, (2, 3))
                        if with_max:
                            max_products(gi + 1, kt - 1, (2, 3))
                        if kt:
                            sums_product(gi, kt - 1)
                    elif kind == "pv":
                        values_product(step[1], TT - 1)
                        sums_product(step[1], TT - 1)
                    elif kind == "p":
                        t = step[1]
                        if t == 0:
                            pe.wait_ge(st["o_ready"], b * 8 + 8)
                        g = claim(u, step)
                        split_product(g[:], [(o_high[:, c, t * P:(t + 1) * P], o_low[:, c, t * P:(t + 1) * P],
                                              p_high[:, c, :], p_low[:, c, :])
                                             for c in range(DC)]).then_inc(st["filled"], 1)

            pe.sem_inc(st["free0"], 1)
            pe.sem_inc(st["free1"], 1)
            pe.sem_inc(st["max_free"], 2)
            pe.sem_inc(st["exp_done"], 2)
            pe.sem_inc(st["pv_done"], 2)
            pe.sem_inc(st["o_read"], 1)
            pe.wait_ge(st["consts"], 1)
            run(-1, attention_opening(l), Banks(before, per, None, None))
            weights.ready(pe, 3)
            over_sequences(pe, lambda b, last: run(b, attention_steps(l, last), banks_for(b, last)))

        @block.scalar
        def _(act):
            def run(b, steps, u):
                for step in steps:
                    kind = step[0]
                    if kind in ("t", "Q", "q", "k", "v", "m"):
                        g = gen[u.bank(step)]
                        freed = st[f"free{u.bank(step)}"]
                        act.wait_ge(st["filled"], u.filled(step))
                    if kind == "t":
                        c = step[1]
                        act.wait_ge(st["h_ready"], b * DC + (DC + c + 1))
                        act.activation(h_full[:], g[:], ACT.Identity, bias=modT[:, l, c, ds(b + 1, 1)],
                                       scale=modT[:, l, 4 + c, ds(b + 1, 1)]).then_inc(st["h_full_done"], 1)
                    elif kind == "Q":
                        half, t = divmod(step[1], TT)
                        act.activation(qk_nat[:, half, t, :], g[:], ACT.Copy).then_inc(st["nat_done"], 1)
                        act.wait_ge(st["sum_ready"], b * 8 + (8 + step[1] + 1))
                        act.activation(squares[:], g[:], ACT.Square).then_inc(freed, 1)
                    elif kind in ("q", "k"):
                        i = ("q", "k").index(kind)
                        if QS == 1 and i == 1:
                            act.wait_ge(st[f"stacked{step[1] % 2}"], b * 192 + (96 * (step[1] // 2) + 48))
                        act.activation(qk_high[:, i % QS, :], g[:], ACT.Copy).then_inc(st["high_done"], 1)
                    elif kind == "v":
                        act.activation(values[:, step[1], :], g[:], ACT.Copy).then_inc(freed, 1)
                    elif kind == "m":
                        act.activation(max_high[:, step[1] % 2, :], g[0:GH * TT, 0:P], ACT.Copy, scale=-1.0
                                       ).then_inc(st["max_high_done"], 1)
                    elif kind == "s":
                        gi, kt = step[1], step[2]
                        act.wait_ge(st["pv_done"], b * 16 + (4 * gi + kt + 1))
                        for h in range(GH):
                            act.wait_ge(st["score_filled"], b * 64 + (16 * gi + 4 * kt + h + 1))
                            act.activation(probs[:, kt % 2, h, :], scb[h % 2][:], ACT.Exp, scale=SCALE
                                           ).then_inc(st["exp_done"], 1)
                    elif kind == "pv":
                        gi = step[1]
                        if gi == 0:
                            act.wait_ge(st["x_done"], b * TT + 2)
                        else:
                            act.wait_ge(st["o_ready"], b * 8 + 2 * gi)
                        act.wait_ge(st["pv_done"], b * 16 + (4 * gi + 4 + 2))
                        act.activation(tmp2[:, 0, :], s_acc[:], ACT.Copy)
                        act.activation(tmp2[:, 1, :], o_acc[:], ACT.Copy).then_inc(st["o_read"], 1)

            act.sem_inc(st["h_ready"], 1)
            if l == 1:
                act.sem_inc(st["sum_ready"], 1)
                for k, out in enumerate((sin_t, cos_t)):
                    act.wait_ge(st["tab_reduced"], k + 1)
                    act.activation(out[:, :, 0:15], part.rearrange("p (t f) -> p t f", f=15), ACT.Sin
                                   ).then_inc(st["tab_sin"], 1)
            weights.high(act, 0)
            steps = attention_opening(l)
            u = Banks(before, per, None, None)
            run(-1, steps[0:DC], u)
            for i in range(1, len(blocks)):
                weights.high(act, i)
            run(-1, steps[DC:], u)
            weights.ready(act, len(blocks) - 1)
            over_sequences(act, lambda b, last: run(b, attention_steps(l, last), banks_for(b, last)))

        @block.vector
        def _(dve):
            def run(b, steps, u):
                def maxima(g, i):
                    for qt in range(TT):
                        dve.wait_ge(st["max_filled"], b * 64 + (16 * g + 4 * i + qt + 1))
                        dve.tensor_reduce(row_max[:, g % 2, 4 * i + qt:4 * i + qt + 1], mxb[qt % 2][:],
                                          AX.X, ALU.max).then_inc(st["max_free"], 1)

                for step in steps:
                    kind = step[0]
                    if kind in ("t", "Q", "q", "k", "m", "p"):
                        g = gen[u.bank(step)]
                        freed = st[f"free{u.bank(step)}"]
                    if kind == "t":
                        c = step[1]
                        dve.wait_ge(st["h_full_done"], b * DC + (DC + c + 1))
                        dve.tensor_copy(h_high[:, c, :], h_full[:]).then_inc(freed, 1)
                        dve.drain()
                        dve.tensor_tensor(h_low[:, c, :], h_full[:], h_high[:, c, :].bitcast(F32), ALU.subtract
                                          ).then_inc(st["h_ready"], 1)
                    elif kind == "rope":
                        i = step[1]
                        if i < 8:
                            key = ("Q", i)
                            dve.wait_ge(st[f"free{u.bank(key)}"], u.released(key))
                            dve.tensor_reduce(ssum[:, i % 2, :], squares[:].rearrange("p (h d) -> p h d", d=HD),
                                              AX.X, ALU.add)
                            dve.drain()
                            dve.tensor_scalar(ssum[:, i % 2, :], ssum[:, i % 2, :], 1.0 / HD, EPS[1], ALU.mult, ALU.add
                                              ).then_inc(st["sum_ready"], 1)
                        if i >= 2:
                            half, t = divmod(i - 2, TT)
                            dve.wait_ge(st["swap_done"], b * 8 + (8 + i - 1))
                            apart = lambda v: v.rearrange("p (r h d) -> p r h d", r=4, d=HD)
                            dve.tensor_tensor(qk_nat[:, half, t, :].rearrange("p (r d h) -> p r h d", r=4, d=HD),
                                              apart(turned[:]), apart(swapped[:]), ALU.add).then_inc(st["roped"], 1)
                            dve.drain()
                        if 1 <= i < 9:
                            half, t = divmod(i - 1, TT)
                            nat = qk_nat[:, half, t, :]
                            dve.wait_ge(st["inv_ready"], b * 8 + (8 + i))
                            dve.tensor_tensor(nat.rearrange("p (h d) -> p h d", d=HD), nat.rearrange("p (h d) -> p h d", d=HD),
                                              sinv[:, (i - 1) % 2, :].unsqueeze(2).to_broadcast([P, HEADS, HD]), ALU.mult
                                              ).then_inc(st["scaled"], 1)
                            dve.drain()
                            dve.tensor_tensor(turned[:].rearrange("p (s h d) -> p s h d", s=2, d=HD),
                                              nat.rearrange("p (s h d) -> p s h d", s=2, d=HD),
                                              turn[:, t, :, :, :].rearrange("p s a e -> p s (a e)").unsqueeze(2)
                                              .to_broadcast([P, 2, HEADS // 2, HD]), ALU.mult)
                            dve.drain()
                    elif kind in ("q", "k"):
                        i = ("q", "k").index(kind)
                        dve.wait_ge(st["high_done"], b * 8 + (2 * step[1] + i + 1))
                        dve.tensor_tensor(qk_low[:, i % QS, :], g[:], qk_high[:, i % QS, :].bitcast(F32), ALU.subtract
                                          ).then_inc(freed, 1)
                    elif kind == "m":
                        gi = step[1]
                        dve.wait_ge(st["max_high_done"], b * NG + (gi + 1))
                        dve.scalar_tensor_tensor(out=max_low[:, gi % 2, :], in0=g[0:GH * TT, 0:P], scalar=-1.0,
                                                 in1=max_high[:, gi % 2, :].bitcast(F32), op0=ALU.mult,
                                                 op1=ALU.subtract).then_inc(freed, 1)
                    elif kind == "max":
                        maxima(step[1], step[2])
                    elif kind == "s" and step[3]:
                        maxima(step[1] + 1, step[2] - 1)
                    elif kind == "norm":
                        gi, a = step[1], step[2] * (N // 2)
                        cols = slice(a, a + N // 2)
                        dve.wait_ge(st["o_read"], b * NG + (gi + 2))
                        dve.reciprocal(tmp2[:, 0, cols], tmp2[:, 0, cols])
                        dve.drain()
                        dve.tensor_tensor(tmp2[:, 1, cols], tmp2[:, 1, cols], tmp2[:, 0, cols], ALU.mult)
                        dve.drain()
                        dve.tensor_copy(o_high[:, gi, cols], tmp2[:, 1, cols])
                        dve.drain()
                        dve.tensor_tensor(o_low[:, gi, cols], tmp2[:, 1, cols], o_high[:, gi, cols].bitcast(F32),
                                          ALU.subtract).then_inc(st["o_ready"], 1)
                    elif kind == "stats":
                        if step[1] == 0:
                            dve.wait_ge(st["x_loaded"], b * 16 + 32)
                        norm_stats(dve, l, x, stats, mv, step[1])
                    elif kind == "power":
                        norm_power_input(dve, l, mv, power_in, EPS[l]).then_inc(st["power_ready"], 1)
                    elif kind == "apply":
                        if step[1] == 0:
                            dve.wait_ge(st["rstd_ready"], b + 2)
                        norm_apply(dve, l, x, mv, rstd, step[1]).then_inc(st["x_normed"], 1)
                    elif kind == "p":
                        t = step[1]
                        if t == 0:
                            dve.drain()
                            dve.wait_ge(st["gate_loaded"], b * 32 + 32)
                        dve.wait_ge(st["filled"], u.filled(step))
                        dve.wait_ge(st["x_done"], b * TT + (t + 1))
                        dve.tensor_tensor(tmp2[:, t % 2, :], g[:], gate[:], ALU.mult).then_inc(freed, 1)

            dve.sem_inc(st["x_done"], 2)
            if l == 1:
                dve.sem_inc(st["roped"], 1)
                dve.wait_ge(st["tab_in"], 64)
                dve.tensor_copy(w_turn[:], wrow)
                dve.tensor_copy(w_swap[:, :, :, 1], wrow[:, :, :, 0])
                dve.tensor_scalar(w_swap[:, :, :, 0], wrow[:, :, :, 1], -1.0, None, ALU.mult)
                dve.memset(cos_t[:, :, 15:16], 1.0)
                dve.memset(sin_t[:, :, 15:16], 0.0)
                dve.tensor_tensor(angle.rearrange("p (t a f) -> p t a f", a=3, f=5),
                                  pos.unsqueeze(3).to_broadcast([P, B * TT, 3, 5]),
                                  freqs.unsqueeze(1).unsqueeze(1).to_broadcast([P, B * TT, 3, 5]), ALU.mult)
                for k, shift in enumerate((0.0, 0.25)):
                    dve.drain()
                    if k == 1:
                        dve.wait_ge(st["tab_sin"], 1)
                    dve.tensor_scalar(turns, angle, 1.0 / TWO_PI, shift, ALU.mult, ALU.add)
                    dve.drain()
                    dve.tensor_scalar(turns, turns, ROUND, None, ALU.add)
                    dve.drain()
                    dve.tensor_scalar(turns, turns, -ROUND, None, ALU.add)
                    dve.drain()
                    dve.scalar_tensor_tensor(out=part, in0=turns, scalar=-PI_A, in1=angle, op0=ALU.mult, op1=ALU.add)
                    for piece in (PI_B, PI_C):
                        dve.drain()
                        dve.scalar_tensor_tensor(out=part, in0=turns, scalar=-piece, in1=part,
                                                 op0=ALU.mult, op1=ALU.add)
                    dve.drain()
                    dve.tensor_scalar(part, part, TWO_PI * shift, 3.1415925, ALU.add, ALU.min)
                    dve.drain()
                    dve.tensor_scalar(part, part, -3.1415925, None, ALU.max).then_inc(st["tab_reduced"], 1)
                dve.drain().then_inc(st["tab_ready"], 1)
            run(-1, [("stats", t) for t in range(TT)] + [("power",)] + [("apply", t) for t in range(TT)], None)
            weights.low(dve, 0)
            steps = attention_opening(l)
            u = Banks(before, per, None, None)
            run(-1, steps[0:DC], u)
            for i in range(1, len(blocks)):
                weights.low(dve, i)
            run(-1, steps[DC:], u)
            over_sequences(dve, lambda b, last: run(b, attention_steps(l, last), banks_for(b, last)))

        @block.gpsimd
        def _(pool):
            def run(b, steps, u):
                for step in steps:
                    kind = step[0]
                    if kind == "tables":
                        wait_and_note(pool, st["roped"], b * 8 + (8 + 1), st["noted"])
                        for table, w, trig in ((turn, w_turn, cos_t), (swap, w_swap, sin_t)):
                            for s in range(2):
                                for e in range(2):
                                    pool.tensor_tensor(table[:, :, s, :, e], trig[:, ds(b * TT + TT, TT), :],
                                                       w[:, s, :, e].unsqueeze(1).to_broadcast([P, TT, PAIRS]),
                                                       ALU.mult).then_inc(st["tables_ready"], 1)
                        wait_and_note(pool, st["tables_ready"], b * 8 + 16, st["noted"])
                    elif kind == "rope":
                        i = step[1]
                        if i < 8:
                            wait_and_note(pool, st["sum_ready"], b * 8 + (8 + i + 2), st["noted"])
                            pool.tensor_tensor(sinv[:, i % 2, :], ssum[:, i % 2, :], minus_half[:], ALU.pow
                                               ).then_inc(st["inv_ready"], 1)
                        if 1 <= i < 9:
                            half, t = divmod(i - 1, TT)
                            nat = qk_nat[:, half, t, :].rearrange("p (s h a e) -> p s h a e", s=2, e=2, a=PAIRS)
                            out = swapped[:].rearrange("p (s h a e) -> p s h a e", s=2, e=2, a=PAIRS)
                            wait_and_note(pool, st["scaled"], b * 8 + (8 + i), st["noted"])
                            for s in range(2):
                                for e in range(2):
                                    mult = pool.tensor_tensor(
                                        out[:, s, :, :, e], nat[:, s, :, :, 1 - e],
                                        swap[:, t, s, :, e].unsqueeze(1).to_broadcast([P, HEADS // 2, PAIRS]),
                                        ALU.mult)
                            mult.then_inc(st["swap_done"], 1)
                    elif kind == "power":
                        wait_and_note(pool, st["power_ready"], b + 2, st["noted"])
                        pool.tensor_tensor(rstd[:], power_in[:], minus_half[:, 0:TT], ALU.pow
                                           ).then_inc(st["rstd_ready"], 1)
                    elif kind == "gate_bias":
                        wait_and_note(pool, st["gate_loaded"], b * 32 + 32, st["noted"])
                        pool.tensor_tensor(gate_bias[:], gate_bias[:], gate[:], ALU.mult)
                        pool.drain()
                    elif kind == "residual":
                        wait_and_note(pool, st["res_loaded"], b * 16 + 16, st["noted"])
                        for t in range(TT):
                            pool.tensor_tensor(x[:, t, :], x[:, t, :], gate_bias[:], ALU.add)
                        pool.drain()
                    elif kind == "p":
                        t = step[1]
                        wait_and_note(pool, st[f"free{u.bank(step)}"], u.released(step), st["noted"])
                        pool.tensor_tensor(x[:, t, :], x[:, t, :], tmp2[:, t % 2, :], ALU.add
                                           ).then_inc(st["x_done"], 1)

            pool.memset(ones[:], 1.0)
            pool.memset(minus_half[:], -0.5)
            pool.drain()
            pool.memset(keys[KROWS:AROWS, :, :, :].bitcast(F32), 1.0)
            pool.drain().then_inc(st["consts"], 1)
            if l == 1:
                pool.dma_start(pos, dram["pos"]).then_inc(st["tab_in"], 16)
                pool.dma_start(freqs, dram["freqs"]).then_inc(st["tab_in"], 16)
                for k in range(2):
                    pool.dma_start(wrow[:, k, :, :].rearrange("p a b -> p (a b)"),
                                   dram["qk_norm"][k:k + 1, :].to_broadcast([P, HD])).then_inc(st["tab_in"], 16)
            run(-1, [("power",)], None)
            if l == 1:
                pool.wait_ge(st["tab_ready"], 1)
                pool.wait_ge(st["tab_sin"], 2)
            run(-1, attention_opening(l), Banks(before, per, None, None))
            over_sequences(pool, lambda b, last: run(b, attention_steps(l, last), banks_for(b, last)))

        @block.sync
        def _(sp):
            def run(b, steps, u):
                for step in steps:
                    kind = step[0]
                    if kind in ("q", "k"):
                        gi, i = step[1], ("q", "k").index(kind)
                        target = (queries, keys)[i]
                        layout = ((qk_high, qk_low, qk_high), (qk_high, qk_high, qk_low))[i]
                        wait_and_note(sp, st[f"free{u.bank(step)}"], u.released(step), st["noted"])
                        for r, src in enumerate(layout):
                            sp.dma_start(target[HD * r:HD * (r + 1), gi % 2, :, :].rearrange("p h n -> p (h n)")
                                         .bitcast(F32), src[:, i % QS, :].bitcast(F32)
                                         ).then_inc(st[f"stacked{gi % 2}"], 16)
                    elif kind == "m":
                        gi = step[1]
                        wait_and_note(sp, st[f"free{u.bank(step)}"], u.released(step), st["noted"])
                        for r, src in enumerate((max_high, max_low)):
                            sp.dma_start(queries[KROWS + r:KROWS + r + 1, gi % 2, :, :].rearrange("p h n -> p (h n)")
                                         .bitcast(F32), src[:, gi % 2, :].bitcast(F32)
                                         ).then_inc(st[f"rows{gi % 2}"], 16)
                    elif kind == "t" and step[1] == DC - 1:
                        wait_and_note(sp, st["filled"], u.filled(step), st["noted"])
                        if not u.opening:
                            sp.dma_start(x[:], seq_view(x_in, b)).then_inc(st["res_loaded"], 16)
                    elif kind == "p":
                        t = step[1]
                        wait_and_note(sp, st["x_done"], b * TT + (t + 1 + 2), st["noted"])
                        sp.dma_start(x_out[ds(b, 1), t * P:(t + 1) * P, :].rearrange("o p d -> p (o d)"), x[:, t, :]
                                     ).then_inc(st["stored"], 16)

            def body(b, last):
                wait_and_note(sp, st["stored"], b * 64 + 16, st["noted"])
                if not last:
                    sp.dma_start(x[:], seq_view(x_in, b + 1)).then_inc(st["x_loaded"], 16)
                else:
                    sp.dma_start(x[:], seq_view(x_in, b)).then_inc(st["res_loaded"], 16)
                sp.dma_start(gate[:], mod_rows[l, ds(b, 1), 2 * D:3 * D].to_broadcast([P, D])
                             ).then_inc(st["gate_loaded"], 16)
                sp.dma_start(gate_bias[:], dram[f"b_proj{l}"].rearrange("(o n) -> o n", o=1).to_broadcast([P, D])
                             ).then_inc(st["gate_loaded"], 16)
                run(b, attention_steps(l, last), banks_for(b, last))

            sp.sem_inc(st["stored"], 16)
            sp.dma_start(x[:], seq_view(x_in, 0)).then_inc(st["x_loaded"], 16)
            weights.load(sp)
            run(-1, attention_opening(l), Banks(before, per, None, None))
            over_sequences(sp, body)
            sp.wait_ge(st["stored"], 16 + 64 * B)


def mlp_steps(l, last):
    chunks = -(-HID[l] // P)
    turn_at = chunks - 5
    s = []
    for j in range(chunks):
        s.append(("a", j))
        if l == 1:
            s.append(("g", j))
        if not last and 1 <= j <= 4:
            s.append(("stats", j - 1))
        if j >= 2 and j < chunks - 1:
            s.append(("c", j - 2))
        if not last and j == 4:
            s.append(("power",))
        if not last and j == 5:
            s += [("apply", t) for t in range(TT)]
        if not last and j == turn_at:
            s += [("t", c) for c in range(DC)]
    if not last:
        s.append(("split",))
    s += [("c", j) for j in (chunks - 3, chunks - 2, chunks - 1)]
    return s + [("p", t) for t in range(TT)]


def mlp_uses(steps):
    bank = {"a": 0, "g": 2, "t": 2}
    return [(s, bank[s[0]] + s[1] % 2) for s in steps if s[0] in bank]


def mlp_stage(nc, l, dram, x_in, x_out, mod_rows, modT, ident):
    nm = f"mlp{l}"
    hid = HID[l]
    chunks = -(-hid // P)
    width = lambda j: min(P, hid - j * P)
    with ExitStack() as ctx:
        sb = lambda n, s, d=F32: ctx.enter_context(nc.sbuf_tensor(f"{nm}_{n}", s, d))
        ups = ["a"] if l == 0 else ["a", "g"]
        up_high = {k: sb(f"up_{k}_high", [P, DC, hid], F32R) for k in ups}
        up_low = {k: sb(f"up_{k}_low", [P, DC, hid], F32R) for k in ups}
        dn_high, dn_low = sb("dn_high", [P, chunks, D], F32R), sb("dn_low", [P, chunks, D], F32R)
        minus_half = sb("minus_half", [P, TT])
        hid_bias = sb("hid_bias", [P, chunks])
        staging = sb("staging", [P, 2, DC * D])

        down = dram[f"down{l}"]
        up_piece, down_piece, pieces = {}, {}, []
        for j in range(0, chunks, 4):
            a, e = j * P, min((j + 4) * P, hid)
            for k in ups:
                up_piece[k, j // 4] = len(pieces)
                pieces.append((dram[f"up_{k}{l}"].rearrange("(c p) n -> p c n", p=P)[:, :, a:e],
                               up_high[k][:, :, a:e], up_low[k][:, :, a:e]))
            full = (e - a) // P
            down_piece[j // 4] = len(pieces)
            pieces.append((down[a:a + full * P, :].rearrange("(c p) n -> p c n", p=P),
                           dn_high[:, j:j + full, :], dn_low[:, j:j + full, :]))
            if a + full * P < e:
                rest = e - a - full * P
                down_piece["rest"] = len(pieces)
                pieces.append((down[a + full * P:e, :].rearrange("(c p) n -> p c n", c=1),
                               dn_high[0:rest, j + full:j + full + 1, :], dn_low[0:rest, j + full:j + full + 1, :]))
        weights = WeightLoader(nc, ctx, nm, [staging[:, i, :] for i in range(2)], pieces)

        x = sb("x", [P, TT, D])
        h_full = sb("h_full", [P, DC, N])
        h_high, h_low = sb("h_high", [P, DC, N], F32R), sb("h_low", [P, DC, N], F32R)
        hid_full = sb("hid_full", [P, 2, N])
        hid_high, hid_low = sb("hid_high", [P, 3, N], F32R), sb("hid_low", [P, 3, N], F32R)
        tmp2 = sb("tmp2", [P, 2, D])
        gate = sb("gate", [P, D])
        gate_bias = sb("gate_bias", [P, D]) if l == 0 else None
        stats, mv = sb("stats", [P, TT, 6]), sb("mv", [P, TT, 2])
        power_in, rstd = sb("power_in", [P, TT]), sb("rstd", [P, TT])
        st = Stage(nc, ctx, nm, 8, [
            "filled", "free0", "free1", "free2", "free3", "down_done", "acc_done", "x_loaded",
            "power_ready", "rstd_ready", "x_normed", "h_high_done", "h_ready", "hid_ready", "res_loaded", "gate_loaded", "gated", "x_done", "stored", "noted", "const_set", "bias_loaded"])
        ring, acc = st.bank[0:4], st.bank[4:8]
        before = mlp_uses([("t", c) for c in range(DC)])
        per = mlp_uses(mlp_steps(l, False))
        banks_for = lambda b, last: Banks(before, per, mlp_uses(mlp_steps(l, last)), b)
        loads = 32 if l == 0 else 16
        block = ctx.enter_context(nc.Block())

        def hid_slot(j):
            return j % 3

        def hid_full_slot(j):
            return j % 2

        def slot_free(b, j, slots):
            if j >= slots:
                return b * chunks + (j + 1)
            last_use = max(i for i in range(chunks) if i % slots == j)
            return b * chunks + (slots - (chunks - 1 - last_use))

        @block.tensor
        def _(pe):
            for i in range(4):
                pe.sem_inc(st[f"free{i}"], 1)
            pe.sem_inc(st["gated"], TT)
            pe.sem_inc(st["down_done"], 3)

            def turn_x(u, key):
                c = key[1]
                g = ring[u.bank(key)]
                pe.wait_ge(st[f"free{u.bank(key)}"], u.freed_before(key))
                for t in range(TT):
                    mm = pe.transpose(g[:, t * P:(t + 1) * P], x[:, t, c * P:(c + 1) * P], ident[:])
                mm.then_inc(st["filled"], 1)

            def first():
                u = Banks(before, per, None, None)
                pe.wait_ge(st["x_normed"], TT)
                for c in range(DC):
                    turn_x(u, ("t", c))

            def body(b, last):
                u = banks_for(b, last)
                for step in mlp_steps(l, last):
                    kind = step[0]
                    if kind in ("a", "g"):
                        j = step[1]
                        w = width(j)
                        g = ring[u.bank(step)]
                        pe.wait_ge(st[f"free{u.bank(step)}"], u.freed_before(step))
                        if j == 0 and kind == "a":
                            pe.wait_ge(st["h_ready"], b * DC + DC)
                        if j % 4 == 0:
                            weights.ready(pe, up_piece[kind, j // 4])
                        for c in range(DC):
                            wh = up_high[kind][:, c, j * P:j * P + w]
                            wl = up_low[kind][:, c, j * P:j * P + w]
                            pe.matmul(g[0:w, :], wh, h_high[:, c, :], start=(c == 0), stop=False)
                            pe.matmul(g[0:w, :], wh, h_low[:, c, :], start=False, stop=False)
                            mm = pe.matmul(g[0:w, :], wl, h_high[:, c, :], start=False, stop=(c == DC - 1))
                        mm.then_inc(st["filled"], 1)
                    elif kind == "c":
                        j = step[1]
                        w = width(j)
                        pe.wait_ge(st["hid_ready"], b * chunks + (j + 1 + 2))
                        if j == 0:
                            pe.wait_ge(st["gated"], b * TT + TT)
                        if j % 4 == 0:
                            weights.ready(pe, down_piece[j // 4])
                        if w < P:
                            weights.ready(pe, down_piece["rest"])
                        for t in range(TT):
                            hh = hid_high[0:w, hid_slot(j), t * P:(t + 1) * P]
                            hl = hid_low[0:w, hid_slot(j), t * P:(t + 1) * P]
                            pe.matmul(acc[t][:], hh, dn_high[0:w, j, :], start=(j == 0), stop=False)
                            pe.matmul(acc[t][:], hh, dn_low[0:w, j, :], start=False, stop=False)
                            mm = pe.matmul(acc[t][:], hl, dn_high[0:w, j, :], start=False, stop=(j == chunks - 1))
                            if j == chunks - 1 and t < TT - 1:
                                mm.then_inc(st["acc_done"], 1)
                        mm.then_inc(st["down_done"], 1)
                    elif kind == "t":
                        if step[1] == 0:
                            pe.wait_ge(st["x_normed"], b * TT + 2 * TT)
                        turn_x(u, step)

            over_sequences(pe, body, first)

        @block.scalar
        def _(act):
            act.sem_inc(st["hid_ready"], 2)

            def modulate(u, key, nb):
                c = key[1]
                act.wait_ge(st["filled"], u.filled(key))
                act.activation(h_full[:, c, :], ring[u.bank(key)][:], ACT.Identity, bias=modT[:, l, 8 + c, ds(nb, 1)],
                               scale=modT[:, l, 12 + c, ds(nb, 1)]
                               ).then_inc(st[f"free{u.bank(key)}"], 1)

            def high_h(u):
                for c in range(DC):
                    act.wait_ge(st[f"free{u.bank(('t', c))}"], u.released(("t", c)))
                    act.activation(h_high[:, c, :], h_full[:, c, :], ACT.Copy).then_inc(st["h_high_done"], 1)

            def first():
                u = Banks(before, per, None, None)
                for c in range(DC):
                    modulate(u, ("t", c), 0)
                high_h(u)
                for i in range(len(pieces)):
                    weights.high(act, i)
                if l == 0:
                    act.wait_ge(st["bias_loaded"], 16)

            def body(b, last):
                u = banks_for(b, last)
                for step in mlp_steps(l, last):
                    kind = step[0]
                    if kind == "a":
                        j = step[1]
                        w = width(j)
                        act.wait_ge(st["filled"], u.filled(step))
                        act.wait_ge(st["hid_ready"], slot_free(b, j, 2))
                        if l == 0:
                            ins = act.activation(hid_full[0:w, hid_full_slot(j), :],
                                                 ring[u.bank(step)][0:w, :], ACT.Gelu, bias=hid_bias[0:w, j:j + 1])
                        else:
                            ins = act.activation(hid_full[0:w, hid_full_slot(j), :], ring[u.bank(step)][0:w, :], ACT.Silu)
                        ins.then_inc(st[f"free{u.bank(step)}"], 1)
                    elif kind == "t":
                        modulate(u, step, b + 1)
                    elif kind == "split":
                        act.wait_ge(st["filled"], u.filled((ups[-1], chunks - 1)))
                        high_h(u)

            over_sequences(act, body, first)

        @block.vector
        def _(dve):
            dve.sem_inc(st["x_done"], 2)

            def low_h(nb):
                for c in range(DC):
                    dve.wait_ge(st["h_high_done"], nb * DC + (c + 1))
                    dve.tensor_tensor(h_low[:, c, :], h_full[:, c, :], h_high[:, c, :].bitcast(F32), ALU.subtract
                                      ).then_inc(st["h_ready"], 1)

            def split_hidden(b, j):
                w = width(j)
                full = hid_full[0:w, hid_full_slot(j), :]
                high, low = hid_high[0:w, hid_slot(j), :], hid_low[0:w, hid_slot(j), :]
                dve.wait_ge(st["down_done"], slot_free(b, j, 3))
                dve.tensor_copy(high, full)
                dve.drain()
                dve.tensor_tensor(low, full, high.bitcast(F32), ALU.subtract).then_inc(st["hid_ready"], 1)

            def first():
                dve.wait_ge(st["x_loaded"], 16)
                for t in range(TT):
                    norm_stats(dve, l, x, stats, mv, t)
                norm_power_input(dve, l, mv, power_in, EPS[l]).then_inc(st["power_ready"], 1)
                dve.wait_ge(st["rstd_ready"], 1)
                for t in range(TT):
                    norm_apply(dve, l, x, mv, rstd, t).then_inc(st["x_normed"], 1)
                low_h(0)
                for i in range(len(pieces)):
                    weights.low(dve, i)

            def body(b, last):
                u = banks_for(b, last)
                for step in mlp_steps(l, last):
                    kind = step[0]
                    if kind == "a" and l == 0:
                        dve.wait_ge(st[f"free{u.bank(step)}"], u.released(step))
                        split_hidden(b, step[1])
                    elif kind == "g":
                        j = step[1]
                        w = width(j)
                        full = hid_full[0:w, hid_full_slot(j), :]
                        dve.wait_ge(st[f"free{u.bank(('a', j))}"], u.released(("a", j)))
                        dve.wait_ge(st["filled"], u.filled(step))
                        dve.tensor_tensor(full, ring[u.bank(step)][0:w, :], full, ALU.mult
                                          ).then_inc(st[f"free{u.bank(step)}"], 1)
                        dve.drain()
                        split_hidden(b, j)
                    elif kind == "stats":
                        if step[1] == 0:
                            dve.wait_ge(st["x_loaded"], b * 16 + 32)
                        norm_stats(dve, l, x, stats, mv, step[1])
                    elif kind == "power":
                        norm_power_input(dve, l, mv, power_in, EPS[l]).then_inc(st["power_ready"], 1)
                    elif kind == "apply":
                        if step[1] == 0:
                            dve.wait_ge(st["rstd_ready"], b + 2)
                        norm_apply(dve, l, x, mv, rstd, step[1]).then_inc(st["x_normed"], 1)
                    elif kind == "split":
                        low_h(b + 1)
                    elif kind == "p":
                        t = step[1]
                        if t == 0:
                            dve.wait_ge(st["gate_loaded"], b * loads + loads)
                        if t < TT - 1:
                            dve.wait_ge(st["acc_done"], b * (TT - 1) + (t + 1))
                        else:
                            dve.wait_ge(st["down_done"], b * chunks + (chunks + 3))
                        dve.wait_ge(st["x_done"], b * TT + (t + 1))
                        dve.tensor_tensor(tmp2[:, t % 2, :], acc[t][:], gate[:], ALU.mult
                                          ).then_inc(st["gated"], 1)

            over_sequences(dve, body, first)

        @block.gpsimd
        def _(pool):
            def power(n):
                wait_and_note(pool, st["power_ready"], n + 1, st["noted"])
                pool.tensor_tensor(rstd[:], power_in[:], minus_half[:], ALU.pow).then_inc(st["rstd_ready"], 1)

            def body(b, last):
                for step in mlp_steps(l, last):
                    kind = step[0]
                    if kind == "power":
                        power(b + 1)
                    elif kind == "c" and step[1] == chunks - 2 and l == 0:
                        wait_and_note(pool, st["gate_loaded"], b * loads + loads, st["noted"])
                        pool.tensor_tensor(gate_bias[:], gate_bias[:], gate[:], ALU.mult)
                        pool.drain()
                        wait_and_note(pool, st["res_loaded"], b * 16 + 16, st["noted"])
                        for t in range(TT):
                            pool.tensor_tensor(x[:, t, :], x[:, t, :], gate_bias[:], ALU.add)
                        pool.drain()
                    elif kind == "p":
                        t = step[1]
                        if t == 0:
                            wait_and_note(pool, st["res_loaded"], b * 16 + 16, st["noted"])
                        wait_and_note(pool, st["gated"], b * TT + (t + 1 + TT), st["noted"])
                        pool.tensor_tensor(x[:, t, :], x[:, t, :], tmp2[:, t % 2, :], ALU.add
                                           ).then_inc(st["x_done"], 1)

            def first():
                pool.memset(minus_half[:], -0.5).then_inc(st["const_set"], 1)
                pool.wait_ge(st["const_set"], 1)
                power(0)

            over_sequences(pool, body, first)

        @block.sync
        def _(sp):
            def first():
                sp.sem_inc(st["stored"], 16)
                sp.dma_start(x[:], seq_view(x_in, 0)).then_inc(st["x_loaded"], 16)
                weights.load(sp)
                if l == 0:
                    sp.dma_start(hid_bias[:], dram["b_fc1"]).then_inc(st["bias_loaded"], 16)
                sp.wait_ge(st["filled"], DC)

            def body(b, last):
                wait_and_note(sp, st["stored"], b * 64 + 16, st["noted"])
                if not last:
                    sp.dma_start(x[:], seq_view(x_in, b + 1)).then_inc(st["x_loaded"], 16)
                else:
                    sp.dma_start(x[:], seq_view(x_in, b)).then_inc(st["res_loaded"], 16)
                sp.dma_start(gate[:], mod_rows[l, ds(b, 1), 5 * D:6 * D].to_broadcast([P, D])
                             ).then_inc(st["gate_loaded"], 16)
                if l == 0:
                    sp.dma_start(gate_bias[:], dram["b_fc2"].rearrange("(o n) -> o n", o=1).to_broadcast([P, D])
                                 ).then_inc(st["gate_loaded"], 16)
                for step in mlp_steps(l, last):
                    if step == ("t", DC - 1):
                        wait_and_note(sp, st["filled"], banks_for(b, last).filled(step), st["noted"])
                        sp.dma_start(x[:], seq_view(x_in, b)).then_inc(st["res_loaded"], 16)
                    elif step[0] == "p":
                        t = step[1]
                        wait_and_note(sp, st["x_done"], b * TT + (t + 1 + 2), st["noted"])
                        sp.dma_start(x_out[ds(b, 1), t * P:(t + 1) * P, :].rearrange("o p d -> p (o d)"), x[:, t, :]
                                     ).then_inc(st["stored"], 16)

            over_sequences(sp, body, first)
            sp.wait_ge(st["stored"], 16 + 64 * B)


def build_program(nc, dram, out):
    mod_rows = nc.dram_tensor("mod_rows", [2, B, 6 * D], F32).ap()
    mid = [nc.dram_tensor(f"x_mid{i}", [B, N, D], F32).ap() for i in range(3)]
    with ExitStack() as ctx:
        ident = ctx.enter_context(nc.sbuf_tensor("ident", [P, P], F32))
        modT = ctx.enter_context(nc.sbuf_tensor("modT", [P, 2, 4 * DC, B], F32))
        modulation_stage(nc, dram, mod_rows, modT, ident)
        attention_stage(nc, 0, dram, dram["x"], mid[0], mod_rows, modT, ident)
        mlp_stage(nc, 0, dram, mid[0], mid[1], mod_rows, modT, ident)
        attention_stage(nc, 1, dram, mid[1], mid[2], mod_rows, modT, ident)
        mlp_stage(nc, 1, dram, mid[2], out, mod_rows, modT, ident)


def kernel(**inputs):
    import concourse.bacc as bacc
    from concourse.bass_utils import run_bass_kernel_spmd

    c = {k: np.asarray(v) for k, v in inputs.items()}
    by_chunk = lambda v: v.reshape(-1, P).T
    wq = c["L1_cond_qkv_w"].T
    half = D // 2
    w_qkv0 = c["L0_cond_w_qkv"].copy()
    w_qkv0[:, 0:2 * D] = (w_qkv0[:, 0:2 * D].reshape(D, 2 * NG, GH, HD).transpose(0, 1, 3, 2).reshape(D, 2 * D))
    w_qkv1 = np.concatenate([wq[:, 0:half], wq[:, D:D + half], wq[:, half:D], wq[:, D + half:2 * D],
                             wq[:, 2 * D:]], axis=1)
    arrays = {
        "x": c["x"],
        "cT": c["cond_1024"].T.reshape(DC, P, B).transpose(1, 0, 2),
        "w_ada0": c["L0_cond_w_ada"], "b_ada0": c["L0_cond_b_ada"],
        "w_ada1": c["L1_cond_ada_w"].T, "b_ada1": c["L1_cond_ada_b"],
        "norm1": by_chunk(c["L1_cond_norm1_w"]), "norm2": by_chunk(c["L1_cond_norm2_w"]),
        "w_qkv0": w_qkv0, "w_qkv1": w_qkv1,
        "w_proj0": c["L0_cond_w_proj"], "w_proj1": c["L1_cond_proj_w"].T,
        "b_proj0": c["L0_cond_b_proj"], "b_proj1": c["L1_cond_proj_b"],
        "up_a0": c["L0_cond_w_fc1"], "b_fc1": by_chunk(c["L0_cond_b_fc1"]),
        "down0": c["L0_cond_w_fc2"], "b_fc2": c["L0_cond_b_fc2"],
        "up_a1": c["L1_cond_w1"].T, "up_g1": c["L1_cond_w3"].T, "down1": c["L1_cond_w2"].T,
        "qk_norm": np.stack([c["L1_cond_q_norm_w"], c["L1_cond_k_norm_w"]]),
        "pos": c["fside_BxSx3_0"].reshape(B * TT, P, 3).transpose(1, 0, 2),
        "freqs": np.tile((1.0 / np.float32(10000.0) ** (np.arange(5, dtype=np.float32) / np.float32(5)))
                         .astype(np.float32), (P, 1)),
    }
    arrays = {k: np.ascontiguousarray(v) for k, v in arrays.items()}
    nc = bacc.Bacc("TRN2", target_bir_lowering=False, num_devices=1)
    dram = {k: nc.dram_tensor(f"in_{k}", v.shape, mybir.dt.from_np(v.dtype), kind="ExternalInput").ap()
            for k, v in arrays.items()}
    out = nc.dram_tensor("out_0", (B, N, D), F32, kind="ExternalOutput").ap()
    build_program(nc, dram, out)
    r = run_bass_kernel_spmd(nc, [{f"in_{k}": v for k, v in arrays.items()}], core_ids=[0])
    return r.results[0]["out_0"]
```

```python
from contextlib import ExitStack

import numpy as np

import concourse.bass as bass
from concourse import mybir

F32 = mybir.dt.float32
F32R = mybir.dt.float32r
ALU = mybir.AluOpType
ACT = mybir.ActivationFunctionType
AX = mybir.AxisListType
ds = bass.ds

P = 128
B, N, D = 8, 512, 512
HEADS = 16
HD = D // HEADS
TT = N // P
DC = D // P
GH = P // HD
NG = HEADS // GH
HID = (2048, 1365)
EPS = (1e-5, 1e-6)
PAIRS = HD // 2
KROWS = 3 * HD
AROWS = KROWS + 2
SCALE = float(HD) ** -0.5
TWO_PI = 6.283185307179586
PI_A, PI_B = 6.28125, 0.0019350051879882812
PI_C = TWO_PI - PI_A - PI_B
ROUND = 12582912.0


class Banks:

    def __init__(self, before, per, now, b):
        count = lambda uses, bank: sum(1 for _, k in uses if k == bank)
        self.opening = b is None
        self.place = {}
        self.earlier = {}
        for bank in {k for _, k in before + per}:
            self.earlier[bank] = 0 if b is None else b * count(per, bank) + count(before, bank)
        for i, (key, bank) in enumerate(before if b is None else now):
            if b is None:
                self.place[key] = (bank, i, count(before[:i], bank))
            else:
                self.place[key] = (bank, b * len(per) + (len(before) + i),
                                   b * count(per, bank) + (count(before, bank) + count(now[:i], bank)))

    def bank(self, key):
        return self.place[key][0]

    def filled(self, key):
        return self.place[key][1] + 1

    def freed_before(self, key):
        return self.place[key][2] + 1

    def all_before(self, bank):
        return self.earlier[bank] + 1

    def released(self, key):
        return self.place[key][2] + 2


class Stage:

    def __init__(self, nc, ctx, name, banks, sems):
        self.nc = nc
        self.name = name
        self.bank = [ctx.enter_context(nc.psum_tensor(f"{name}_bank{i}", [P, 512], F32)) for i in range(banks)]
        self.sem = {s: ctx.enter_context(nc.semaphore(f"{name}_{s}")) for s in sems}

    def __getitem__(self, s):
        return self.sem[s]


def over_sequences(eng, body, before=None, peel_first=False):
    if before is not None:
        before()
    if peel_first:
        body(0, False)
    with eng.Fori(int(peel_first), B - 1) as b:
        body(b, False)
    body(B - 1, True)


def seq_view(x, b):
    return x[ds(b, 1), :, :].rearrange("o (t p) d -> p (o t) d", p=P)


def tile_view(x, b, t):
    return x[ds(b, 1), t * P:(t + 1) * P, :].rearrange("o p d -> p (o d)")


def wait_and_note(eng, sem, value, noted):
    eng.wait_ge(sem, value)
    eng.sem_inc(noted, 1)


def modulation_stage(nc, dram, mod_rows, modT, ident):
    with ExitStack() as ctx:
        sb = lambda n, s, d=F32: ctx.enter_context(nc.sbuf_tensor(n, s, d))
        cT = sb("mod_cT", [P, DC, B])
        act_c = sb("mod_act_c", [P, DC, B])
        wada = [sb(f"mod_wada{l}", [P, DC, 6 * D]) for l in range(2)]
        bias = sb("mod_bias", [B, 2, 6 * D])
        rows = sb("mod_rows_sb", [B, 2, 6 * D])
        normw = sb("mod_normw", [P, 2, DC])
        st = Stage(nc, ctx, "mod", 5, ["c_in", "b_in", "silu", "filled", "rows_ready",
                                       "turned", "id0", "id1", "stored"]
                   + [f"w{l}{c}_in" for l in range(2) for c in range(DC)])
        block = ctx.enter_context(nc.Block())

        @block.sync
        def _(sp):
            sp.dma_start(cT[:], dram["cT"]).then_inc(st["c_in"], 16)
            for l in range(2):
                for c in range(DC):
                    sp.dma_start(wada[l][:, c, :], dram[f"w_ada{l}"][c * P:(c + 1) * P, :]
                                 ).then_inc(st[f"w{l}{c}_in"], 16)
                if l == 0:
                    sp.dma_start(normw[:, 0, :], dram["norm1"]).then_inc(st["b_in"], 16)
                    sp.dma_start(normw[:, 1, :], dram["norm2"]).then_inc(st["b_in"], 16)
                    for k in range(2):
                        sp.dma_start(bias[:, k, :], dram[f"b_ada{k}"].rearrange("(o n) -> o n", o=1)
                                     .to_broadcast([B, 6 * D])).then_inc(st["b_in"], 16)
            for l in range(2):
                sp.wait_ge(st["rows_ready"], 6 * (l + 1))
                sp.dma_start(mod_rows[l, :, :], rows[:, l, :]).then_inc(st["stored"], 16)
            sp.wait_ge(st["stored"], 32)

        @block.gpsimd
        def _(pool):
            pool.memset(ident[:], 0.0).then_inc(st["id0"], 1)
            pool.wait_ge(st["id0"], 1)
            pool.affine_select(out=ident[:], in_=ident[:], compare_op=ALU.not_equal, fill=1.0, base=0,
                               pattern=[[-1, P]], channel_multiplier=1).then_inc(st["id1"], 1)

        @block.scalar
        def _(act):
            act.wait_ge(st["c_in"], 16)
            act.activation(act_c[:], cT[:], ACT.Silu).then_inc(st["silu"], 1)

        @block.tensor
        def _(pe):
            for l in range(2):
                cond = act_c if l == 0 else cT
                if l == 0:
                    pe.wait_ge(st["silu"], 1)
                for c in range(DC):
                    pe.wait_ge(st[f"w{l}{c}_in"], 16)
                    for j in range(6):
                        mm = pe.matmul(st.bank[2 * l + j // 4][32 * (j % 4):32 * (j % 4) + B, :], cond[:, c, :],
                                       wada[l][:, c, j * D:(j + 1) * D], start=(c == 0), stop=(c == DC - 1))
                mm.then_inc(st["filled"], 1)
            pe.wait_ge(st["id1"], 1)
            for l in range(2):
                pe.wait_ge(st["rows_ready"], 6 * (l + 1))
                for k in range(4 * DC):
                    off = (0, 1, 3, 4)[k // DC] * D + (k % DC) * P
                    mm = pe.transpose(st.bank[4][:, (l * 16 + k) * B:(l * 16 + k + 1) * B],
                                      rows[:, l, off:off + P], ident[0:B, 0:B])
                mm.then_inc(st["turned"], 1)

        @block.vector
        def _(dve):
            dve.wait_ge(st["b_in"], 64)
            for l in range(2):
                dve.wait_ge(st["filled"], l + 1)
                for j in range(6):
                    dve.tensor_tensor(rows[:, l, j * D:(j + 1) * D],
                                      st.bank[2 * l + j // 4][32 * (j % 4):32 * (j % 4) + B, :],
                                      bias[:, l, j * D:(j + 1) * D], ALU.add).then_inc(st["rows_ready"], 1)
            dve.wait_ge(st["turned"], 2)
            dve.tensor_copy(modT[:].rearrange("p l k b -> p (l k b)"), st.bank[4][:, 0:2 * 16 * B])
            dve.drain()
            for l in range(2):
                for half in range(2):
                    scale = modT[:, l, 4 + 8 * half:8 + 8 * half, :]
                    dve.tensor_scalar(scale, scale, 1.0, None, ALU.add)
                    if l == 1:
                        dve.drain()
                        dve.tensor_tensor(scale, scale, normw[:, half, :].unsqueeze(2).to_broadcast([P, DC, B]),
                                          ALU.mult)


class WeightLoader:

    def __init__(self, nc, ctx, name, slots, pieces):
        self.slots, self.pieces = slots, pieces
        self.sem = {s: ctx.enter_context(nc.semaphore(f"{name}_w_{s}")) for s in
                    ["high_done", "low_done"] + [f"in{i}" for i in range(len(slots))]}

    def staged(self, i):
        src = self.pieces[i][0]
        r, c, n = src.shape
        return self.slots[i % len(self.slots)][0:r, 0:c * n].rearrange("p (c n) -> p c n", c=c)

    def load(self, sp, first=0, end=None):
        for i in range(first, len(self.pieces) if end is None else end):
            src, k = self.pieces[i][0], len(self.slots)
            if i >= k:
                sp.wait_ge(self.sem["low_done"], i - k + 1)
            sp.dma_start(self.staged(i), src).then_inc(self.sem[f"in{i % k}"], 16)

    def high(self, act, i):
        k = len(self.slots)
        act.wait_ge(self.sem[f"in{i % k}"], 16 * (i // k + 1))
        act.activation(self.pieces[i][1], self.staged(i), ACT.Copy).then_inc(self.sem["high_done"], 1)

    def low(self, dve, i):
        dve.wait_ge(self.sem["high_done"], i + 1)
        dve.tensor_tensor(self.pieces[i][2], self.staged(i), self.pieces[i][1].bitcast(F32), ALU.subtract
                          ).then_inc(self.sem["low_done"], 1)

    def ready(self, eng, i):
        eng.wait_ge(self.sem["low_done"], i + 1)


def norm_stats(dve, l, x, stats, mv, t):
    dve.bn_stats(stats[:, t, :], x[:, t, :])
    dve.drain()
    dve.bn_aggr(mv[:, t, :], stats[:, t, :])


def norm_power_input(dve, l, mv, power_in, eps):
    dve.drain()
    if l == 0:
        return dve.tensor_scalar(power_in[:, :], mv[:, :, 1], eps, None, ALU.add)
    dve.tensor_tensor(power_in[:, :], mv[:, :, 0], mv[:, :, 0], ALU.mult)
    dve.drain()
    return dve.scalar_tensor_tensor(out=power_in[:, :], in0=power_in[:, :], scalar=eps, in1=mv[:, :, 1],
                                    op0=ALU.add, op1=ALU.add)


def norm_apply(dve, l, x, mv, rstd, t):
    if l == 0:
        return dve.tensor_scalar(x[:, t, :], x[:, t, :], mv[:, t, 0:1], rstd[:, t:t + 1], ALU.subtract, ALU.mult)
    return dve.tensor_scalar(x[:, t, :], x[:, t, :], rstd[:, t:t + 1], None, ALU.mult)


def attention_opening(l):
    s = [("t", c) for c in range(DC)]
    if l == 0:
        s += [("split", 1), ("q", NG), ("k", NG), ("split", 2), ("v", 0), ("v", 1), ("max", NG, 0), ("v", 2),
              ("max", NG, 1), ("v", 3), ("max", NG, 2), ("max", NG, 3)]
    else:
        query = lambda i: [("Q", i), ("square", i), ("rope", i)]
        s += query(0) + [("angles",), ("split", 1), ("tables",)]
        for i in range(1, 7):
            s += query(i) + [("split", 2)] * (i == 2)
        s += [("v", 0), ("v", 1), ("q", NG), ("k", NG), ("v", 2)] + query(7)
        s += [("v", 3), ("max", NG, 0), ("rope", 8), ("max", NG, 1), ("rope", 9), ("max", NG, 2), ("rope", 10),
              ("max", NG, 3)]
    return s + [("q", NG + 1), ("m", NG), ("k", NG + 1), ("split", 3)]


def attention_steps(l, last):
    s = []
    for g in range(NG):
        more = g + 1 < NG or not last
        after = g + 2 < NG or not last
        maxima = lambda a, e: (a, e) if more else (0, 0)

        def ahead(*steps):
            if not last:
                s.extend(steps)

        def query(i):
            ahead(("Q", i), ("rope", i))

        s.append(("s", g, 0, 0, (0, 0)))
        if g == 2 - l:
            ahead(("t", 2))
            s.append(("norm", g - 1, 0))
        s.append(("s", g, 0, 1, (0, 0)))
        if g == 2 - l:
            ahead(("t", 3))
            s.append(("norm", g - 1, 1))
        elif g > 0:
            s += [("norm", g - 1, 0), ("norm", g - 1, 1)]
        if g == 0:
            s += [("q", 2), ("gate_bias",)]
        if g == 1 and l == 1:
            ahead(("tables",))
        if l == 1 and g == 2:
            query(3)
        if g == 1:
            s.append(("q", g + 2))
        if l == 0 and g == 3:
            ahead(("q", g + 2))
        s.append(("s", g, 1, 0, maxima(0, 2)))
        if l == 0 and g == 2:
            ahead(("q", g + 2))
        if l == 1 and g == 2:
            query(4)
        s.append(("s", g, 1, 1, maxima(2, 5)))
        if g > 0:
            s.append(("split_o", g - 1))
        s.append(("s", g, 2, 0, maxima(5, 8)))
        if l == 1 and g == 0:
            ahead(("stats", 0), ("stats", 1))
        if l == 1 and g in (1, 2):
            query(5 * g - 5)
        s.append(("s", g, 2, 1, maxima(8, 11)))
        if l == 1 and g == 0:
            ahead(("stats", 2), ("stats", 3), ("power",))
        if g == NG - 1:
            s.append(("residual",))
        if l == 0 and g == 1:
            ahead(("apply", 0), ("apply", 1))
        s.append(("s", g, 3, 0, maxima(11, 14)))
        if l == 1 and g in (1, 2):
            query(5 * g - 4)
        if l == 0 and g == 1:
            ahead(("apply", 2), ("apply", 3))
        if l == 1 and g == 0:
            ahead(("apply", 0), ("apply", 1))
        s.append(("s", g, 3, 1, maxima(14, 16)))
        if l == 1 and g == 0:
            ahead(("apply", 2), ("apply", 3))
        if more:
            s.append(("m", g + 1))
        if l == 0 and g == 0:
            ahead(("stats", 0))
        if after and not (l == 0 or g < 2):
            s.append(("q", g + 2))
        if after:
            s.append(("k", g + 2))
        if l == 0 and g == 0:
            ahead(("stats", 1), ("stats", 2), ("stats", 3), ("power",))
        if g == 1 - l:
            ahead(("t", 0))
        if l == 1 and g in (1, 2):
            query(5 * g - 3)
        if l == 1 and g == 3:
            ahead(("rope", 8))
        s.append(("values", g))
        if g == 1 - l:
            ahead(("t", 1))
    s += [("sums", NG - 1), ("norm", NG - 1, 0), ("norm", NG - 1, 1)]
    if l == 1 and not last:
        s += [("rope", 9), ("rope", 10)]
    if not last:
        s += [("v", t) for t in range(TT)]
    for i in range(8):
        if ("Q", i) in s:
            at = next(n for n in range(s.index(("Q", i)), len(s)) if s[n][0] == "s")
            s.insert(at + 1, ("square", i))
    return s + [("p", t) for t in range(TT)]


RING = 4


def uses_of(steps):
    uses = []
    for step in steps:
        if step[0] in ("q", "k", "v", "m", "t", "p", "Q"):
            uses.append(step)
        elif step[0] == "max":
            uses += [("max of", step[1], n) for n in range(TT * step[2], TT * step[2] + TT)]
        elif step[0] == "s":
            uses += [("max of", step[1] + 1, n) for n in range(*step[4])]
    return [(use, i % RING) for i, use in enumerate(uses)]


def attention_stage(nc, l, dram, x_in, x_out, mod_rows, modT, ident):
    nm = f"att{l}"
    with ExitStack() as ctx:
        sb = lambda n, s, d=F32: ctx.enter_context(nc.sbuf_tensor(f"{nm}_{n}", s, d))
        w_high, w_low = sb("w_high", [P, DC, 3 * D], F32R), sb("w_low", [P, DC, 3 * D], F32R)
        p_high, p_low = sb("p_high", [P, DC, D], F32R), sb("p_low", [P, DC, D], F32R)
        ones = sb("ones", [P, HD])
        minus_half = sb("minus_half", [P, HEADS])
        keys, queries = sb("keys", [AROWS, 2, GH, N], F32R), sb("queries", [AROWS, 2, GH, N], F32R)
        x = sb("x", [P, TT, D])
        h_full = sb("h_full", [P, N])
        h_high, h_low = sb("h_high", [P, DC, N], F32R), sb("h_low", [P, DC, N], F32R)
        qk_high, qk_low = sb("qk_high", [P, 2, N], F32R), sb("qk_low", [P, 2, N], F32R)
        values = sb("values", [P, TT, D])
        probs = sb("probs", [P, 2, GH, N])
        o_high, o_low = sb("o_high", [P, DC, N], F32R), sb("o_low", [P, DC, N], F32R)
        tmp2 = sb("tmp2", [P, 2, D])
        gate, gate_bias = sb("gate", [P, D]), sb("gate_bias", [P, D])
        row_max = sb("row_max", [P, 2, GH * TT])
        max_high, max_low = sb("max_high", [GH * TT, P], F32R), sb("max_low", [GH * TT, P], F32R)
        stats, mv = sb("stats", [P, TT, 6]), sb("mv", [P, TT, 2])
        power_in, rstd, x_shift = sb("power_in", [P, TT]), sb("rstd", [P, TT]), sb("x_shift", [P, TT])
        if l == 1:
            cos_t, sin_t = sb("cos_t", [P, B * TT, PAIRS]), sb("sin_t", [P, B * TT, PAIRS])
            w_turn = sb("w_turn", [P, 2, PAIRS, 2])
            w_swap = sb("w_swap", [P, 2, PAIRS, 2])
            qk_nat = sb("qk_nat", [P, 2, TT, N])
            turn, swap = sb("turn", [P, TT, 2, PAIRS, 2]), sb("swap", [P, TT, 2, PAIRS, 2])
            square_sum = sb("square_sum", [P, TT])
            squares = h_full
            turned, swapped = sb("turned", [P, N]), sb("swapped", [P, N])
            ssum, sinv = sb("ssum", [P, 2, HEADS]), sb("sinv", [P, 2, HEADS])
            room = values[:].rearrange("p t n -> p (t n)")
            n_ang = B * TT * 15
            angle, turns, part = (room[:, i * n_ang:(i + 1) * n_ang] for i in range(3))
            pos = room[:, 3 * n_ang:3 * n_ang + B * TT * 3].rearrange("p (t a) -> p t a", a=3)
            freqs = room[:, 3 * n_ang + 96:3 * n_ang + 101]
            wrow = room[:, 3 * n_ang + 104:3 * n_ang + 104 + 2 * HD].rearrange("p (s a e) -> p s a e", s=2, e=2)

        st = Stage(nc, ctx, nm, 8, [
            "filled", "free0", "free1", "free2", "free3", "score_filled", "exp_done", "pv_done", "o_read",
            "o_ready", "high_done", "max_high_done", "stacked0", "stacked1", "rows0", "rows1", "x_loaded",
            "power_ready", "rstd_ready", "x_normed", "h_ready", "res_loaded", "gate_loaded",
            "x_done", "stored0", "stored1", "stored2", "stored3", "noted", "consts", "o_inverse", "o_scaled", "o_high_done"]
            + ["q_squared", "sum_ready", "inv_ready", "scaled", "swap_done", "roped", "tables_ready", "squared",
               "tab_in", "tab_reduced", "tab_sin", "tab_ready"] * l)
        ring, scb = st.bank[0:RING], st.bank[4:6]
        o_acc, s_acc = st.bank[6], st.bank[7]
        before = uses_of(attention_opening(l))
        per = uses_of(attention_steps(l, False))

        def banks_for(b, last):
            return Banks(before, per, uses_of(attention_steps(l, last)), b)

        wv = dram[f"w_qkv{l}"].rearrange("(c p) n -> p c n", p=P)
        blocks = [(wv[:, :, i * D:(i + 1) * D], w_high[:, :, i * D:(i + 1) * D], w_low[:, :, i * D:(i + 1) * D])
                  for i in range(3)]
        blocks.append((dram[f"w_proj{l}"].rearrange("(c p) n -> p c n", p=P), p_high[:], p_low[:]))
        weights = WeightLoader(nc, ctx, nm, [probs[:, i, :, :].rearrange("p h n -> p (h n)") for i in range(2)], blocks)
        block = ctx.enter_context(nc.Block())

        @block.tensor
        def _(pe):
            def claim(u, key):
                pe.wait_ge(st[f"free{u.bank(key)}"], u.freed_before(key))
                return ring[u.bank(key)]

            def split_product(out, terms):
                for i, (sh, sl, mh, ml) in enumerate(terms):
                    pe.matmul(out, sh, mh, start=(i == 0), stop=False)
                    pe.matmul(out, sh, ml, start=False, stop=False)
                    mm = pe.matmul(out, sl, mh, start=False, stop=(i == len(terms) - 1))
                return mm

            def run(b, steps, u):
                opening = u.opening

                def max_products(g, first, end):
                    for n in range(first, end):
                        i, qt = divmod(n, TT)
                        bank = claim(u, ("max of", g, n))
                        pe.matmul(bank[:], queries[0:KROWS, g % 2, i, qt * P:(qt + 1) * P],
                                  keys[0:KROWS, g % 2, i, :], start=True, stop=True).then_inc(st["filled"], 1)

                def score_product(g, kt, h):
                    pe.wait_ge(st["exp_done"], b * 64 + (16 * g + 4 * kt + h + 1))
                    pe.matmul(scb[h % 2][:], keys[0:AROWS, g % 2, h, kt * P:(kt + 1) * P],
                              queries[0:AROWS, g % 2, h, :], start=True, stop=True).then_inc(st["score_filled"], 1)

                def values_product(g, kt):
                    pe.wait_ge(st["exp_done"], b * 64 + (16 * g + 4 * kt + 4 + 2))
                    if kt == 0:
                        pe.wait_ge(st["o_read"], b * NG + (g + 1))
                        if g == 0:
                            for i in range(RING):
                                pe.wait_ge(st[f"free{i}"], u.all_before(i))
                    for h in range(GH):
                        pe.matmul(o_acc[HD * h:HD * (h + 1), :], values[:, kt, (GH * g + h) * HD:(GH * g + h + 1) * HD],
                                  probs[:, kt % 2, h, :], start=(kt == 0), stop=(kt == TT - 1))

                def sums_product(g, kt):
                    if kt == 0:
                        pe.wait_ge(st["o_inverse"], b * 8 + (2 * g + 2))
                    for h in range(GH):
                        mm = pe.matmul(s_acc[HD * h:HD * (h + 1), :], ones[:], probs[:, kt % 2, h, :],
                                       start=(kt == 0), stop=(kt == TT - 1))
                    mm.then_inc(st["pv_done"], 1)

                def stacked(g):
                    pe.wait_ge(st[f"stacked{g % 2}"], b * 192 + (96 * (g // 2) + 96))

                for step in steps:
                    kind = step[0]
                    if kind == "t":
                        c = step[1]
                        if c == 0:
                            pe.wait_ge(st["x_normed"], b * TT + 2 * TT)
                        g = claim(u, step)
                        for t in range(TT):
                            mm = pe.transpose(g[:, t * P:(t + 1) * P], x[:, t, c * P:(c + 1) * P], ident[:])
                        mm.then_inc(st["filled"], 1)
                    elif kind == "Q":
                        half, t = divmod(step[1], TT)
                        g = claim(u, step)
                        if step[1] == 0:
                            pe.wait_ge(st["h_ready"], b * DC + (2 * DC + 1))
                        if opening and t == 0:
                            weights.ready(pe, half)
                        split_product(g[:], [(h_high[:, c, t * P:(t + 1) * P], h_low[:, c, t * P:(t + 1) * P],
                                              w_high[:, c, half * D:(half + 1) * D],
                                              w_low[:, c, half * D:(half + 1) * D])
                                             for c in range(DC)]).then_inc(st["filled"], 1)
                    elif kind in ("q", "k") and l == 0:
                        i = ("q", "k").index(kind)
                        a = i * D + (step[1] % NG) * P
                        if step == ("q", NG):
                            pe.wait_ge(st["h_ready"], b * DC + (2 * DC + 1))
                        if opening:
                            weights.ready(pe, i)
                        g = claim(u, step)
                        split_product(g[:], [(w_high[:, c, a:a + P], w_low[:, c, a:a + P],
                                              h_high[:, c, :], h_low[:, c, :])
                                             for c in range(DC)]).then_inc(st["filled"], 1)
                    elif kind in ("q", "k"):
                        gi = step[1] % NG
                        half, a = gi // 2, ("q", "k").index(kind) * 256 + (gi % 2) * P
                        if kind == "q" and gi % 2 == 0:
                            pe.wait_ge(st["roped"], b * 8 + (5 + 8 if gi == 0 else 9))
                        g = claim(u, step)
                        for t in range(TT):
                            mm = pe.transpose(g[:, t * P:(t + 1) * P], qk_nat[:, half, t, a:a + P], ident[:])
                        mm.then_inc(st["filled"], 1)
                    elif kind == "v":
                        t = step[1]
                        if opening and t == 0:
                            weights.ready(pe, 2)
                        g = claim(u, step)
                        split_product(g[:], [(h_high[:, c, t * P:(t + 1) * P], h_low[:, c, t * P:(t + 1) * P],
                                              w_high[:, c, 2 * D:3 * D], w_low[:, c, 2 * D:3 * D])
                                             for c in range(DC)]).then_inc(st["filled"], 1)
                    elif kind == "max":
                        if opening and step[2] == 0:
                            stacked(step[1])
                        max_products(step[1], TT * step[2], TT * step[2] + TT)
                    elif kind == "m":
                        gi = step[1]
                        g = claim(u, step)
                        final = ("max of", gi, GH * TT - 1)
                        pe.wait_ge(st[f"free{u.bank(final)}"], u.released(final))
                        pe.transpose(g[0:GH * TT, 0:P], row_max[:, gi % 2, :], ident[:]).then_inc(st["filled"], 1)
                    elif kind == "s":
                        gi, kt, half, (a, e) = step[1:]
                        if kt == 0 and half == 0:
                            pe.wait_ge(st[f"rows{gi % 2}"], b * 64 + (32 * (gi // 2) + 32))
                        if a == 0 and e > 0:
                            stacked(gi + 1)
                        score_product(gi, kt, 2 * half)
                        score_product(gi, kt, 2 * half + 1)
                        max_products(gi + 1, a, min(a + 2, e))
                        if kt and half == 0:
                            values_product(gi, kt - 1)
                        elif kt:
                            sums_product(gi, kt - 1)
                        elif gi and half == 0:
                            sums_product(gi - 1, TT - 1)
                        max_products(gi + 1, min(a + 2, e), e)
                    elif kind == "values":
                        values_product(step[1], TT - 1)
                    elif kind == "sums":
                        sums_product(step[1], TT - 1)
                    elif kind == "p":
                        t = step[1]
                        if t == 0:
                            pe.wait_ge(st["o_ready"], b * 8 + 8)
                        g = claim(u, step)
                        split_product(g[:], [(o_high[:, c, t * P:(t + 1) * P], o_low[:, c, t * P:(t + 1) * P],
                                              p_high[:, c, :], p_low[:, c, :])
                                             for c in range(DC)]).then_inc(st["filled"], 1)

            for i in range(RING):
                pe.sem_inc(st[f"free{i}"], 1)
            pe.sem_inc(st["exp_done"], 2)
            pe.sem_inc(st["pv_done"], 2)
            pe.sem_inc(st["o_read"], 1)
            pe.sem_inc(st["o_inverse"], 2)
            pe.wait_ge(st["consts"], 1)
            run(-1, attention_opening(l), Banks(before, per, None, None))
            weights.ready(pe, 3)
            over_sequences(pe, lambda b, last: run(b, attention_steps(l, last), banks_for(b, last)))

        @block.scalar
        def _(act):
            def run(b, steps, u):
                opening = u.opening

                def take_output(gi):
                    if gi == 0:
                        act.wait_ge(st["x_done"], b * TT + 2)
                    else:
                        act.wait_ge(st["o_ready"], b * 8 + 2 * gi)
                    act.wait_ge(st["pv_done"], b * 16 + (4 * gi + 4 + 2))
                    act.activation(tmp2[:, 1, :], o_acc[:], ACT.Copy).then_inc(st["o_read"], 1)

                for step in steps:
                    kind = step[0]
                    if l == 1 and step == ("t", 0):
                        act.drain()
                    if kind in ("t", "Q", "q", "k", "v", "m"):
                        g = ring[u.bank(step)]
                        freed = st[f"free{u.bank(step)}"]
                        act.wait_ge(st["filled"], u.filled(step))
                    if kind == "t":
                        c = step[1]
                        act.wait_ge(st["h_ready"], b * DC + (DC + c + 1))
                        for out in (h_full[:], h_high[:, c, :]):
                            ins = act.activation(out, g[:], ACT.Identity, bias=modT[:, l, c, ds(b + 1, 1)],
                                                 scale=modT[:, l, 4 + c, ds(b + 1, 1)])
                        ins.then_inc(freed, 1)
                    elif kind == "stats" and l == 1:
                        t = step[1]
                        if t == 0:
                            act.wait_ge(st["x_loaded"], b * 64 + 128)
                            act.wait_ge(st["sum_ready"], b * 8 + 9)
                        else:
                            act.drain()
                        act.activation(squares[:], x[:, t, :], ACT.Square, accum_out=square_sum[:, t:t + 1]
                                       ).then_inc(st["squared"], 1)
                    elif kind == "apply":
                        t = step[1]
                        if t == 0:
                            act.wait_ge(st["rstd_ready"], b + 2)
                        if l == 0:
                            ins = act.activation(x[:, t, :], x[:, t, :], ACT.Identity, bias=x_shift[:, t:t + 1],
                                                 scale=rstd[:, t:t + 1])
                        else:
                            ins = act.activation(x[:, t, :], x[:, t, :], ACT.Copy, scale=rstd[:, t:t + 1])
                        ins.then_inc(st["x_normed"], 1)
                    elif kind == "Q":
                        half, t = divmod(step[1], TT)
                        act.activation(qk_nat[:, half, t, :], g[:], ACT.Copy).then_inc(freed, 1)
                    elif kind == "square":
                        half, t = divmod(step[1], TT)
                        key = ("Q", step[1])
                        act.wait_ge(st["sum_ready"], b * 8 + (8 + step[1] + 1))
                        act.wait_ge(st[f"free{u.bank(key)}"], u.released(key))
                        act.activation(squares[:], qk_nat[:, half, t, :], ACT.Square).then_inc(st["q_squared"], 1)
                    elif kind in ("q", "k"):
                        i = ("q", "k").index(kind)
                        if not opening or step[1] > NG:
                            act.wait_ge(st[f"stacked{(step[1] - 1) % 2}"], b * 192 + (96 * ((step[1] - 1) // 2) + 96))
                        act.activation(qk_high[:, i, :], g[:], ACT.Copy).then_inc(st["high_done"], 1)
                    elif kind == "v":
                        act.activation(values[:, step[1], :], g[:], ACT.Copy).then_inc(freed, 1)
                    elif kind == "m":
                        act.activation(max_high[:], g[0:GH * TT, 0:P], ACT.Copy, scale=-1.0
                                       ).then_inc(st["max_high_done"], 1)
                    elif kind == "s":
                        gi, kt, half = step[1:4]
                        if half == 0:
                            act.wait_ge(st["pv_done"], b * 16 + (4 * gi + kt + 1))
                        for h in (2 * half, 2 * half + 1):
                            act.wait_ge(st["score_filled"], b * 64 + (16 * gi + 4 * kt + h + 1))
                            act.activation(probs[:, kt % 2, h, :], scb[h % 2][:], ACT.Exp, scale=SCALE
                                           ).then_inc(st["exp_done"], 1)
                        if kt == 0 and half == 1 and gi:
                            take_output(gi - 1)
                    elif kind == "split":
                        weights.high(act, step[1])
                    elif kind == "angles":
                        for k, out in enumerate((sin_t, cos_t)):
                            act.wait_ge(st["tab_reduced"], k + 1)
                            act.activation(out[:, :, 0:15], part.rearrange("p (t f) -> p t f", f=15), ACT.Sin
                                           ).then_inc(st["tab_sin"], 1)
                    elif kind == "split_o":
                        gi = step[1]
                        act.wait_ge(st["o_scaled"], b * (NG - 1) + (gi + 1))
                        act.activation(o_high[:, gi, :], tmp2[:, 1, :], ACT.Copy).then_inc(st["o_high_done"], 1)
                    elif kind == "sums":
                        take_output(step[1])

            act.sem_inc(st["h_ready"], 1)
            if l == 1:
                act.sem_inc(st["sum_ready"], 1)
            u = Banks(before, per, None, None)
            run(-1, [("stats", t) for t in range(TT)] + [("split", 0)] + [("apply", t) for t in range(TT)], u)
            run(-1, attention_opening(l), u)
            weights.ready(act, len(blocks) - 1)
            over_sequences(act, lambda b, last: run(b, attention_steps(l, last), banks_for(b, last)))

        @block.vector
        def _(dve):
            def angles():
                dve.wait_ge(st["tab_in"], 64)
                dve.tensor_copy(w_turn[:], wrow)
                dve.tensor_copy(w_swap[:, :, :, 1], wrow[:, :, :, 0])
                dve.tensor_scalar(w_swap[:, :, :, 0], wrow[:, :, :, 1], -1.0, None, ALU.mult)
                dve.memset(cos_t[:, :, 15:16], 1.0)
                dve.memset(sin_t[:, :, 15:16], 0.0)
                dve.tensor_tensor(angle.rearrange("p (t a f) -> p t a f", a=3, f=5),
                                  pos.unsqueeze(3).to_broadcast([P, B * TT, 3, 5]),
                                  freqs.unsqueeze(1).unsqueeze(1).to_broadcast([P, B * TT, 3, 5]), ALU.mult)
                for k, shift in enumerate((0.0, 0.25)):
                    dve.drain()
                    if k == 1:
                        dve.wait_ge(st["tab_sin"], 1)
                    dve.tensor_scalar(turns, angle, 1.0 / TWO_PI, shift, ALU.mult, ALU.add)
                    dve.drain()
                    dve.tensor_scalar(turns, turns, ROUND, None, ALU.add)
                    dve.drain()
                    dve.tensor_scalar(turns, turns, -ROUND, None, ALU.add)
                    dve.drain()
                    dve.scalar_tensor_tensor(out=part, in0=turns, scalar=-PI_A, in1=angle, op0=ALU.mult, op1=ALU.add)
                    for piece in (PI_B, PI_C):
                        dve.drain()
                        dve.scalar_tensor_tensor(out=part, in0=turns, scalar=-piece, in1=part,
                                                 op0=ALU.mult, op1=ALU.add)
                    dve.drain()
                    dve.tensor_scalar(part, part, TWO_PI * shift, 3.1415925, ALU.add, ALU.min)
                    dve.drain()
                    dve.tensor_scalar(part, part, -3.1415925, None, ALU.max).then_inc(st["tab_reduced"], 1)
                dve.drain().then_inc(st["tab_ready"], 1)

            def run(b, steps, u):
                def maxima(g, first, end):
                    for n in range(first, end):
                        key = ("max of", g, n)
                        dve.wait_ge(st["filled"], u.filled(key))
                        dve.tensor_reduce(row_max[:, g % 2, n:n + 1], ring[u.bank(key)][:], AX.X, ALU.max
                                          ).then_inc(st[f"free{u.bank(key)}"], 1)

                for step in steps:
                    kind = step[0]
                    if kind in ("t", "Q", "q", "k", "m", "p"):
                        g = ring[u.bank(step)]
                        freed = st[f"free{u.bank(step)}"]
                    if kind == "t":
                        c = step[1]
                        dve.wait_ge(freed, u.released(step))
                        dve.tensor_tensor(h_low[:, c, :], h_full[:], h_high[:, c, :].bitcast(F32), ALU.subtract
                                          ).then_inc(st["h_ready"], 1)
                    elif kind == "rope":
                        i = step[1]
                        if 1 <= i < 9:
                            dve.wait_ge(st["q_squared"], b * 8 + (8 + i))
                            dve.tensor_reduce(ssum[:, (i - 1) % 2, :], squares[:].rearrange("p (h d) -> p h d", d=HD),
                                              AX.X, ALU.add)
                            dve.drain()
                            dve.tensor_scalar(ssum[:, (i - 1) % 2, :], ssum[:, (i - 1) % 2, :], 1.0 / HD, EPS[1],
                                              ALU.mult, ALU.add).then_inc(st["sum_ready"], 1)
                        if i >= 3:
                            half, t = divmod(i - 3, TT)
                            dve.wait_ge(st["swap_done"], b * 8 + (8 + i - 2))
                            apart = lambda v: v.rearrange("p (r h d) -> p r h d", r=4, d=HD)
                            dve.tensor_tensor(qk_nat[:, half, t, :].rearrange("p (r d h) -> p r h d", r=4, d=HD),
                                              apart(turned[:]), apart(swapped[:]), ALU.add).then_inc(st["roped"], 1)
                            dve.drain()
                        if 2 <= i < 10:
                            half, t = divmod(i - 2, TT)
                            nat = qk_nat[:, half, t, :]
                            dve.wait_ge(st["inv_ready"], b * 8 + (8 + i - 1))
                            dve.tensor_tensor(nat.rearrange("p (h d) -> p h d", d=HD), nat.rearrange("p (h d) -> p h d", d=HD),
                                              sinv[:, (i - 2) % 2, :].unsqueeze(2).to_broadcast([P, HEADS, HD]), ALU.mult
                                              ).then_inc(st["scaled"], 1)
                            dve.drain()
                            dve.tensor_tensor(turned[:].rearrange("p (s h d) -> p s h d", s=2, d=HD),
                                              nat.rearrange("p (s h d) -> p s h d", s=2, d=HD),
                                              turn[:, t, :, :, :].rearrange("p s a e -> p s (a e)").unsqueeze(2)
                                              .to_broadcast([P, 2, HEADS // 2, HD]), ALU.mult)
                            dve.drain()
                    elif kind in ("q", "k"):
                        i = ("q", "k").index(kind)
                        dve.wait_ge(st["high_done"], b * 8 + (2 * step[1] + i + 1))
                        dve.tensor_tensor(qk_low[:, i, :], g[:], qk_high[:, i, :].bitcast(F32), ALU.subtract
                                          ).then_inc(freed, 1)
                    elif kind == "split":
                        weights.low(dve, step[1])
                    elif kind == "angles":
                        angles()
                    elif kind == "m":
                        gi = step[1]
                        dve.wait_ge(st["max_high_done"], b * NG + (gi + 1))
                        dve.scalar_tensor_tensor(out=max_low[:], in0=g[0:GH * TT, 0:P], scalar=-1.0,
                                                 in1=max_high[:].bitcast(F32), op0=ALU.mult,
                                                 op1=ALU.subtract).then_inc(freed, 1)
                    elif kind == "max":
                        maxima(step[1], TT * step[2], TT * step[2] + TT)
                    elif kind == "s":
                        maxima(step[1] + 1, *step[4])
                    elif kind == "norm":
                        gi, a = step[1], step[2] * (N // 2)
                        cols = slice(a, a + N // 2)
                        if gi == 0:
                            dve.wait_ge(st["x_done"], b * TT + 2)
                        else:
                            dve.wait_ge(st["o_ready"], b * 8 + 2 * gi)
                        dve.wait_ge(st["pv_done"], b * 16 + (4 * gi + 4 + 2))
                        dve.reciprocal(tmp2[:, 0, cols], s_acc[:, cols]).then_inc(st["o_inverse"], 1)
                        if gi < NG - 1:
                            continue
                        dve.drain()
                        dve.wait_ge(st["o_read"], b * NG + (gi + 2))
                        dve.tensor_tensor(tmp2[:, 1, cols], tmp2[:, 1, cols], tmp2[:, 0, cols], ALU.mult)
                        dve.drain()
                        dve.tensor_copy(o_high[:, gi, cols], tmp2[:, 1, cols])
                        dve.drain()
                        dve.tensor_tensor(o_low[:, gi, cols], tmp2[:, 1, cols], o_high[:, gi, cols].bitcast(F32),
                                          ALU.subtract).then_inc(st["o_ready"], 1)
                    elif kind == "stats" and l == 0:
                        if step[1] == 0:
                            dve.wait_ge(st["x_loaded"], b * 64 + 128)
                        norm_stats(dve, l, x, stats, mv, step[1])
                    elif kind == "power":
                        if l == 0:
                            dve.drain()
                            dve.tensor_scalar(x_shift[:], mv[:, :, 0], -1.0, None, ALU.mult)
                            norm_power_input(dve, l, mv, power_in, EPS[l]).then_inc(st["power_ready"], 1)
                        else:
                            dve.wait_ge(st["squared"], b * TT + 2 * TT)
                            dve.tensor_scalar(power_in[:, :], square_sum[:, :], 1.0 / D, EPS[1], ALU.mult, ALU.add
                                              ).then_inc(st["power_ready"], 1)
                    elif kind == "p":
                        t = step[1]
                        if t == 0:
                            dve.drain()
                            dve.wait_ge(st["gate_loaded"], b * 32 + 32)
                        dve.wait_ge(st["filled"], u.filled(step))
                        dve.wait_ge(st["x_done"], b * TT + (t + 1))
                        dve.tensor_tensor(tmp2[:, t % 2, :], g[:], gate[:], ALU.mult).then_inc(freed, 1)

            dve.sem_inc(st["x_done"], 2)
            if l == 1:
                dve.sem_inc(st["roped"], 1)
            run(-1, [("stats", t) for t in range(TT)] + [("power",), ("split", 0)], None)
            run(-1, attention_opening(l), Banks(before, per, None, None))
            over_sequences(dve, lambda b, last: run(b, attention_steps(l, last), banks_for(b, last)))

        @block.gpsimd
        def _(pool):
            def run(b, steps, u):
                for step in steps:
                    kind = step[0]
                    if kind == "tables":
                        if u.opening:
                            pool.wait_ge(st["tab_ready"], 1)
                            pool.wait_ge(st["tab_sin"], 2)
                        wait_and_note(pool, st["roped"], b * 8 + (8 + 1), st["noted"])
                        for table, w, trig in ((turn, w_turn, cos_t), (swap, w_swap, sin_t)):
                            for s in range(2):
                                for e in range(2):
                                    pool.tensor_tensor(table[:, :, s, :, e], trig[:, ds(b * TT + TT, TT), :],
                                                       w[:, s, :, e].unsqueeze(1).to_broadcast([P, TT, PAIRS]),
                                                       ALU.mult).then_inc(st["tables_ready"], 1)
                        wait_and_note(pool, st["tables_ready"], b * 8 + 16, st["noted"])
                    elif kind == "rope":
                        i = step[1]
                        if 1 <= i < 9:
                            wait_and_note(pool, st["sum_ready"], b * 8 + (8 + i + 1), st["noted"])
                            pool.tensor_tensor(sinv[:, (i - 1) % 2, :], ssum[:, (i - 1) % 2, :], minus_half[:], ALU.pow
                                               ).then_inc(st["inv_ready"], 1)
                        if 2 <= i < 10:
                            half, t = divmod(i - 2, TT)
                            nat = qk_nat[:, half, t, :].rearrange("p (s h a e) -> p s h a e", s=2, e=2, a=PAIRS)
                            out = swapped[:].rearrange("p (s h a e) -> p s h a e", s=2, e=2, a=PAIRS)
                            wait_and_note(pool, st["scaled"], b * 8 + (8 + i - 1), st["noted"])
                            for s in range(2):
                                for e in range(2):
                                    mult = pool.tensor_tensor(
                                        out[:, s, :, :, e], nat[:, s, :, :, 1 - e],
                                        swap[:, t, s, :, e].unsqueeze(1).to_broadcast([P, HEADS // 2, PAIRS]),
                                        ALU.mult)
                            mult.then_inc(st["swap_done"], 1)
                    elif kind == "power":
                        wait_and_note(pool, st["power_ready"], b + 2, st["noted"])
                        root = pool.tensor_tensor(rstd[:], power_in[:], minus_half[:, 0:TT], ALU.pow)
                        if l == 0:
                            pool.drain()
                            root = pool.tensor_tensor(x_shift[:], x_shift[:], rstd[:], ALU.mult)
                        root.then_inc(st["rstd_ready"], 1)
                    elif kind == "gate_bias":
                        wait_and_note(pool, st["gate_loaded"], b * 32 + 32, st["noted"])
                        pool.tensor_tensor(gate_bias[:], gate_bias[:], gate[:], ALU.mult)
                        pool.drain()
                    elif kind == "split_o":
                        gi = step[1]
                        wait_and_note(pool, st["o_inverse"], b * 8 + (2 * gi + 4), st["noted"])
                        wait_and_note(pool, st["o_read"], b * NG + (gi + 2), st["noted"])
                        pool.tensor_tensor(tmp2[:, 1, :], tmp2[:, 1, :], tmp2[:, 0, :], ALU.mult
                                           ).then_inc(st["o_scaled"], 1)
                        wait_and_note(pool, st["o_high_done"], b * (NG - 1) + (gi + 1), st["noted"])
                        pool.tensor_tensor(o_low[:, gi, :], tmp2[:, 1, :], o_high[:, gi, :].bitcast(F32), ALU.subtract
                                           ).then_inc(st["o_ready"], 2)
                    elif kind == "residual":
                        wait_and_note(pool, st["res_loaded"], b * 64 + 64, st["noted"])
                        for t in range(TT):
                            pool.tensor_tensor(x[:, t, :], x[:, t, :], gate_bias[:], ALU.add)
                        pool.drain()
                    elif kind == "p":
                        t = step[1]
                        wait_and_note(pool, st[f"free{u.bank(step)}"], u.released(step), st["noted"])
                        pool.tensor_tensor(x[:, t, :], x[:, t, :], tmp2[:, t % 2, :], ALU.add
                                           ).then_inc(st["x_done"], 1)

            pool.memset(ones[:], 1.0)
            pool.memset(minus_half[:], -0.5)
            pool.drain()
            pool.memset(keys[KROWS:AROWS, :, :, :].bitcast(F32), 1.0)
            pool.drain().then_inc(st["consts"], 1)
            if l == 1:
                pool.dma_start(pos, dram["pos"]).then_inc(st["tab_in"], 16)
                pool.dma_start(freqs, dram["freqs"]).then_inc(st["tab_in"], 16)
                for k in range(2):
                    pool.dma_start(wrow[:, k, :, :].rearrange("p a b -> p (a b)"),
                                   dram["qk_norm"][k:k + 1, :].to_broadcast([P, HD])).then_inc(st["tab_in"], 16)
            run(-1, [("power",)], None)
            run(-1, attention_opening(l), Banks(before, per, None, None))
            over_sequences(pool, lambda b, last: run(b, attention_steps(l, last), banks_for(b, last)))

        @block.sync
        def _(sp):
            def run(b, steps, u):
                for step in steps:
                    kind = step[0]
                    if kind in ("q", "k"):
                        gi, i = step[1], ("q", "k").index(kind)
                        target = (queries, keys)[i]
                        layout = ((qk_high, qk_low, qk_high), (qk_high, qk_high, qk_low))[i]
                        def stack(r):
                            src = layout[r]
                            sp.dma_start(target[HD * r:HD * (r + 1), gi % 2, :, :].rearrange("p h n -> p (h n)")
                                         .bitcast(F32), src[:, i, :].bitcast(F32)
                                         ).then_inc(st[f"stacked{gi % 2}"], 16)

                        if not u.opening:
                            wait_and_note(sp, st["score_filled"], b * 64 + 16 * (gi - 1), st["noted"])
                        wait_and_note(sp, st["high_done"], b * 8 + (2 * gi + i + 1), st["noted"])
                        for r in range(3):
                            if layout[r] is qk_high:
                                stack(r)
                        wait_and_note(sp, st[f"free{u.bank(step)}"], u.released(step), st["noted"])
                        stack(layout.index(qk_low))
                    elif kind == "m":
                        gi = step[1]
                        for r, src in enumerate((max_high, max_low)):
                            if r == 0:
                                wait_and_note(sp, st["max_high_done"], b * NG + (gi + 1), st["noted"])
                            else:
                                wait_and_note(sp, st[f"free{u.bank(step)}"], u.released(step), st["noted"])
                            sp.dma_start(queries[KROWS + r:KROWS + r + 1, gi % 2, :, :].rearrange("p h n -> p (h n)")
                                         .bitcast(F32), src[:].bitcast(F32)
                                         ).then_inc(st[f"rows{gi % 2}"], 16)
                    elif kind == "t" and step[1] == DC - 1:
                        wait_and_note(sp, st["filled"], u.filled(step), st["noted"])
                        if not u.opening:
                            sp.dma_start(x[:], seq_view(x_in, b)).then_inc(st["res_loaded"], 64)
                    elif kind == "p":
                        t = step[1]
                        wait_and_note(sp, st["x_done"], b * TT + (t + 1 + 2), st["noted"])
                        sp.dma_start(tile_view(x_out, b, t), x[:, t, :]
                                     ).then_inc(st[f"stored{t}"], 16)

            def body(b, last):
                for t in range(TT):
                    wait_and_note(sp, st[f"stored{t}"], b * 16 + 16, st["noted"])
                    nb, loaded = (b, "res_loaded") if last else (b + 1, "x_loaded")
                    sp.dma_start(x[:, t, :], tile_view(x_in, nb, t)).then_inc(st[loaded], 16)
                sp.dma_start(gate[:], mod_rows[l, ds(b, 1), 2 * D:3 * D].to_broadcast([P, D])
                             ).then_inc(st["gate_loaded"], 16)
                sp.dma_start(gate_bias[:], dram[f"b_proj{l}"].rearrange("(o n) -> o n", o=1).to_broadcast([P, D])
                             ).then_inc(st["gate_loaded"], 16)
                run(b, attention_steps(l, last), banks_for(b, last))

            for t in range(TT):
                sp.sem_inc(st[f"stored{t}"], 16)
                sp.dma_start(x[:, t, :], tile_view(x_in, 0, t)).then_inc(st["x_loaded"], 16)
            weights.load(sp)
            run(-1, attention_opening(l), Banks(before, per, None, None))
            over_sequences(sp, body)
            for t in range(TT):
                sp.wait_ge(st[f"stored{t}"], 16 + 16 * B)


def mlp_steps(l, last):
    chunks = -(-HID[l] // P)
    turn_at = chunks - 5
    s = []
    for j in range(chunks):
        s.append(("a", j))
        if l == 1:
            s.append(("g", j))
        if not last and 1 <= j <= 4:
            s.append(("stats", j - 1))
        if j >= 2 and j < chunks - 1:
            s.append(("c", j - 2))
        if not last and j == 4:
            s.append(("power",))
        if not last and j == 5:
            s += [("apply", t) for t in range(TT)]
        if not last and j == turn_at:
            s += [("t", c) for c in range(DC)]
    if not last:
        s.append(("split",))
    s += [("c", j) for j in (chunks - 3, chunks - 2, chunks - 1)]
    return s + [("p", t) for t in range(TT)]


def mlp_uses(steps):
    bank = {"a": 0, "g": 2, "t": 2}
    return [(s, bank[s[0]] + s[1] % 2) for s in steps if s[0] in bank]


def mlp_stage(nc, l, dram, x_in, x_out, mod_rows, modT, ident):
    nm = f"mlp{l}"
    hid = HID[l]
    chunks = -(-hid // P)
    width = lambda j: min(P, hid - j * P)
    with ExitStack() as ctx:
        sb = lambda n, s, d=F32: ctx.enter_context(nc.sbuf_tensor(f"{nm}_{n}", s, d))
        ups = ["a"] if l == 0 else ["a", "g"]
        up_high = {k: sb(f"up_{k}_high", [P, DC, hid], F32R) for k in ups}
        up_low = {k: sb(f"up_{k}_low", [P, DC, hid], F32R) for k in ups}
        dn_high, dn_low = sb("dn_high", [P, chunks, D], F32R), sb("dn_low", [P, chunks, D], F32R)
        minus_half = sb("minus_half", [P, TT])
        hid_bias = sb("hid_bias", [P, chunks])
        staging = sb("staging", [P, 2, DC * D])

        down = dram[f"down{l}"]
        up_piece, down_piece, pieces = {}, {}, []
        for j in range(0, chunks, 4):
            a, e = j * P, min((j + 4) * P, hid)
            for k in ups:
                up_piece[k, j // 4] = len(pieces)
                pieces.append((dram[f"up_{k}{l}"].rearrange("(c p) n -> p c n", p=P)[:, :, a:e],
                               up_high[k][:, :, a:e], up_low[k][:, :, a:e]))
            full = (e - a) // P
            down_piece[j // 4] = len(pieces)
            pieces.append((down[a:a + full * P, :].rearrange("(c p) n -> p c n", p=P),
                           dn_high[:, j:j + full, :], dn_low[:, j:j + full, :]))
            if a + full * P < e:
                rest = e - a - full * P
                down_piece["rest"] = len(pieces)
                pieces.append((down[a + full * P:e, :].rearrange("(c p) n -> p c n", c=1),
                               dn_high[0:rest, j + full:j + full + 1, :], dn_low[0:rest, j + full:j + full + 1, :]))
        weights = WeightLoader(nc, ctx, nm, [staging[:, i, :] for i in range(2)], pieces)

        x = sb("x", [P, TT, D])
        h_full = sb("h_full", [P, DC, N])
        h_high, h_low = sb("h_high", [P, DC, N], F32R), sb("h_low", [P, DC, N], F32R)
        hid_full = sb("hid_full", [P, 2, N])
        hid_high, hid_low = sb("hid_high", [P, 3, N], F32R), sb("hid_low", [P, 3, N], F32R)
        tmp2 = sb("tmp2", [P, 2, D])
        gate = sb("gate", [P, D])
        gate_bias = sb("gate_bias", [P, D]) if l == 0 else None
        stats, mv = sb("stats", [P, TT, 6]), sb("mv", [P, TT, 2])
        power_in, rstd = sb("power_in", [P, TT]), sb("rstd", [P, TT])
        st = Stage(nc, ctx, nm, 8, [
            "filled", "free0", "free1", "free2", "free3", "down_done", "acc_done", "x_loaded",
            "power_ready", "rstd_ready", "x_normed", "h_high_done", "h_ready", "hid_ready", "res_loaded", "gate_loaded", "gated", "x_done", "stored", "noted", "const_set", "bias_loaded"])
        ring, acc = st.bank[0:4], st.bank[4:8]
        before = mlp_uses([("t", c) for c in range(DC)])
        per = mlp_uses(mlp_steps(l, False))
        banks_for = lambda b, last: Banks(before, per, mlp_uses(mlp_steps(l, last)), b)
        loads = 32 if l == 0 else 16
        block = ctx.enter_context(nc.Block())

        ups_and_down = len(ups) + 1

        def first_sequence(b):
            return isinstance(b, int) and b == 0

        def hid_slot(j):
            return j % 3

        def hid_full_slot(j):
            return j % 2

        def slot_free(b, j, slots):
            if j >= slots:
                return b * chunks + (j + 1)
            last_use = max(i for i in range(chunks) if i % slots == j)
            return b * chunks + (slots - (chunks - 1 - last_use))

        @block.tensor
        def _(pe):
            for i in range(4):
                pe.sem_inc(st[f"free{i}"], 1)
            pe.sem_inc(st["gated"], TT)
            pe.sem_inc(st["down_done"], 3)

            def turn_x(u, key):
                c = key[1]
                g = ring[u.bank(key)]
                pe.wait_ge(st[f"free{u.bank(key)}"], u.freed_before(key))
                for t in range(TT):
                    mm = pe.transpose(g[:, t * P:(t + 1) * P], x[:, t, c * P:(c + 1) * P], ident[:])
                mm.then_inc(st["filled"], 1)

            def first():
                u = Banks(before, per, None, None)
                pe.wait_ge(st["x_normed"], TT)
                for c in range(DC):
                    turn_x(u, ("t", c))

            def body(b, last):
                u = banks_for(b, last)
                for step in mlp_steps(l, last):
                    kind = step[0]
                    if kind in ("a", "g"):
                        j = step[1]
                        w = width(j)
                        g = ring[u.bank(step)]
                        pe.wait_ge(st[f"free{u.bank(step)}"], u.freed_before(step))
                        if j == 0 and kind == "a":
                            pe.wait_ge(st["h_ready"], b * DC + DC)
                        if j % 4 == 0:
                            weights.ready(pe, up_piece[kind, j // 4])
                        for c in range(DC):
                            wh = up_high[kind][:, c, j * P:j * P + w]
                            wl = up_low[kind][:, c, j * P:j * P + w]
                            pe.matmul(g[0:w, :], wh, h_high[:, c, :], start=(c == 0), stop=False)
                            pe.matmul(g[0:w, :], wh, h_low[:, c, :], start=False, stop=False)
                            mm = pe.matmul(g[0:w, :], wl, h_high[:, c, :], start=False, stop=(c == DC - 1))
                        mm.then_inc(st["filled"], 1)
                    elif kind == "c":
                        j = step[1]
                        w = width(j)
                        pe.wait_ge(st["hid_ready"], b * chunks + (j + 1 + 2))
                        if j == 0:
                            pe.wait_ge(st["gated"], b * TT + TT)
                        if j % 4 == 0:
                            weights.ready(pe, down_piece[j // 4])
                        if w < P:
                            weights.ready(pe, down_piece["rest"])
                        for t in range(TT):
                            hh = hid_high[0:w, hid_slot(j), t * P:(t + 1) * P]
                            hl = hid_low[0:w, hid_slot(j), t * P:(t + 1) * P]
                            pe.matmul(acc[t][:], hh, dn_high[0:w, j, :], start=(j == 0), stop=False)
                            pe.matmul(acc[t][:], hh, dn_low[0:w, j, :], start=False, stop=False)
                            mm = pe.matmul(acc[t][:], hl, dn_high[0:w, j, :], start=False, stop=(j == chunks - 1))
                            if j == chunks - 1 and t < TT - 1:
                                mm.then_inc(st["acc_done"], 1)
                        mm.then_inc(st["down_done"], 1)
                    elif kind == "t":
                        if step[1] == 0:
                            pe.wait_ge(st["x_normed"], b * TT + 2 * TT)
                        turn_x(u, step)

            over_sequences(pe, body, first, True)

        @block.scalar
        def _(act):
            act.sem_inc(st["hid_ready"], 2)

            def modulate(u, key, nb):
                c = key[1]
                act.wait_ge(st["filled"], u.filled(key))
                act.activation(h_full[:, c, :], ring[u.bank(key)][:], ACT.Identity, bias=modT[:, l, 8 + c, ds(nb, 1)],
                               scale=modT[:, l, 12 + c, ds(nb, 1)]
                               ).then_inc(st[f"free{u.bank(key)}"], 1)

            def high_h(u):
                for c in range(DC):
                    act.wait_ge(st[f"free{u.bank(('t', c))}"], u.released(("t", c)))
                    act.activation(h_high[:, c, :], h_full[:, c, :], ACT.Copy).then_inc(st["h_high_done"], 1)

            def first():
                u = Banks(before, per, None, None)
                weights.high(act, 0)
                weights.high(act, 1)
                for c in range(DC):
                    modulate(u, ("t", c), 0)
                high_h(u)
                if l == 1:
                    weights.high(act, 2)
                if l == 0:
                    act.wait_ge(st["bias_loaded"], 16)

            def body(b, last):
                u = banks_for(b, last)
                for step in mlp_steps(l, last):
                    kind = step[0]
                    if kind == "a":
                        j = step[1]
                        w = width(j)
                        act.wait_ge(st["filled"], u.filled(step))
                        act.wait_ge(st["hid_ready"], slot_free(b, j, 2))
                        if l == 0:
                            ins = act.activation(hid_full[0:w, hid_full_slot(j), :],
                                                 ring[u.bank(step)][0:w, :], ACT.Gelu, bias=hid_bias[0:w, j:j + 1])
                        else:
                            ins = act.activation(hid_full[0:w, hid_full_slot(j), :], ring[u.bank(step)][0:w, :], ACT.Silu)
                        ins.then_inc(st[f"free{u.bank(step)}"], 1)
                        if first_sequence(b) and ups_and_down + j < len(pieces):
                            weights.high(act, ups_and_down + j)
                    elif kind == "t":
                        modulate(u, step, b + 1)
                    elif kind == "split":
                        act.wait_ge(st["filled"], u.filled((ups[-1], chunks - 1)))
                        high_h(u)

            over_sequences(act, body, first, True)

        @block.vector
        def _(dve):
            dve.sem_inc(st["x_done"], 2)

            def low_h(nb):
                for c in range(DC):
                    dve.wait_ge(st["h_high_done"], nb * DC + (c + 1))
                    dve.tensor_tensor(h_low[:, c, :], h_full[:, c, :], h_high[:, c, :].bitcast(F32), ALU.subtract
                                      ).then_inc(st["h_ready"], 1)

            def more_weights(b, j):
                if first_sequence(b) and ups_and_down + j < len(pieces):
                    weights.low(dve, ups_and_down + j)

            def split_hidden(b, j):
                w = width(j)
                full = hid_full[0:w, hid_full_slot(j), :]
                high, low = hid_high[0:w, hid_slot(j), :], hid_low[0:w, hid_slot(j), :]
                dve.wait_ge(st["down_done"], slot_free(b, j, 3))
                dve.tensor_copy(high, full)
                dve.drain()
                dve.tensor_tensor(low, full, high.bitcast(F32), ALU.subtract).then_inc(st["hid_ready"], 1)

            def first():
                dve.wait_ge(st["x_loaded"], 16)
                for t in range(TT):
                    norm_stats(dve, l, x, stats, mv, t)
                norm_power_input(dve, l, mv, power_in, EPS[l]).then_inc(st["power_ready"], 1)
                dve.wait_ge(st["rstd_ready"], 1)
                for t in range(TT):
                    norm_apply(dve, l, x, mv, rstd, t).then_inc(st["x_normed"], 1)
                weights.low(dve, 0)
                low_h(0)
                weights.low(dve, 1)
                if l == 1:
                    weights.low(dve, 2)

            def body(b, last):
                u = banks_for(b, last)
                for step in mlp_steps(l, last):
                    kind = step[0]
                    if kind == "a" and l == 0:
                        dve.wait_ge(st[f"free{u.bank(step)}"], u.released(step))
                        split_hidden(b, step[1])
                        more_weights(b, step[1])
                    elif kind == "g":
                        j = step[1]
                        w = width(j)
                        full = hid_full[0:w, hid_full_slot(j), :]
                        dve.wait_ge(st[f"free{u.bank(('a', j))}"], u.released(("a", j)))
                        dve.wait_ge(st["filled"], u.filled(step))
                        dve.tensor_tensor(full, ring[u.bank(step)][0:w, :], full, ALU.mult
                                          ).then_inc(st[f"free{u.bank(step)}"], 1)
                        dve.drain()
                        split_hidden(b, j)
                        more_weights(b, j)
                    elif kind == "stats":
                        if step[1] == 0:
                            dve.wait_ge(st["x_loaded"], b * 16 + 32)
                        norm_stats(dve, l, x, stats, mv, step[1])
                    elif kind == "power":
                        norm_power_input(dve, l, mv, power_in, EPS[l]).then_inc(st["power_ready"], 1)
                    elif kind == "apply":
                        if step[1] == 0:
                            dve.wait_ge(st["rstd_ready"], b + 2)
                        norm_apply(dve, l, x, mv, rstd, step[1]).then_inc(st["x_normed"], 1)
                    elif kind == "split":
                        low_h(b + 1)
                    elif kind == "p":
                        t = step[1]
                        if t == 0:
                            dve.wait_ge(st["gate_loaded"], b * loads + loads)
                        if t < TT - 1:
                            dve.wait_ge(st["acc_done"], b * (TT - 1) + (t + 1))
                        else:
                            dve.wait_ge(st["down_done"], b * chunks + (chunks + 3))
                        dve.wait_ge(st["x_done"], b * TT + (t + 1))
                        dve.tensor_tensor(tmp2[:, t % 2, :], acc[t][:], gate[:], ALU.mult
                                          ).then_inc(st["gated"], 1)

            over_sequences(dve, body, first, True)

        @block.gpsimd
        def _(pool):
            def power(n):
                wait_and_note(pool, st["power_ready"], n + 1, st["noted"])
                pool.tensor_tensor(rstd[:], power_in[:], minus_half[:], ALU.pow).then_inc(st["rstd_ready"], 1)

            def body(b, last):
                for step in mlp_steps(l, last):
                    kind = step[0]
                    if kind == "power":
                        power(b + 1)
                    elif kind == "c" and step[1] == chunks - 2 and l == 0:
                        wait_and_note(pool, st["gate_loaded"], b * loads + loads, st["noted"])
                        pool.tensor_tensor(gate_bias[:], gate_bias[:], gate[:], ALU.mult)
                        pool.drain()
                        wait_and_note(pool, st["res_loaded"], b * 16 + 16, st["noted"])
                        for t in range(TT):
                            pool.tensor_tensor(x[:, t, :], x[:, t, :], gate_bias[:], ALU.add)
                        pool.drain()
                    elif kind == "p":
                        t = step[1]
                        if t == 0:
                            wait_and_note(pool, st["res_loaded"], b * 16 + 16, st["noted"])
                        wait_and_note(pool, st["gated"], b * TT + (t + 1 + TT), st["noted"])
                        pool.tensor_tensor(x[:, t, :], x[:, t, :], tmp2[:, t % 2, :], ALU.add
                                           ).then_inc(st["x_done"], 1)

            def first():
                pool.memset(minus_half[:], -0.5).then_inc(st["const_set"], 1)
                pool.wait_ge(st["const_set"], 1)
                power(0)

            over_sequences(pool, body, first, True)

        @block.sync
        def _(sp):
            def first():
                sp.sem_inc(st["stored"], 16)
                sp.dma_start(x[:], seq_view(x_in, 0)).then_inc(st["x_loaded"], 16)
                weights.load(sp, 0, ups_and_down + 2)
                if l == 0:
                    sp.dma_start(hid_bias[:], dram["b_fc1"]).then_inc(st["bias_loaded"], 16)
                sp.wait_ge(st["filled"], DC)

            def body(b, last):
                wait_and_note(sp, st["stored"], b * 64 + 16, st["noted"])
                if not last:
                    sp.dma_start(x[:], seq_view(x_in, b + 1)).then_inc(st["x_loaded"], 16)
                else:
                    sp.dma_start(x[:], seq_view(x_in, b)).then_inc(st["res_loaded"], 16)
                sp.dma_start(gate[:], mod_rows[l, ds(b, 1), 5 * D:6 * D].to_broadcast([P, D])
                             ).then_inc(st["gate_loaded"], 16)
                if l == 0:
                    sp.dma_start(gate_bias[:], dram["b_fc2"].rearrange("(o n) -> o n", o=1).to_broadcast([P, D])
                                 ).then_inc(st["gate_loaded"], 16)
                if first_sequence(b):
                    weights.load(sp, ups_and_down + 2)
                for step in mlp_steps(l, last):
                    if step == ("t", DC - 1):
                        wait_and_note(sp, st["filled"], banks_for(b, last).filled(step), st["noted"])
                        sp.dma_start(x[:], seq_view(x_in, b)).then_inc(st["res_loaded"], 16)
                    elif step[0] == "p":
                        t = step[1]
                        wait_and_note(sp, st["x_done"], b * TT + (t + 1 + 2), st["noted"])
                        sp.dma_start(x_out[ds(b, 1), t * P:(t + 1) * P, :].rearrange("o p d -> p (o d)"), x[:, t, :]
                                     ).then_inc(st["stored"], 16)

            over_sequences(sp, body, first, True)
            sp.wait_ge(st["stored"], 16 + 64 * B)


def build_program(nc, dram, out):
    mod_rows = nc.dram_tensor("mod_rows", [2, B, 6 * D], F32).ap()
    mid = [nc.dram_tensor(f"x_mid{i}", [B, N, D], F32).ap() for i in range(3)]
    with ExitStack() as ctx:
        ident = ctx.enter_context(nc.sbuf_tensor("ident", [P, P], F32))
        modT = ctx.enter_context(nc.sbuf_tensor("modT", [P, 2, 4 * DC, B], F32))
        modulation_stage(nc, dram, mod_rows, modT, ident)
        attention_stage(nc, 0, dram, dram["x"], mid[0], mod_rows, modT, ident)
        mlp_stage(nc, 0, dram, mid[0], mid[1], mod_rows, modT, ident)
        attention_stage(nc, 1, dram, mid[1], mid[2], mod_rows, modT, ident)
        mlp_stage(nc, 1, dram, mid[2], out, mod_rows, modT, ident)


def kernel(**inputs):
    import concourse.bacc as bacc
    from concourse.bass_utils import run_bass_kernel_spmd

    c = {k: np.asarray(v) for k, v in inputs.items()}
    by_chunk = lambda v: v.reshape(-1, P).T
    wq = c["L1_cond_qkv_w"].T
    half = D // 2
    w_qkv0 = c["L0_cond_w_qkv"].copy()
    w_qkv0[:, 0:2 * D] = (w_qkv0[:, 0:2 * D].reshape(D, 2 * NG, GH, HD).transpose(0, 1, 3, 2).reshape(D, 2 * D))
    w_qkv1 = np.concatenate([wq[:, 0:half], wq[:, D:D + half], wq[:, half:D], wq[:, D + half:2 * D],
                             wq[:, 2 * D:]], axis=1)
    arrays = {
        "x": c["x"],
        "cT": c["cond_1024"].T.reshape(DC, P, B).transpose(1, 0, 2),
        "w_ada0": c["L0_cond_w_ada"], "b_ada0": c["L0_cond_b_ada"],
        "w_ada1": c["L1_cond_ada_w"].T, "b_ada1": c["L1_cond_ada_b"],
        "norm1": by_chunk(c["L1_cond_norm1_w"]), "norm2": by_chunk(c["L1_cond_norm2_w"]),
        "w_qkv0": w_qkv0, "w_qkv1": w_qkv1,
        "w_proj0": c["L0_cond_w_proj"], "w_proj1": c["L1_cond_proj_w"].T,
        "b_proj0": c["L0_cond_b_proj"], "b_proj1": c["L1_cond_proj_b"],
        "up_a0": c["L0_cond_w_fc1"], "b_fc1": by_chunk(c["L0_cond_b_fc1"]),
        "down0": c["L0_cond_w_fc2"], "b_fc2": c["L0_cond_b_fc2"],
        "up_a1": c["L1_cond_w1"].T, "up_g1": c["L1_cond_w3"].T, "down1": c["L1_cond_w2"].T,
        "qk_norm": np.stack([c["L1_cond_q_norm_w"], c["L1_cond_k_norm_w"]]),
        "pos": c["fside_BxSx3_0"].reshape(B * TT, P, 3).transpose(1, 0, 2),
        "freqs": np.tile((1.0 / np.float32(10000.0) ** (np.arange(5, dtype=np.float32) / np.float32(5)))
                         .astype(np.float32), (P, 1)),
    }
    arrays = {k: np.ascontiguousarray(v) for k, v in arrays.items()}
    nc = bacc.Bacc("TRN2", target_bir_lowering=False, num_devices=1)
    dram = {k: nc.dram_tensor(f"in_{k}", v.shape, mybir.dt.from_np(v.dtype), kind="ExternalInput").ap()
            for k, v in arrays.items()}
    out = nc.dram_tensor("out_0", (B, N, D), F32, kind="ExternalOutput").ap()
    build_program(nc, dram, out)
    r = run_bass_kernel_spmd(nc, [{f"in_{k}": v for k, v in arrays.items()}], core_ids=[0])
    return r.results[0]["out_0"]
```
